# Optimizing a Trainium2 kernel written in Bass

```python
import numpy as np
import jax
import jax.numpy as jnp

def _softmax(x, axis=-1):
    return jax.nn.softmax(x, axis=axis)

def _gelu(x):
    return jax.nn.gelu(x, approximate=True)

def _silu(x):
    return jax.nn.silu(x)

def _sigmoid(x):
    return jax.nn.sigmoid(x)

def _layernorm(x, axis=-1, eps=1e-05):
    m = jnp.mean(x, axis=axis, keepdims=True)
    v = jnp.var(x, axis=axis, keepdims=True)
    return (x - m) / jnp.sqrt(v + eps)

def _scatter_add(tgt, idx, src, axis=0):
    return tgt.at[idx].add(src)

def _segment_sum(src, seg, n):
    return jax.ops.segment_sum(src, seg, n)
kernel_name = 'mk_xattn_seq_d4_seqx_r8_4c3444'

def setup_inputs(seed: int=0):
    np.random.seed(seed)
    _w = jnp.asarray

    def _rec_inputs():
        import jax
        import jax.numpy as jnp
        _rk = jax.random.key(seed)
        x = -0.0002928 + 1 * jax.random.normal(jax.random.fold_in(_rk, 1), (8, 128, 256), jnp.float32)
        _lenS = 128 - jax.random.randint(jax.random.fold_in(_rk, 7), (8,), 0, max(1, 128 // 4) + 1, jnp.int32)
        _lenS2 = 128 - jax.random.randint(jax.random.fold_in(_rk, 8), (8,), 0, max(1, 128 // 4) + 1, jnp.int32)
        _ctx_2048P = jax.random.normal(jax.random.fold_in(_rk, 11), (8, 16, 256), jnp.float32)
        _ctx_2048c = jax.random.dirichlet(jax.random.fold_in(_rk, 511), 0.3 * jnp.ones((16,), jnp.float32), (8, 128))
        _ctx_2048t = jnp.einsum('bsk,bkd->bsd', _ctx_2048c, _ctx_2048P)
        _ctx_2048t = _ctx_2048t * jax.lax.rsqrt(jnp.mean(jnp.square(_ctx_2048t)) + 1e-12) * 0.953939
        ctx_2048 = -1.39393e-06 + 0.999914 * (_ctx_2048t + 0.3 * jax.random.normal(jax.random.fold_in(_rk, 611), (8, 128, 256), jnp.float32))
        _validS = jnp.arange(128)[None, :] < _lenS[:, None]
        _validS2 = jnp.arange(128)[None, :] < _lenS2[:, None]
        _causal = jnp.tril(jnp.ones((128, 128), dtype=bool))
        mask_BxS2_ik0 = jnp.where(jnp.broadcast_to(_validS2[:, :], (8, 128)), 0, 1).astype(jnp.int32)
        mask_BxS2_bf1 = jnp.ones((8, 128), dtype=bool)
        mask_Bx1x2048_bf1 = jnp.ones((8, 1, 256), dtype=bool)
        return (x, ctx_2048, mask_BxS2_ik0, mask_BxS2_bf1, mask_Bx1x2048_bf1)
    x, ctx_2048, mask_BxS2_ik0, mask_BxS2_bf1, mask_Bx1x2048_bf1 = _rec_inputs()

    def _L0_xattn_setup():
        import jax, jax.numpy as jnp
        import numpy as np
        D_MODEL = 128
        N_HEAD = 16
        D_HEAD = 64
        IDX_LIST = [128, 256]
        SCALE = 1.0 / D_HEAD ** 0.5
        LN_EPS = 1e-05
        key = jax.random.key(seed)
        ks = jax.random.split(key, 9)
        s = 0.02
        B, L = (2, 256)
        return {'z1ss': jax.random.normal(ks[0], (B, D_MODEL, L), dtype=jnp.float32), 'u1ss': jax.random.normal(ks[1], (B, D_MODEL, L), dtype=jnp.float32), 'Wqkv0': jax.random.normal(ks[2], (3 * N_HEAD * D_HEAD, D_MODEL), dtype=jnp.float32) * s, 'Wqkv1': jax.random.normal(ks[3], (3 * N_HEAD * D_HEAD, D_MODEL), dtype=jnp.float32) * s, 'Winj0': jax.random.normal(ks[4], (3 * N_HEAD * D_HEAD, D_MODEL), dtype=jnp.float32) * s, 'Winj1': jax.random.normal(ks[5], (3 * N_HEAD * D_HEAD, D_MODEL), dtype=jnp.float32) * s, 'Wo': jax.random.normal(ks[6], (D_MODEL, N_HEAD * D_HEAD), dtype=jnp.float32) * s, 'bo': jax.random.normal(ks[7], (D_MODEL,), dtype=jnp.float32) * s, 'r_w_bias': jax.random.uniform(ks[8], (N_HEAD, D_HEAD), minval=-0.05, maxval=0.05, dtype=jnp.float32)}
    _L0_xattn_all = _L0_xattn_setup()
    _L0_xattn_in = {k: v for k, v in _L0_xattn_all.items() if k in ('Wqkv0', 'Wqkv1', 'Winj0', 'Winj1', 'Wo', 'bo', 'r_w_bias')}
    del _L0_xattn_all

    def _L1_xattn_setup():
        import jax, jax.numpy as jnp
        import numpy as np
        B, P, K, H, NH = (4, 256, 32, 256, 16)
        DH = H // NH
        EPS = 1e-06

        def rmsnorm(x, w):
            var = jnp.mean(jnp.square(x), axis=-1, keepdims=True)
            return x * jax.lax.rsqrt(var + EPS) * w
        key = jax.random.key(seed)
        ks = jax.random.split(key, 12)
        s = 0.02
        return {'x': jax.random.normal(ks[0], (B, P, H), jnp.float32), 'latents': jax.random.normal(ks[1], (B, K, H), jnp.float32), 'attention_mask': jax.random.randint(ks[2], (B, P), 0, 2, jnp.int32), 'q_w': s * jax.random.normal(ks[3], (H, H), jnp.float32), 'q_b': jnp.zeros((H,), jnp.float32), 'kv_w': s * jax.random.normal(ks[4], (H, 2 * H), jnp.float32), 'kv_b': jnp.zeros((2 * H,), jnp.float32), 'out_w': s * jax.random.normal(ks[5], (H, H), jnp.float32), 'out_b': jnp.zeros((H,), jnp.float32), 'postnorm_w': jnp.ones((H,), jnp.float32), 'mlp_w1': s * jax.random.normal(ks[6], (H, 4 * H), jnp.float32), 'mlp_b1': jnp.zeros((4 * H,), jnp.float32), 'mlp_w2': s * jax.random.normal(ks[7], (4 * H, H), jnp.float32), 'mlp_b2': jnp.zeros((H,), jnp.float32)}
    _L1_xattn_all = _L1_xattn_setup()
    _L1_xattn_in = {k: v for k, v in _L1_xattn_all.items() if k in ('q_w', 'q_b', 'kv_w', 'kv_b', 'out_w', 'out_b', 'postnorm_w', 'mlp_w1', 'mlp_b1', 'mlp_w2', 'mlp_b2')}
    del _L1_xattn_all

    def _L2_xattn_setup():
        import jax, jax.numpy as jnp
        import numpy as np
        D = 256
        H = 16
        HD = D // H
        INNER = 4 * D
        EPS = 1e-05

        def layer_norm(x, w, b):
            mu = jnp.mean(x, axis=-1, keepdims=True)
            var = jnp.mean(jnp.square(x - mu), axis=-1, keepdims=True)
            return (x - mu) * jax.lax.rsqrt(var + EPS) * w + b
        key = jax.random.key(seed)
        ks = jax.random.split(key, 12)
        B, LQ, LK = (4, 128, 256)
        std = 0.02
        inp = {'hidden_states': jax.random.normal(ks[0], (B, LQ, D), jnp.float32), 'encoder_hidden_states': jax.random.normal(ks[1], (B, LK, D), jnp.float32), 'encoder_attention_mask': jnp.ones((B, LK), dtype=bool), 'ln1_w': jnp.ones((D,), jnp.float32), 'ln1_b': jnp.zeros((D,), jnp.float32), 'q_w': jax.random.normal(ks[2], (D, D), jnp.float32) * std, 'q_b': jnp.zeros((D,), jnp.float32), 'k_w': jax.random.normal(ks[3], (D, D), jnp.float32) * std, 'k_b': jnp.zeros((D,), jnp.float32), 'v_w': jax.random.normal(ks[4], (D, D), jnp.float32) * std, 'v_b': jnp.zeros((D,), jnp.float32), 'cproj_w': jax.random.normal(ks[5], (D, D), jnp.float32) * std, 'cproj_b': jnp.zeros((D,), jnp.float32), 'ln2_w': jnp.ones((D,), jnp.float32), 'ln2_b': jnp.zeros((D,), jnp.float32), 'fc_w': jax.random.normal(ks[6], (D, INNER), jnp.float32) * std, 'fc_b': jnp.zeros((INNER,), jnp.float32), 'proj_w': jax.random.normal(ks[7], (INNER, D), jnp.float32) * std, 'proj_b': jnp.zeros((D,), jnp.float32)}
        return inp
    _L2_xattn_all = _L2_xattn_setup()
    _L2_xattn_in = {k: v for k, v in _L2_xattn_all.items() if k in ('ln1_w', 'ln1_b', 'q_w', 'q_b', 'k_w', 'k_b', 'v_w', 'v_b', 'cproj_w', 'cproj_b', 'ln2_w', 'ln2_b', 'fc_w', 'fc_b', 'proj_w', 'proj_b')}
    del _L2_xattn_all

    def _L3_xattn_setup():
        import jax, jax.numpy as jnp
        import numpy as np
        import math
        N_HEADS = 16
        EPS = 1e-05

        def _masked_instance_norm(x, mask):
            m = mask.astype(x.dtype)
            x = x * m
            n_valid = jnp.sum(m, axis=-1, keepdims=True)
            mean = jnp.sum(x, axis=-1, keepdims=True) / n_valid
            var = jnp.sum(x * x, axis=-1, keepdims=True) / n_valid - mean * mean
            x = (x - mean) / jnp.sqrt(jax.nn.relu(var) + EPS)
            return x * m
        key = jax.random.key(seed)
        ks = jax.random.split(key, 8)
        bs, c, t1, t2 = (2, 128, 256, 256)
        s = 1.0 / math.sqrt(c)
        return {'x': jax.random.normal(ks[0], (bs, c, t1), jnp.float32), 'mask': jnp.ones((bs, 1, t1), jnp.bool_), 'kv': jax.random.normal(ks[1], (bs, c, t2), jnp.float32), 'kv_mask': jnp.ones((bs, 1, t2), jnp.bool_), 'Wq': jax.random.normal(ks[2], (c, c), jnp.float32) * s, 'bq': jnp.zeros((c,), jnp.float32), 'Wk': jax.random.normal(ks[3], (c, c), jnp.float32) * s, 'bk': jnp.zeros((c,), jnp.float32), 'Wv': jax.random.normal(ks[4], (c, c), jnp.float32) * s, 'bv': jnp.zeros((c,), jnp.float32)}
    _L3_xattn_all = _L3_xattn_setup()
    _L3_xattn_in = {k: v for k, v in _L3_xattn_all.items() if k in ('Wq', 'bq', 'Wk', 'bk', 'Wv', 'bv')}
    del _L3_xattn_all
    return {'x': x, 'ctx_2048': ctx_2048, 'mask_BxS2_ik0': mask_BxS2_ik0, 'mask_BxS2_bf1': mask_BxS2_bf1, 'mask_Bx1x2048_bf1': mask_Bx1x2048_bf1, 'L0_xattn_Wqkv0': _L0_xattn_in['Wqkv0'], 'L0_xattn_Wqkv1': _L0_xattn_in['Wqkv1'], 'L0_xattn_Winj0': _L0_xattn_in['Winj0'], 'L0_xattn_Winj1': _L0_xattn_in['Winj1'], 'L0_xattn_Wo': _L0_xattn_in['Wo'], 'L0_xattn_bo': _L0_xattn_in['bo'], 'L0_xattn_r_w_bias': _L0_xattn_in['r_w_bias'], 'L1_xattn_q_w': _L1_xattn_in['q_w'], 'L1_xattn_q_b': _L1_xattn_in['q_b'], 'L1_xattn_kv_w': _L1_xattn_in['kv_w'], 'L1_xattn_kv_b': _L1_xattn_in['kv_b'], 'L1_xattn_out_w': _L1_xattn_in['out_w'], 'L1_xattn_out_b': _L1_xattn_in['out_b'], 'L1_xattn_postnorm_w': _L1_xattn_in['postnorm_w'], 'L1_xattn_mlp_w1': _L1_xattn_in['mlp_w1'], 'L1_xattn_mlp_b1': _L1_xattn_in['mlp_b1'], 'L1_xattn_mlp_w2': _L1_xattn_in['mlp_w2'], 'L1_xattn_mlp_b2': _L1_xattn_in['mlp_b2'], 'L2_xattn_ln1_w': _L2_xattn_in['ln1_w'], 'L2_xattn_ln1_b': _L2_xattn_in['ln1_b'], 'L2_xattn_q_w': _L2_xattn_in['q_w'], 'L2_xattn_q_b': _L2_xattn_in['q_b'], 'L2_xattn_k_w': _L2_xattn_in['k_w'], 'L2_xattn_k_b': _L2_xattn_in['k_b'], 'L2_xattn_v_w': _L2_xattn_in['v_w'], 'L2_xattn_v_b': _L2_xattn_in['v_b'], 'L2_xattn_cproj_w': _L2_xattn_in['cproj_w'], 'L2_xattn_cproj_b': _L2_xattn_in['cproj_b'], 'L2_xattn_ln2_w': _L2_xattn_in['ln2_w'], 'L2_xattn_ln2_b': _L2_xattn_in['ln2_b'], 'L2_xattn_fc_w': _L2_xattn_in['fc_w'], 'L2_xattn_fc_b': _L2_xattn_in['fc_b'], 'L2_xattn_proj_w': _L2_xattn_in['proj_w'], 'L2_xattn_proj_b': _L2_xattn_in['proj_b'], 'L3_xattn_Wq': _L3_xattn_in['Wq'], 'L3_xattn_bq': _L3_xattn_in['bq'], 'L3_xattn_Wk': _L3_xattn_in['Wk'], 'L3_xattn_bk': _L3_xattn_in['bk'], 'L3_xattn_Wv': _L3_xattn_in['Wv'], 'L3_xattn_bv': _L3_xattn_in['bv']}

def reference(x, ctx_2048, mask_BxS2_ik0, mask_BxS2_bf1, mask_Bx1x2048_bf1, L0_xattn_Wqkv0, L0_xattn_Wqkv1, L0_xattn_Winj0, L0_xattn_Winj1, L0_xattn_Wo, L0_xattn_bo, L0_xattn_r_w_bias, L1_xattn_q_w, L1_xattn_q_b, L1_xattn_kv_w, L1_xattn_kv_b, L1_xattn_out_w, L1_xattn_out_b, L1_xattn_postnorm_w, L1_xattn_mlp_w1, L1_xattn_mlp_b1, L1_xattn_mlp_w2, L1_xattn_mlp_b2, L2_xattn_ln1_w, L2_xattn_ln1_b, L2_xattn_q_w, L2_xattn_q_b, L2_xattn_k_w, L2_xattn_k_b, L2_xattn_v_w, L2_xattn_v_b, L2_xattn_cproj_w, L2_xattn_cproj_b, L2_xattn_ln2_w, L2_xattn_ln2_b, L2_xattn_fc_w, L2_xattn_fc_b, L2_xattn_proj_w, L2_xattn_proj_b, L3_xattn_Wq, L3_xattn_bq, L3_xattn_Wk, L3_xattn_bk, L3_xattn_Wv, L3_xattn_bv):
    import jax
    import jax.numpy as jnp

    def _L0_xattn_ref(z1ss, u1ss, Wqkv0, Wqkv1, Winj0, Winj1, Wo, bo, r_w_bias):
        import jax, jax.numpy as jnp
        import numpy as np
        D_MODEL = 128
        N_HEAD = 16
        D_HEAD = 64
        IDX_LIST = [128, 256]
        SCALE = 1.0 / D_HEAD ** 0.5
        LN_EPS = 1e-05
        bsz, d_model, qlen = z1ss.shape
        bounds = [0] + IDX_LIST
        Wq_list, Wi_list = ([Wqkv0, Wqkv1], [Winj0, Winj1])
        chunks = []
        for i in range(len(IDX_LIST)):
            s, e = (bounds[i], bounds[i + 1])
            h = jnp.einsum('od,bdl->bol', Wq_list[i], z1ss[:, :, s:e])
            h = h + jnp.einsum('od,bdl->bol', Wi_list[i], u1ss[:, :, s:e])
            chunks.append(h)
        w_heads = jnp.concatenate(chunks, axis=2)
        q, k, v = jnp.split(w_heads, 3, axis=1)
        q = q[:, :, -qlen:]
        klen = k.shape[2]
        q = q.reshape(bsz, N_HEAD, D_HEAD, qlen)
        k = k.reshape(bsz, N_HEAD, D_HEAD, klen)
        v = v.reshape(bsz, N_HEAD, D_HEAD, klen)
        rq = q + r_w_bias[None, :, :, None]
        score = jnp.einsum('bndi,bndj->bnij', rq, k) * SCALE
        prob = jax.nn.softmax(score, axis=-1)
        attn_vec = jnp.einsum('bnij,bndj->bndi', prob, v)
        attn_vec = attn_vec.reshape(bsz, N_HEAD * D_HEAD, qlen)
        attn_out = jnp.einsum('od,bdl->bol', Wo, attn_vec) + bo[None, :, None]
        x = attn_out + z1ss
        m = jnp.mean(x, axis=1, keepdims=True)
        var = jnp.var(x, axis=1, keepdims=True)
        return (x - m) * jax.lax.rsqrt(var + LN_EPS)

    def _L1_xattn_ref(x, latents, attention_mask, q_w, q_b, kv_w, kv_b, out_w, out_b, postnorm_w, mlp_w1, mlp_b1, mlp_w2, mlp_b2):
        import jax, jax.numpy as jnp
        import numpy as np
        B, P, K, H, NH = (4, 256, 32, 256, 16)
        DH = H // NH
        EPS = 1e-06

        def rmsnorm(x, w):
            var = jnp.mean(jnp.square(x), axis=-1, keepdims=True)
            return x * jax.lax.rsqrt(var + EPS) * w
        b, p, _ = x.shape
        k_len = latents.shape[1]
        residual = latents
        h = jnp.concatenate([x, latents], axis=1)
        q = (latents @ q_w + q_b).reshape(b, k_len, NH, DH)
        kv = (h @ kv_w + kv_b).reshape(b, p + k_len, NH, DH, 2)
        kmat, v = (kv[..., 0], kv[..., 1])
        attn = jnp.einsum('bkhd,bnhd->bhkn', q, kmat) / DH
        full_mask = jnp.concatenate([attention_mask.astype(bool), jnp.ones((b, k_len), bool)], axis=-1)
        attn = jnp.where(full_mask[:, None, None, :], attn, -jnp.inf)
        attn = jax.nn.softmax(attn.astype(jnp.float32), axis=-1).astype(q.dtype)
        attn_out = jnp.einsum('bhkn,bnhd->bkhd', attn, v).reshape(b, k_len, H)
        attn_out = attn_out @ out_w + out_b + residual
        out = rmsnorm(attn_out, postnorm_w)
        out = jax.nn.gelu(out @ mlp_w1 + mlp_b1) @ mlp_w2 + mlp_b2
        return out + residual

    def _L2_xattn_ref(hidden_states, encoder_hidden_states, encoder_attention_mask, ln1_w, ln1_b, q_w, q_b, k_w, k_b, v_w, v_b, cproj_w, cproj_b, ln2_w, ln2_b, fc_w, fc_b, proj_w, proj_b):
        import jax, jax.numpy as jnp
        import numpy as np
        D = 256
        H = 16
        HD = D // H
        INNER = 4 * D
        EPS = 1e-05

        def layer_norm(x, w, b):
            mu = jnp.mean(x, axis=-1, keepdims=True)
            var = jnp.mean(jnp.square(x - mu), axis=-1, keepdims=True)
            return (x - mu) * jax.lax.rsqrt(var + EPS) * w + b
        B, LQ, _ = hidden_states.shape
        LK = encoder_hidden_states.shape[1]
        residual = hidden_states
        x = layer_norm(hidden_states, ln1_w, ln1_b)
        q = (x @ q_w + q_b).reshape(B, LQ, H, HD).transpose(0, 2, 1, 3)
        k = (encoder_hidden_states @ k_w + k_b).reshape(B, LK, H, HD).transpose(0, 2, 1, 3)
        v = (encoder_hidden_states @ v_w + v_b).reshape(B, LK, H, HD).transpose(0, 2, 1, 3)
        scale = 1.0 / np.sqrt(HD).astype(np.float32)
        scores = jnp.einsum('bhqd,bhkd->bhqk', q, k) * scale
        mask = encoder_attention_mask[:, None, None, :]
        mask_value = jnp.finfo(scores.dtype).min
        scores = jnp.where(mask, scores, mask_value)
        attn = jax.nn.softmax(scores, axis=-1)
        out = jnp.einsum('bhqk,bhkd->bhqd', attn, v)
        out = out.transpose(0, 2, 1, 3).reshape(B, LQ, D)
        out = out @ cproj_w + cproj_b
        hidden = out + residual
        residual = hidden
        y = layer_norm(hidden, ln2_w, ln2_b)
        y = jax.nn.gelu(y @ fc_w + fc_b, approximate=True)
        y = y @ proj_w + proj_b
        return residual + y

    def _L3_xattn_ref(x, mask, kv, kv_mask, Wq, bq, Wk, bk, Wv, bv):
        import jax, jax.numpy as jnp
        import numpy as np
        import math
        N_HEADS = 16
        EPS = 1e-05

        def _masked_instance_norm(x, mask):
            m = mask.astype(x.dtype)
            x = x * m
            n_valid = jnp.sum(m, axis=-1, keepdims=True)
            mean = jnp.sum(x, axis=-1, keepdims=True) / n_valid
            var = jnp.sum(x * x, axis=-1, keepdims=True) / n_valid - mean * mean
            x = (x - mean) / jnp.sqrt(jax.nn.relu(var) + EPS)
            return x * m
        bs, c, t1 = x.shape
        h = N_HEADS
        d = c // h
        scale = 1.0 / math.sqrt(d)
        q = jnp.einsum('oc,bct->bot', Wq, x) + bq[None, :, None]
        k = jnp.einsum('oc,bct->bot', Wk, kv) + bk[None, :, None]
        v = jnp.einsum('oc,bct->bot', Wv, kv) + bv[None, :, None]
        q = q.reshape(bs, h, d, t1).transpose(0, 1, 3, 2)
        k = k.reshape(bs, h, d, -1)
        v = v.reshape(bs, h, d, -1).transpose(0, 1, 3, 2)
        attn = jnp.einsum('bhqd,bhdk->bhqk', q * scale, k)
        attn = jnp.where(kv_mask[:, :, None, :], attn, -jnp.inf)
        attn = jax.nn.softmax(attn, axis=-1)
        mean = jnp.einsum('bhqk,bhkd->bhqd', attn, v)
        ex2 = jnp.einsum('bhqk,bhkd->bhqd', attn, v * v)
        std = jnp.sqrt(jax.nn.relu(ex2 - mean * mean))
        mean = mean.transpose(0, 1, 3, 2).reshape(bs, c, t1)
        std = std.transpose(0, 1, 3, 2).reshape(bs, c, t1)
        xn = _masked_instance_norm(x, mask)
        out = (xn * std + mean) * mask.astype(x.dtype)
        return out
    x = _L0_xattn_ref(x, ctx_2048, L0_xattn_Wqkv0, L0_xattn_Wqkv1, L0_xattn_Winj0, L0_xattn_Winj1, L0_xattn_Wo, L0_xattn_bo, L0_xattn_r_w_bias)
    x = _L1_xattn_ref(ctx_2048, x, mask_BxS2_ik0, L1_xattn_q_w, L1_xattn_q_b, L1_xattn_kv_w, L1_xattn_kv_b, L1_xattn_out_w, L1_xattn_out_b, L1_xattn_postnorm_w, L1_xattn_mlp_w1, L1_xattn_mlp_b1, L1_xattn_mlp_w2, L1_xattn_mlp_b2)
    x = _L2_xattn_ref(x, ctx_2048, mask_BxS2_bf1, L2_xattn_ln1_w, L2_xattn_ln1_b, L2_xattn_q_w, L2_xattn_q_b, L2_xattn_k_w, L2_xattn_k_b, L2_xattn_v_w, L2_xattn_v_b, L2_xattn_cproj_w, L2_xattn_cproj_b, L2_xattn_ln2_w, L2_xattn_ln2_b, L2_xattn_fc_w, L2_xattn_fc_b, L2_xattn_proj_w, L2_xattn_proj_b)
    x = _L3_xattn_ref(x, mask_Bx1x2048_bf1, ctx_2048, mask_Bx1x2048_bf1, L3_xattn_Wq, L3_xattn_bq, L3_xattn_Wk, L3_xattn_bk, L3_xattn_Wv, L3_xattn_bv)
    return x

_drawn_inputs = setup_inputs


def setup_inputs(seed=0):
    import zlib

    import numpy as np

    out = dict(_drawn_inputs(seed))
    spreads = {'L1_xattn_q_b': (0.0, 0.8),
     'L1_xattn_kv_b': (0.0, 0.8),
     'L1_xattn_out_b': (0.0, 0.8),
     'L1_xattn_postnorm_w': (1.0, 0.6),
     'L1_xattn_mlp_b1': (0.0, 0.1),
     'L1_xattn_mlp_b2': (0.0, 0.1),
     'L2_xattn_ln1_w': (1.0, 0.6),
     'L2_xattn_ln1_b': (0.0, 0.8),
     'L2_xattn_q_b': (0.0, 0.8),
     'L2_xattn_k_b': (0.0, 2.0),
     'L2_xattn_v_b': (0.0, 0.271),
     'L2_xattn_cproj_b': (0.0, 0.1),
     'L2_xattn_ln2_w': (1.0, 0.6),
     'L2_xattn_ln2_b': (0.0, 0.731),
     'L2_xattn_fc_b': (0.0, 0.1),
     'L2_xattn_proj_b': (0.0, 0.1),
     'L3_xattn_bq': (0.0, 0.287),
     'L3_xattn_bk': (0.0, 2.0),
     'L3_xattn_bv': (0.0, 0.1)}
    factors = {'L0_xattn_Wqkv0': 8.0,
     'L0_xattn_Wqkv1': 8.0,
     'L0_xattn_Winj0': 8.0,
     'L0_xattn_Winj1': 8.0,
     'L0_xattn_Wo': 8.0,
     'L0_xattn_bo': 55.752,
     'L0_xattn_r_w_bias': 8.0,
     'L1_xattn_q_w': 8.0,
     'L1_xattn_kv_w': 8.0,
     'L1_xattn_out_w': 8.0,
     'L2_xattn_q_w': 8.0,
     'L2_xattn_k_w': 8.0}
    for name, (base, spread) in spreads.items():
        noise = np.random.default_rng([zlib.crc32(name.encode()), seed]).standard_normal(out[name].shape)
        drawn = base * np.exp(spread * noise) if base else spread * noise
        out[name] = jnp.asarray(drawn.astype(out[name].dtype))
    for name, factor in factors.items():
        out[name] = (out[name] * factor).astype(out[name].dtype)
    return out
```

```python
from contextlib import ExitStack

import concourse.bass as bass
from concourse import mybir
from concourse.alu_op_type import AluOpType as ALU

F32 = mybir.dt.float32
BF16 = mybir.dt.bfloat16
I32 = mybir.dt.int32
U8 = mybir.dt.uint8
ACT = mybir.ActivationFunctionType
AX_X = mybir.AxisListType.X

P = 128
B = 8
D = 256
NH = 16
HG = 4
NG = NH // HG
NQKV = 3 * NH * 64
NEG = -(2.0 ** 100)
GELU_C = 0.7978845608028654
GELU_A = 0.044715

COLS = {}
for _name, _n in (("bo", 1), ("rwb", 8), ("qb1", 2), ("kb1", 2), ("b1", 8), ("qb2", 2), ("kb2", 2),
                  ("fcb", 8), ("bq", 1), ("bk", 1)):
    COLS[_name] = (sum(n for _, n in COLS.values()), _n)
NCOLS = sum(n for _, n in COLS.values())
ROWS = {}
for _name, _n in (("vb1", D), ("ob1", D), ("pw", D), ("b2", D), ("ln1w", D), ("ln1b", D), ("vb2", D),
                  ("cb", D), ("ln2w", D), ("ln2b", D), ("pb", D), ("bv", P)):
    ROWS[_name] = (sum(n for _, n in ROWS.values()), _n)
NROWS = sum(n for _, n in ROWS.values())

STEPS = {0: 4, 1: 2, 2: 1, 3: 4}
SC_BASE = {0: 0, 1: 16, 2: 24, 3: 28}
SC_N = 44
PV_BASE = {0: 0, 1: 8, 2: 10, 3: 12}
MX_UNITS = [(L, g, u) for L in range(4) for g in range(NG) for u in [*range(STEPS[L]), "T"]]
MX_N = len(MX_UNITS)

N_MSK = 7
V_STEPS = 16 + 8 + 1 + 4 * 2 + 4 + 8
P_STEPS = 7
F_STEPS = 7

PROJ = [f"qp{i}" for i in range(4)] + [f"kp{i}" for i in range(4)] + [f"vp{i}" for i in range(4)]
BODY = ["wo", PROJ[0], "mean", PROJ[1], PROJ[2], "var", PROJ[3], PROJ[4], PROJ[5], "latT", PROJ[6],
        "q1", "k1", "v1", "o1", PROJ[7], PROJ[8], "oT", "m0", "m1", "k2", "w2", PROJ[9], PROJ[10],
        "yT", "q2", "v2", "o2", PROJ[11], "k3", "yT2", "n0", "n1", "v3", "w4", "q3"]
LAST = [u for u in BODY if u not in PROJ]


TAKEN = {"wo": ("x0", 1, 1), "mean": ("d0", 1, 1), "var": ("sd0", 1, 1), "latT": ("hT", 1, 1),
         "q1": ("Qx", 8, 2), "k1": ("K1", 1, 1), "v1": ("V1", 1, 1), "o1": ("xa", 2, 1), "oT": ("oT", 3, 1),
         "m0": ("X", 4, 1), "m1": ("X", 4, 2), "k2": ("K2", 1, 1), "w2": ("x1", 1, 1), "yT": ("oT", 3, 2),
         "q2": ("Qx", 8, 4), "v2": ("V2", 1, 1), "o2": ("xa", 2, 2), "k3": ("K3", 1, 1),
         "yT2": ("oT", 3, 3), "n0": ("X", 4, 3), "n1": ("X", 4, 4), "v3": ("v3", 1, 1), "w4": ("x3", 1, 1),
         "q3": ("Qx", 8, 8)}
TAKEN.update({u: ({"q": "Q0", "k": "K0", "v": "V0"}[u[0]], 4, int(u[-1]) + 1) for u in PROJ})


def build(nc, z_in, ctxT_in, ctx_in, mask1, mask2, mask3, w0, wo, w1qk, w1v, w1o, w1a, w1b,
          w2qkv, w2o, w2a, w2b, w3, cols_in, rows_in, ident_in, hmask_in, sel_in, out):
    with ExitStack() as stack:
        def sb(name, shape, dt=F32):
            return stack.enter_context(nc.sbuf_tensor(name, shape, dt))

        def ps(name):
            return stack.enter_context(nc.psum_tensor(name, [P, 512], F32))

        def sem(name):
            return stack.enter_context(nc.semaphore(name))

        MX = [ps(f"MX{i}") for i in range(2)]
        SC = [ps(f"SC{i}") for i in range(2)]
        PV = [ps(f"PV{i}") for i in range(2)]
        GP = [ps(f"GP{i}") for i in range(2)]

        W0 = sb("W0", [P, 6, 4, 512])
        WO = sb("WO", [P, 8, P])
        W1QK = sb("W1QK", [P, 2, 2, D])
        W1V = sb("W1V", [P, 2, D])
        W1O = sb("W1O", [P, NG, D])
        W2QKV = sb("W2QKV", [P, 3, 2, D])
        W2O = sb("W2O", [P, NG, D])
        WA = sb("WA", [P, 2, 1024])
        WB = sb("WB", [P, 8, D])
        W3 = sb("W3", [P, 3, P])
        cols = sb("cols", [P, NCOLS])
        rows = sb("rows", [P, NROWS])
        ident = sb("ident", [P, P])
        identb = sb("identb", [P, P], BF16)
        hmask = sb("hmask", [P, 8 + 16])
        sel = sb("sel", [P, HG + 1, P], BF16)
        ones = sb("ones", [P, 64])
        mean_w = sb("mean_w", [P, P])

        work = sb("work", [P, 3 * HG * D])
        sel32 = work[:, 0:(HG + 1) * P].rearrange("p (h k) -> p h k", k=P)
        A0 = work[:, 0:8 * D].rearrange("p (c l) -> p c l", l=D)
        Q12 = work[:, 0:NH * P].rearrange("p (h l) -> p h l", l=P)
        Q3 = work[:].rearrange("p (h l) -> p h l", l=D)
        X, T, G = (work[:, 1024 * i:1024 * i + 1024] for i in range(3))

        zP = sb("zP", [P, D])
        uP = sb("uP", [P, D])
        zR = sb("zR", [P, D])
        uC = sb("uC", [P, D])
        hT = sb("hT", [P, 2, D])
        Q0 = sb("Q0", [P, NH, D])
        K0 = sb("K0", [P, 8, D])
        K0b = sb("K0b", [P, 2, 2, D], BF16)
        Qb = sb("Qb", [P, 2, HG, D], BF16)
        V0 = sb("V0", [P, 2, 1024])
        Pr = sb("Pr", [P, 4, 512])
        Psum = sb("Psum", [P, 2, 512])
        mx = sb("mx", [P, 2, 2, HG])
        nm = sb("nm", [P, 2, 2, 8], BF16)
        nmT = sb("nmT", [P, 2, D], BF16)
        U3 = sb("U3", [P, NG, D])
        x0, d0, sq0, rec = (U3[:, i, :] for i in range(4))
        lat = d0
        K1 = sb("K1", [P, 2, D])
        K1b = sb("K1b", [P, 2, D], BF16)
        V1 = sb("V1", [P, 2, NH, 32])
        K2 = sb("K2", [P, 2, P])
        K2b = sb("K2b", [P, 2, P], BF16)
        V2 = sb("V2", [P, NH, 32])
        K3 = sb("K3", [P, D])
        K3b = sb("K3b", [P, D], BF16)
        V3 = V1
        den = rec
        Ax = sb("Ax", [P, NG, P])
        res1 = sb("res1", [P, D])
        res2 = sb("res2", [P, D])
        xa = sb("xa", [P, D])
        xb = sb("xb", [P, D])
        oT = sb("oT", [P, 2, P])
        x1 = sb("x1", [P, D])
        x3 = x1
        stat = sb("stat", [P, 16])
        gate = sb("gate", [P, 2])
        half = sb("half", [P, 1])
        epsc = sb("epsc", [P, 1])
        sd0 = sq0
        junk = sq0
        m1row = sb("m1row", [P, P], I32)
        m1col = sb("m1col", [P, 1], I32)
        m2row = sb("m2row", [P, P], U8)
        m2col = sb("m2col", [P, 1], U8)
        m3row = sb("m3row", [P, D], U8)
        m3col = sb("m3col", [P, 2], U8)
        b1row = sb("b1row", [P, D], BF16)
        b2row = sb("b2row", [P, P], BF16)
        b3row = sb("b3row", [P, D], BF16)
        bcol = sb("bcol", [P, 5])
        m3 = sb("m3", [P, D])
        xm = sb("xm", [P, D])
        xn = xm
        stat3 = sb("stat3", [P, 4])
        C3 = sb("C3", [P, 4, D])
        scratch = nc.dram_tensor("scratch", [P, NG, D], F32, kind="Internal").ap()

        def col(name, i=0):
            return cols[:, COLS[name][0] + i:COLS[name][0] + i + 1]

        def colrange(name, a, b):
            return cols[:, COLS[name][0] + a:COLS[name][0] + b]

        def row(name):
            return rows[:, ROWS[name][0]:ROWS[name][0] + ROWS[name][1]]

        ld_w0 = [sem(f"ld_w0_{i}") for i in range(6)]
        ld_proj, ld_par, ld_rows, ld_wo, ld_w1, ld_w2, ld_w3, ld_mlp, ld_ctx, ld_res, ld_msk, ld_c3, st_u3, st_out = (
            sem(n) for n in ("ld_proj", "ld_par", "ld_rows", "ld_wo", "ld_w1", "ld_w2", "ld_w3", "ld_mlp", "ld_ctx",
                             "ld_res", "ld_msk", "ld_c3", "st_u3", "st_out"))
        const_p, const_v = sem("const_p"), sem("const_v")
        mx_full = [sem(f"mx_full{i}") for i in range(2)]
        gp_full = [sem(f"gp_full{i}") for i in range(2)]
        sc_full, pv_done, den_done = sem("sc_full"), sem("pv_done"), sem("den_done")
        mx_done, nm_ready, nmT_ready, p_ready, ps_ready = (
            sem(n) for n in ("mx_done", "nm_ready", "nmT_ready", "p_ready", "ps_ready"))
        (s_Q0, s_Qb, s_K0, s_V0, s_A0, s_x0, s_d0, s_sq0, s_sd0, s_lat, s_hT, s_Qx, s_K1, s_V1, s_K2,
         s_V2, s_K3, s_v3, s_V3, s_Ax, s_U3) = (sem("s_" + n) for n in (
             "Q0", "Qb", "K0", "V0", "A0", "x0", "d0", "sq0", "sd0", "lat", "hT", "Qx", "K1", "V1", "K2",
             "V2", "K3", "v3", "V3", "Ax", "U3"))
        (s_res1, s_res2, s_xa, s_ssq, s_var, s_pow, s_xb, s_oT, s_X, s_sq, s_T, s_th, s_G, s_x1, s_x3) = (
            sem("s_" + n) for n in ("res1", "res2", "xa", "ssq", "var", "pow", "xb", "oT", "X", "sq", "T", "th",
                                    "G", "x1", "x3"))
        (s_msk, s_xm, s_nst, s_ninv, s_xn, s_v, s_std, s_o3) = (
            sem("s_" + n) for n in ("msk", "xm", "nst", "ninv", "xn", "v", "std", "o3"))
        v_step, p_step, f_step, v_apart, p_apart = (
            sem(n) for n in ("v_step", "p_step", "f_step", "v_apart", "p_apart"))

        def is_first(b):
            return isinstance(b, int) and b == 0

        def is_last(b):
            return isinstance(b, int) and b == B - 1

        class Order:

            def __init__(self, names, base, b):
                self.names, self.base, self.b = names, base, b

            def at(self, name):
                n = self.names.index(name)
                return n % 2, self.base + n // 2

            def bank_taken(self, name):
                n = self.names.index(name) - 2
                if n < 0 and self.b is None:
                    return None
                if n < 0:
                    name, k = (PROJ[n], 0) if is_first(self.b) else (BODY[n], self.b - 1)
                else:
                    name = self.names[n]
                    k = (0 if self.b is None else self.b + 1) if name in PROJ else self.b
                tile, per_batch, count = TAKEN[name]
                return by_tile[tile], per_batch * k + count

        by_tile = {"x0": s_x0, "d0": s_d0, "sd0": s_sd0, "hT": s_hT, "Qx": s_Qx, "K1": s_K1, "V1": s_V1,
                   "xa": s_xa, "oT": s_oT, "X": s_X, "K2": s_K2, "x1": s_x1, "V2": s_V2, "K3": s_K3,
                   "v3": s_v3, "x3": s_x3, "Q0": s_Q0, "K0": s_K0, "V0": s_V0}

        def order_of(b):
            return Order(LAST if is_last(b) else BODY, b * (len(BODY) // 2) + len(PROJ) // 2, b)

        prologue = Order(PROJ, 0, None)

        def mx_bank_taken(b, n):
            L, g, u = MX_UNITS[n - 2]
            k = b - 1 if n < 2 else b
            if u == "T":
                return nmT_ready, 16 * k + 4 * L + g + 1
            return mx_done, SC_N * k + SC_BASE[L] + g * STEPS[L] + u + 1

        def pv_bank_taken(b, m):
            k, m = (b - 1, m + 12) if m < 2 else (b, m - 2)
            if m < 8:
                return s_A0, 8 * k + m + 1
            return (s_Ax, 4 * k + m - 7) if m < 12 else (s_U3, 2 * k + m - 11)

        def wait(eng, s, value):
            if isinstance(value, int) and value <= 0:
                return
            eng.wait_ge(s, value)

        class Apart:

            def __init__(self, eng, scratch, s, per_batch):
                self.eng, self.scratch, self.s, self.per_batch = eng, scratch, s, per_batch

            def begin(self, b):
                self.b, self.n = b, 0

            def wait(self, *waits):
                for s, v in waits:
                    wait(self.eng, s, v)
                wait(self.eng, self.s, self.b * self.per_batch + self.n)
                self.eng.tensor_tensor(self.scratch, half[:], half[:], ALU.add).then_inc(self.s, 1)
                self.n += 1

            def end(self):
                assert self.n == self.per_batch, self.n

        class Chain:

            def __init__(self, eng, s, per_batch):
                self.eng, self.s, self.per_batch = eng, s, per_batch

            def begin(self, b):
                self.b, self.n = b, 0

            def step(self, instruction, apart=None):
                instruction.then_inc(self.s, 1)
                self.n += 1
                if apart is not None:
                    apart.wait((self.s, self.b * self.per_batch + self.n))
                else:
                    self.eng.wait_ge(self.s, self.b * self.per_batch + self.n)

            def end(self):
                assert self.n == self.per_batch, self.n

        def unit_heads(L, g, u):
            if L in (0, 3):
                h = HG * g + 2 * (u // 2)
                return [h, h + 1], u % 2, D
            return list(range(HG * g, HG * g + HG)), u if L == 1 else 0, P

        def order_of_maxima(L):
            steps = STEPS[L]
            before = [[] for _ in range(NG * steps + 1)]
            for _, g, u in (unit for unit in MX_UNITS if unit[0] == L):
                at = g * steps - 1 if u == "T" else g * steps + u - steps - 1
                before[max(at, -1)].append((g, u))
            return before

        def every_batch(eng, body):
            body(0)
            with eng.Fori(1, B - 1) as b:
                body(b)
            body(B - 1)

        block = stack.enter_context(nc.Block())

        @block.sync
        def _(sp):
            def load_mlp(a, c):
                sp.dma_start(WA[:], a).then_inc(ld_mlp, 16)
                sp.dma_start(WB[:], c).then_inc(ld_mlp, 16)

            sp.dma_start(zP[:], z_in[0]).then_inc(ld_proj, 16)
            sp.dma_start(uP[:], ctx_in[0]).then_inc(ld_proj, 16)
            for i in range(6):
                sp.dma_start(W0[:, i], w0[i]).then_inc(ld_w0[i], 16)
                if i == 0:
                    sp.dma_start(cols[:], cols_in).then_inc(ld_par, 16)
                    sp.dma_start(ident[:], ident_in).then_inc(ld_par, 16)
                    sp.dma_start(hmask[:], hmask_in).then_inc(ld_par, 16)
                    sp.dma_start(sel32, sel_in).then_inc(ld_par, 16)
            sp.dma_start(WO[:], wo).then_inc(ld_wo, 16)
            sp.dma_start(rows[:], rows_in.to_broadcast([P, NROWS])).then_inc(ld_rows, 16)
            for dst, src in ((W1QK, w1qk), (W1V, w1v), (W1O, w1o)):
                sp.dma_start(dst[:], src).then_inc(ld_w1, 16)
            load_mlp(w1a, w1b)
            for dst, src in ((W2QKV, w2qkv), (W2O, w2o)):
                sp.dma_start(dst[:], src).then_inc(ld_w2, 16)
            sp.dma_start(W3[:], w3).then_inc(ld_w3, 16)

            def store_batch(b):
                sp.wait_ge(s_o3, b + 1)
                sp.dma_start(out[b], C3[:, 3, :]).then_inc(st_out, 16)

            def body(b):
                wait(sp, s_V3, b)
                sp.dma_start(hT[:, :, 0:P], ctxT_in[b]).then_inc(ld_ctx, 16)
                sp.dma_start(uC[:], ctx_in[b]).then_inc(ld_ctx, 16)
                wait(sp, s_x0, b)
                sp.dma_start(zR[:], z_in[b]).then_inc(ld_res, 16)
                wait(sp, s_msk, N_MSK * b)
                sp.dma_start(m1row[0:1, :], mask1[b]).then_inc(ld_msk, 16)
                sp.dma_start(m1col[:], mask1[b].rearrange("o p -> p o")).then_inc(ld_msk, 16)
                sp.dma_start(m2row[0:1, :], mask2[b]).then_inc(ld_msk, 16)
                sp.dma_start(m2col[:], mask2[b].rearrange("o p -> p o")).then_inc(ld_msk, 16)
                sp.dma_start(m3row[:], mask3[b].to_broadcast([P, D])).then_inc(ld_msk, 16)
                for c in range(2):
                    sp.dma_start(m3col[:, c:c + 1], mask3[b][:, c * P:c * P + P].rearrange("o p -> p o"))\
                        .then_inc(ld_msk, 16)
                if not is_last(b):
                    sp.wait_ge(s_V0, 4 * b + 4)
                    sp.dma_start(zP[:], z_in[b + 1]).then_inc(ld_proj, 16)
                    sp.dma_start(uP[:], ctx_in[b + 1]).then_inc(ld_proj, 16)
                if not is_first(b):
                    store_batch(b - 1)
                sp.wait_ge(s_x1, b + 1)
                load_mlp(w2a, w2b)
                if not is_last(b):
                    sp.wait_ge(s_x3, b + 1)
                    load_mlp(w1a, w1b)
                sp.wait_ge(s_U3, 2 * b + 2)
                sp.dma_start(scratch, U3[:]).then_inc(st_u3, 16)
                sp.wait_ge(st_u3, 16 * b + 16)
                for q in range(3):
                    for g in range(NG):
                        src = scratch.rearrange("(s r) g i -> g s r i", r=32)[g][:, 8 * q:8 * q + 8, :]
                        sp.dma_start(C3[32 * g:32 * g + 32, q, :], src).then_inc(ld_c3, 16)

            every_batch(sp, body)
            store_batch(B - 1)
            sp.wait_ge(st_out, 16 * B)

        @block.tensor
        def _(pe):
            def project(name, o, k):
                bank, n = o.at(name)
                i = int(name[-1])
                if name == PROJ[0]:
                    pe.wait_ge(ld_proj, 32 * k + 32)
                if n >= 1 if isinstance(n, int) else True:
                    pe.wait_ge(*o.bank_taken(name))
                if name[0] in "qk":
                    for c in range(2):
                        piece, at = divmod((2 * i + c + (8 if name[0] == "k" else 0)) * P, 512)
                        pe.wait_ge(ld_w0[piece], 16)
                        for s in range(2):
                            dst = GP[bank][:, c * D + s * P:c * D + s * P + P]
                            pe.matmul(dst, W0[:, piece, 2 * s, at:at + P], zP[:, s * P:s * P + P],
                                      start=True, stop=False)
                            mm = pe.matmul(dst, W0[:, piece, 2 * s + 1, at:at + P], uP[:, s * P:s * P + P],
                                           start=False, stop=True)
                else:
                    s, w = divmod(i, 2)
                    pe.wait_ge(ld_w0[4 + w], 16)
                    pe.matmul(GP[bank][:], zP[:, s * P:s * P + P], W0[:, 4 + w, 2 * s, :], start=True, stop=False)
                    mm = pe.matmul(GP[bank][:], uP[:, s * P:s * P + P], W0[:, 4 + w, 2 * s + 1, :],
                                   start=False, stop=True)
                mm.then_inc(gp_full[bank], 1)

            def attention(b, o, L, K, Kb, Qf, V, mrow, ready, between=None):
                steps = STEPS[L]
                halves = 2 if L in (0, 3) else 1

                def ready_group(g):
                    pe.wait_ge(s_Qb, 16 * b + 4 * L + g + 1)
                    if g == 0:
                        for s, v in ready:
                            pe.wait_ge(s, v)
                    if L == 0:
                        pe.wait_ge(s_K0, 4 * b + g + 1)

                def maxima(g, u):
                    n = MX_UNITS.index((L, g, u))
                    dst = MX[n % 2]
                    wait(pe, *mx_bank_taken(b, n))
                    if mrow is not None:
                        keys = mrow.shape[1]
                        pe.matmul(dst[:].rearrange("p (a k) -> p a k", k=keys), sel[:, HG, :],
                                  mrow.unsqueeze(1).to_broadcast([P, 512 // keys, keys]), start=True, stop=False,
                                  skip_group_check=True)
                    if L in (0, 3):
                        parts = [(HG * g + u, s) for s in range(2)]
                    else:
                        per = HG // steps
                        parts = [(HG * g + per * u + j, 0) for j in range(per)]
                    w = 512 // len(parts)
                    for j, (h, s) in enumerate(parts):
                        mm = pe.matmul(dst[:, j * w:j * w + w], Qb[:, g % 2, h % HG, s * P:s * P + P], Kb(h),
                                       start=mrow is None, stop=True, skip_group_check=True)
                    mm.then_inc(mx_full[n % 2], 1)

                def shift_rows(g):
                    n = MX_UNITS.index((L, g, "T"))
                    rows_out = MX[n % 2][:].bitcast(BF16)
                    wait(pe, *mx_bank_taken(b, n))
                    pe.wait_ge(nm_ready, 16 * b + 4 * L + g + 1)
                    for s in range(halves):
                        mm = pe.transpose(rows_out[0:8, s * P:s * P + P], nm[:, g % 2, s, :], identb[:])
                    mm.then_inc(mx_full[n % 2], 1)

                def scores(g, u):
                    n = SC_BASE[L] + g * steps + u
                    heads, kc, w = unit_heads(L, g, u)
                    wait(pe, p_ready, SC_N * b + n - 1)
                    if u == 0:
                        pe.wait_ge(nmT_ready, 16 * b + 4 * L + g + 1)
                    for j, h in enumerate(heads):
                        dst = SC[n % 2][:, j * w:j * w + w]
                        pe.matmul(dst, sel[:, h % HG, :], nmT[:, g % 2, 0:w], start=True, stop=False,
                                  skip_group_check=True)
                        mm = pe.matmul(dst, K(h)[:, kc * P:kc * P + P], Qf(h), start=False, stop=True,
                                       skip_group_check=True)
                    mm.then_inc(sc_full, 1)

                def pv(g, u):
                    n = SC_BASE[L] + g * steps + u
                    heads, kc, w = unit_heads(L, g, u)
                    m = 2 * g + u // 2 if L == 0 else PV_BASE[L] + g // 2
                    pe.wait_ge(p_ready, SC_N * b + n + 1)
                    if (kc == 0 if L == 0 else g % 2 == 0 and u == 0):
                        wait(pe, *pv_bank_taken(b, m))
                    for j, h in enumerate(heads):
                        if L == 0:
                            dst, v = PV[m % 2][64 * j:64 * j + 64, 0:D], V[:, kc, h * 64:h * 64 + 64]
                        else:
                            s = 32 * (h % HG)
                            dst, v = PV[m % 2][s:s + 32, (g % 2) * w:(g % 2) * w + w], V(h, kc)
                        mm = pe.matmul(dst, v, Pr[:, n % 4, j * w:j * w + w], start=(kc == 0),
                                       stop=(kc == 1 or L == 2), skip_group_check=True)
                    mm.then_inc(pv_done, 1)

                def denominator(c):
                    pe.wait_ge(ps_ready, 8 * b + c + 1)
                    for j in range(2):
                        mm = pe.matmul(PV[c % 2][64 * j:64 * j + 64, D:2 * D], ones[:],
                                       Psum[:, c % 2, j * D:j * D + D], start=True, stop=True,
                                       skip_group_check=True)
                    mm.then_inc(den_done, 1)

                def out_chunk(c):
                    bank, n = o.at("wo")
                    if c == 0:
                        pe.wait_ge(*o.bank_taken("wo"))
                        pe.wait_ge(ld_wo, 16)
                    pe.wait_ge(s_A0, 8 * b + c + 1)
                    mm = pe.matmul(GP[bank][:, 0:D], WO[:, c, :], A0[:, c, :], start=(c == 0), stop=(c == 7),
                                   skip_group_check=True)
                    if c == 7:
                        mm.then_inc(gp_full[bank], 1)

                def maxima_before(n):
                    for g, u in order_of_maxima(L)[n]:
                        if u == "T":
                            shift_rows(g)
                        else:
                            if u == 0:
                                ready_group(g)
                            maxima(g, u)

                maxima_before(-1)
                units = [(g, u) for g in range(NG) for u in range(steps)]
                for n, (g, u) in enumerate(units):
                    maxima_before(n)
                    scores(g, u)
                    if n >= 2:
                        pv(*units[n - 2])
                    if L == 0 and n % 2 and n >= 3:
                        denominator((n - 3) // 2)
                    if L == 0 and n % 2 and n >= 7:
                        out_chunk((n - 7) // 2)
                pv(*units[-2])
                pv(*units[-1])
                if L == 0:
                    denominator(7)
                    for c in range(5, 8):
                        if c == 7:
                            between()
                        out_chunk(c)

            def body(b):
                o = order_of(b)

                def fill(*names):
                    if not is_last(b):
                        for name in names:
                            project(name, o, b + 1)

                def begin(name, *ready):
                    bank, n = o.at(name)
                    pe.wait_ge(*o.bank_taken(name))
                    for s, v in ready:
                        pe.wait_ge(s, v)
                    return GP[bank], gp_full[bank]

                def transpose_pair(name, src, ready):
                    g, full = begin(name, ready)
                    for c in range(2):
                        mm = pe.transpose(g[:, c * P:c * P + P], src[:, c * P:c * P + P], ident[:])
                    mm.then_inc(full, 1)

                def heads_T(name, W, rhs, width, *ready):
                    g, full = begin(name, *ready)
                    for m in range(2):
                        for c in range(2):
                            mm = pe.matmul(g[:, m * width:m * width + width], W[:, c, m * P:m * P + P], rhs(c),
                                           start=(c == 0), stop=(c == 1), skip_group_check=True)
                    mm.then_inc(full, 1)

                def slots_out(name, W, which):
                    g, full = begin(name)
                    for s in range(NG):
                        if s % 2 == 0:
                            pe.wait_ge(s_Ax, 4 * b + 2 * which + s // 2 + 1)
                        mm = pe.matmul(g[:, 0:D], Ax[:, s, :], W[:, s, :], start=(s == 0), stop=(s == NG - 1))
                    mm.then_inc(full, 1)

                def mlp_in(name, *ready):
                    g, full = begin(name, *ready)
                    for j in range(4):
                        f = 4 * int(name[1]) + j
                        for c in range(2):
                            mm = pe.matmul(g[:, j * P:j * P + P], WA[:, c, f * P:f * P + P], oT[:, c, :],
                                           start=(c == 0), stop=(c == 1), skip_group_check=True)
                    mm.then_inc(full, 1)

                def mlp_out(name, which):
                    g, full = begin(name)
                    for f in range(8):
                        if f % 4 == 0:
                            pe.wait_ge(s_G, 4 * b + 2 * which + f // 4 + 1)
                        mm = pe.matmul(g[:, 0:D], G[:, f * P:f * P + P], WB[:, f, :], start=(f == 0), stop=(f == 7))
                    mm.then_inc(full, 1)

                attention(b, o, 0, lambda h: K0[:, h // 2, :], lambda h: K0b[:, h // HG % 2, h // 2 % 2, :],
                          lambda h: Q0[:, h, :], V0, None, [(s_V0, 4 * b + 4)],
                          lambda: fill(PROJ[0]))
                g, full = begin("mean", (s_x0, b + 1))
                pe.matmul(g[:, 0:D], mean_w[:], x0, start=True, stop=True).then_inc(full, 1)
                fill(PROJ[1], PROJ[2])
                g, full = begin("var", (s_sq0, b + 1))
                pe.matmul(g[:, 0:D], mean_w[:], sq0, start=True, stop=True).then_inc(full, 1)
                fill(PROJ[3], PROJ[4], PROJ[5])
                transpose_pair("latT", lat, (s_lat, b + 1))
                fill(PROJ[6])
                heads_T("q1", W1QK[:, 0], lambda c: hT[:, c, P:D], P, (s_hT, b + 1), (ld_w1, 48))
                heads_T("k1", W1QK[:, 1], lambda c: hT[:, c, :], D, (ld_ctx, 32 * b + 32))
                g, full = begin("v1")
                for kc in range(2):
                    for c in range(2):
                        mm = pe.matmul(g[:, kc * D:kc * D + D], hT[:, c, kc * P:kc * P + P], W1V[:, c, :],
                                       start=(c == 0), stop=(c == 1), skip_group_check=True)
                mm.then_inc(full, 1)

                attention(b, o, 1, lambda h: K1[:, h // 8, :], lambda h: K1b[:, h // 8, :], lambda h: Q12[:, h, :],
                          lambda h, kc: V1[:, kc, h, :], b1row[:],
                          [(s_K1, b + 1), (s_V1, b + 1), (s_msk, N_MSK * (b + 1))])
                slots_out("o1", W1O, 0)
                fill(PROJ[7], PROJ[8])
                transpose_pair("oT", xb, (s_xb, 3 * b + 1))
                mlp_in("m0", (s_oT, 3 * b + 1), (ld_mlp, 64 * b + 32))
                mlp_in("m1")
                heads_T("k2", W2QKV[:, 1], lambda c: hT[:, c, 0:P], P, (ld_w2, 32))
                mlp_out("w2", 0)
                fill(PROJ[9], PROJ[10])
                transpose_pair("yT", xb, (s_xb, 3 * b + 2))
                heads_T("q2", W2QKV[:, 0], lambda c: oT[:, c, :], P, (s_oT, 3 * b + 2))
                g, full = begin("v2")
                for c in range(2):
                    mm = pe.matmul(g[:, 0:D], hT[:, c, 0:P], W2QKV[:, 2, c, :], start=(c == 0), stop=(c == 1))
                mm.then_inc(full, 1)

                attention(b, o, 2, lambda h: K2[:, h // 8, :], lambda h: K2b[:, h // 8, :], lambda h: Q12[:, h, :],
                          lambda h, kc: V2[:, h, :], b2row[:], [(s_K2, b + 1), (s_V2, b + 1)])
                slots_out("o2", W2O, 1)
                fill(PROJ[11])
                g, full = begin("k3", (ld_w3, 16))
                pe.matmul(g[:, 0:D], W3[:, 1, :], uC[:], start=True, stop=True).then_inc(full, 1)
                transpose_pair("yT2", xb, (s_xb, 3 * b + 3))
                mlp_in("n0", (s_oT, 3 * b + 3), (ld_mlp, 64 * b + 64))
                mlp_in("n1")
                g, full = begin("v3")
                for kc in range(2):
                    mm = pe.matmul(g[:, kc * P:kc * P + P], uC[:, kc * P:kc * P + P], W3[:, 2, :],
                                   start=True, stop=True, skip_group_check=True)
                mm.then_inc(full, 1)
                mlp_out("w4", 1)
                g, full = begin("q3", (s_x3, b + 1))
                pe.matmul(g[:, 0:D], W3[:, 0, :], x3[:], start=True, stop=True).then_inc(full, 1)

                attention(b, o, 3, lambda h: K3[:], lambda h: K3b[:], lambda h: Q3[:, h % 12, :],
                          lambda h, kc: V3[:, kc, h, :], b3row[:], [(s_K3, b + 1), (s_V3, b + 1)])

            pe.wait_ge(const_v, 1)
            pe.wait_ge(const_p, 1)
            pe.wait_ge(ld_par, 64)
            for name in PROJ:
                project(name, prologue, 0)
            every_batch(pe, body)

        @block.scalar
        def _(act):
            def take(o, name):
                bank, n = o.at(name)
                act.wait_ge(gp_full[bank], n + 1)
                return GP[bank]

            def project(name, o):
                g = take(o, name)
                i = int(name[-1])
                if name[0] == "k":
                    act.activation(K0[:, 2 * i:2 * i + 2, :].rearrange("p c l -> p (c l)"), g[:], ACT.Copy)\
                        .then_inc(s_K0, 1)
                else:
                    s, w = divmod(i, 2)
                    act.activation(V0[:, s, w * 512:w * 512 + 512], g[:], ACT.Copy).then_inc(s_V0, 1)

            def attention(b, L, scale, middle=None, bank_done=None):
                steps = STEPS[L]

                def shift_rows(g):
                    n = MX_UNITS.index((L, g, "T"))
                    w = D if L in (0, 3) else P
                    act.wait_ge(mx_full[n % 2], b * (MX_N // 2) + n // 2 + 1)
                    act.activation(nmT[0:8, g % 2, 0:w], MX[n % 2][:].bitcast(BF16)[0:8, 0:w], ACT.Copy)\
                        .then_inc(nmT_ready, 1)

                def exp(g, u):
                    n = SC_BASE[L] + g * steps + u
                    kc = unit_heads(L, g, u)[1]
                    act.wait_ge(sc_full, SC_N * b + n + 1)
                    wait(act, pv_done, SC_N * b + n - 3)
                    if 4 <= n < 20:
                        act.wait_ge(ps_ready, 8 * b + (n - 4) // 2 + 1)
                    bias = {0: 0.0, 1: bcol[:, kc:kc + 1], 2: bcol[:, 2:3], 3: bcol[:, 3 + kc:4 + kc]}[L]
                    act.activation(Pr[:, n % 4, :], SC[n % 2][:], ACT.Exp, bias=bias, scale=scale)\
                        .then_inc(p_ready, 1)

                def cast(g):
                    j = 4 * L + g - 2
                    k, j = (b - 1, j + 16) if j < 0 else (b, j)
                    wait(act, mx_done, SC_N * k + SC_BASE[j // 4] + (j % 4 + 1) * STEPS[j // 4])
                    dst = Qb[:, g % 2]
                    if L == 0:
                        act.wait_ge(s_K0, 4 * b + g + 1)
                        act.activation(K0b[:, g % 2], K0[:, 2 * g:2 * g + 2, :], ACT.Copy)
                        act.wait_ge(s_Q0, 4 * b + g + 1)
                        src = Q0[:, HG * g:HG * g + HG, :]
                    elif L == 3:
                        act.wait_ge(s_Qx, 8 * b + 5 + g)
                        src = Q3[:, HG * (g % 3):HG * (g % 3) + HG, :]
                    else:
                        act.wait_ge(s_Qx, 8 * b + 2 * (L - 1) + g // 2 + 1)
                        dst, src = Qb[:, g % 2, :, 0:P], Q12[:, HG * g:HG * g + HG, :]
                    act.activation(dst, src, ACT.Copy).then_inc(s_Qb, 1)

                cast(0)
                cast(1)
                lead = steps + 2 if steps == 1 else steps + 3
                for g, u in order_of_maxima(L)[-1]:
                    if u == "T":
                        shift_rows(g)
                for g in range(2, NG):
                    if g * steps < lead:
                        cast(g)
                for n in range(NG * steps):
                    for g, u in order_of_maxima(L)[n]:
                        if u == "T":
                            shift_rows(g)
                    exp(*divmod(n, steps))
                    if bank_done and n == 10:
                        bank_done(0)
                    for g in range(2, NG):
                        if g * steps - lead == n:
                            cast(g)
                    if middle and n == 3 * steps - 1:
                        middle()

            def std3(b):
                act.wait_ge(s_v, b + 1)
                wait(act, st_out, 16 * b)
                act.activation(C3[:, 3, :], C3[:, 1, :], ACT.Sqrt).then_inc(s_std, 1)

            def mlp(b, which, between):
                for i in range(2):
                    h = slice(512 * i, 512 * i + 512)
                    act.wait_ge(s_X, 4 * b + 2 * which + i + 1)
                    act.activation(T[:, h], X[:, h], ACT.Square).then_inc(s_sq, 1)
                between()
                for i in range(2):
                    h = slice(512 * i, 512 * i + 512)
                    act.wait_ge(s_T, 4 * b + 2 * which + i + 1)
                    act.activation(T[:, h], T[:, h], ACT.Tanh, scale=GELU_C).then_inc(s_th, 1)

            def body(b):
                o = order_of(b)

                def fill(*names):
                    if not is_last(b):
                        for name in names:
                            project(name, o)

                def turned(name, dst, s):
                    g = take(o, name)
                    act.activation(dst, g[:, 0:D].rearrange("p (c k) -> p c k", c=2), ACT.Copy).then_inc(s, 1)

                def keys(name, K, Kb, bias, width, s):
                    g = take(o, name)
                    n = width and len(bias)
                    for m in range(n):
                        for dst in (K, Kb):
                            ins = act.activation(dst(m), g[:, m * width:m * width + width], ACT.Identity, bias=bias[m])
                    ins.then_inc(s, 1)

                attention(b, 0, 0.125, middle=None if is_first(b) else lambda: std3(b - 1))
                act.wait_ge(s_d0, b + 1)
                act.activation(sq0, d0, ACT.Square).then_inc(s_sq0, 1)
                g = take(o, "var")
                act.activation(sd0, g[:, 0:D], ACT.Sqrt, bias=epsc[:]).then_inc(s_sd0, 1)
                fill(PROJ[4], PROJ[5])
                turned("latT", hT[:, :, P:D], s_hT)
                fill(PROJ[6])
                keys("k1", lambda m: K1[:, m, :], lambda m: K1b[:, m, :], [col("kb1", 0), col("kb1", 1)], D, s_K1)
                attention(b, 1, 1.0 / 16)
                act.wait_ge(s_xa, 2 * b + 1)
                act.activation(junk, xa[:], ACT.Square, accum_out=stat[:, 0:1]).then_inc(s_ssq, 1)
                fill(PROJ[7], PROJ[8])
                turned("oT", oT[:], s_oT)
                mlp(b, 0, lambda: keys("k2", lambda m: K2[:, m, :], lambda m: K2b[:, m, :],
                                       [col("kb2", 0), col("kb2", 1)], P, s_K2))
                fill(PROJ[9], PROJ[10])
                turned("yT", oT[:], s_oT)
                attention(b, 2, 0.25)
                fill(PROJ[11])
                keys("k3", lambda m: K3[:], lambda m: K3b[:], [col("bk")], D, s_K3)
                turned("yT2", oT[:], s_oT)

                def squares():
                    act.wait_ge(s_v3, b + 1)
                    act.activation(V3[:, :, :, 8:16], V3[:, :, :, 0:8], ACT.Square).then_inc(s_V3, 1)
                mlp(b, 1, lambda: None)
                squares()
                def norm_sums():
                    act.wait_ge(s_xm, b + 1)
                    for i, (src, func) in enumerate(((xm, ACT.Copy), (xm, ACT.Square), (m3, ACT.Copy))):
                        act.activation(junk, src[:], func, accum_out=stat[:, 4 + i:5 + i]).then_inc(s_nst, 1)
                        act.wait_ge(s_nst, 3 * b + i + 1)

                def sums(i):
                    act.wait_ge(pv_done, SC_N * b + SC_BASE[3] + 8 * i + 8)
                    wait(act, st_u3, 16 * b)
                    act.activation(U3[:, 2 * i:2 * i + 2, :].rearrange("p g i -> p (g i)"), PV[(PV_BASE[3] + i) % 2][:],
                                   ACT.Copy).then_inc(s_U3, 1)
                attention(b, 3, 8.0 ** -0.5, middle=norm_sums, bank_done=sums)
                sums(1)

            act.wait_ge(const_v, 1)
            act.wait_ge(const_p, 1)
            act.wait_ge(ld_par, 64)
            for name in PROJ[4:]:
                project(name, prologue)
            every_batch(act, body)
            std3(B - 1)

        @block.vector
        def _(dve):
            chain = Chain(dve, v_step, V_STEPS)
            ending = Chain(dve, f_step, F_STEPS)
            apart = Apart(dve, gate[:, 1:2], v_apart, 6)

            def take(o, name):
                bank, n = o.at(name)
                dve.wait_ge(gp_full[bank], n + 1)
                return GP[bank]

            def project(name, o):
                g = take(o, name)
                i = int(name[-1])
                for r in range(2):
                    p = slice(64 * r, 64 * r + 64)
                    bias = colrange("rwb", 2 * i, 2 * i + 2)[p].unsqueeze(2).to_broadcast([64, 2, D])
                    ins = dve.tensor_tensor(Q0[p, 4 * i + r:4 * i + r + 3:2, :],
                                            g[p, :].rearrange("p (c l) -> p c l", c=2), bias, ALU.add)
                ins.then_inc(s_Q0, 1)

            def attention(b, L, after_step=None):
                steps = STEPS[L]
                halves = 2 if L in (0, 3) else 1

                def maxima(g, u):
                    n = MX_UNITS.index((L, g, u))
                    dve.wait_ge(mx_full[n % 2], b * (MX_N // 2) + n // 2 + 1)
                    if halves == 2:
                        dst, a = mx[:, g % 2, :, u], 2
                    else:
                        a = HG // steps
                        dst = mx[:, g % 2, 0, a * u:a * u + a]
                    dve.tensor_reduce(dst, MX[n % 2][:].rearrange("p (a k) -> p a k", a=a), AX_X, ALU.max,
                                      negate=True).then_inc(mx_done, 1)

                def split(g):
                    m, hi, lo = mx[:, g % 2, 0:halves], nm[:, g % 2, 0:halves, 0:4], nm[:, g % 2, 0:halves, 4:8]
                    dve.wait_ge(mx_done, SC_N * b + SC_BASE[L] + (g + 1) * steps)
                    chain.step(dve.tensor_copy(hi, m))
                    dve.tensor_tensor(lo, m, hi, ALU.subtract).then_inc(nm_ready, 1)

                def maxima_before(n):
                    for g, u in order_of_maxima(L)[n]:
                        if u != "T":
                            maxima(g, u)
                        if u == steps - 1:
                            split(g)

                maxima_before(-1)
                for n in range(NG * steps):
                    maxima_before(n)
                    if after_step:
                        after_step(n)

            def quotient0(b, c):
                dve.wait_ge(den_done, 8 * b + c + 1)
                wait(dve, s_Ax, 4 * b) if c == 0 else dve.wait_ge(s_A0, 8 * b + c)
                chain.step(dve.reciprocal(rec, PV[c % 2][:, D:2 * D]))
                dve.tensor_tensor(A0[:, c, :], PV[c % 2][:, 0:D], rec, ALU.mult).then_inc(s_A0, 1)

            def quotient(b, L, i):
                bank = PV[(PV_BASE[L] + i) % 2][:, 0:D]
                used = 2 * (L - 1) + i
                apart.wait((s_Ax, 4 * b + used) if used else (s_A0, 8 * b + 8),
                           (pv_done, SC_N * b + SC_BASE[L] + (2 * i + 2) * STEPS[L]))
                chain.step(dve.stream_shuffle(den, bank, [16 + r % 16 for r in range(32)]))
                chain.step(dve.reciprocal(den, den))
                dve.tensor_tensor(Ax[:, 2 * i:2 * i + 2, :].rearrange("p g k -> p (g k)"), bank, den, ALU.mult)\
                    .then_inc(s_Ax, 1)

            def blocks12(o, name, bias):
                g = take(o, name)
                for i in range(2):
                    dve.scalar_tensor_tensor(
                        out=Q12[:, 8 * i:8 * i + 8, :], in0=g[:, i * P:i * P + P].unsqueeze(1).to_broadcast([P, 8, P]),
                        scalar=col(bias, i), in1=hmask[:, 0:8].unsqueeze(2).to_broadcast([P, 8, P]),
                        op0=ALU.add, op1=ALU.mult).then_inc(s_Qx, 1)

            def block3(b, o, i):
                g = take(o, "q3")
                at = HG * (i % 3)
                if i == 3:
                    dve.wait_ge(sc_full, SC_N * b + SC_BASE[3] + 4)
                dve.scalar_tensor_tensor(
                    out=Q3[:, at:at + HG, :], in0=g[:, 0:D].unsqueeze(1).to_broadcast([P, HG, D]),
                    scalar=col("bq"), in1=hmask[:, 8 + HG * i:8 + HG * i + HG].unsqueeze(2).to_broadcast([P, HG, D]),
                    op0=ALU.add, op1=ALU.mult).then_inc(s_Qx, 1)

            def mlp(b, o, names, bias, which):
                for i, name in enumerate(names):
                    g = take(o, name)
                    h = slice(512 * i, 512 * i + 512)
                    dve.tensor_tensor(X[:, h].rearrange("p (f k) -> p f k", k=P),
                                      g[:].rearrange("p (f k) -> p f k", k=P),
                                      colrange(bias, 4 * i, 4 * i + 4).unsqueeze(2).to_broadcast([P, 4, P]),
                                      ALU.add).then_inc(s_X, 1)
                for i in range(2):
                    h = slice(512 * i, 512 * i + 512)
                    dve.wait_ge(s_sq, 4 * b + 2 * which + i + 1)
                    chain.step(dve.tensor_scalar(T[:, h], T[:, h], GELU_A, 1.0, ALU.mult, ALU.add))
                    dve.tensor_tensor(T[:, h], T[:, h], X[:, h], ALU.mult).then_inc(s_T, 1)
                for i in range(2):
                    h = slice(512 * i, 512 * i + 512)
                    dve.wait_ge(s_th, 4 * b + 2 * which + i + 1)
                    dve.scalar_tensor_tensor(out=G[:, h], in0=T[:, h], scalar=1.0, in1=X[:, h], op0=ALU.add,
                                             op1=ALU.mult).then_inc(s_G, 1)

            def layer_norm(b, src, ready, w, bias, k):
                dve.wait_ge(*ready)
                chain.step(dve.bn_stats(stat[:, 8:14], src[:]), apart)
                chain.step(dve.bn_aggr(stat[:, 14:16], stat[:, 8:14]))
                dve.tensor_scalar(stat[:, 1:2], stat[:, 15:16], 1e-5, None, ALU.add).then_inc(s_var, 1)
                dve.wait_ge(s_pow, 3 * b + k)
                chain.step(dve.tensor_scalar(xb[:], src[:], stat[:, 14:15], stat[:, 2:3], ALU.subtract, ALU.mult))
                chain.step(dve.tensor_tensor(xb[:], xb[:], row(w), ALU.mult))
                dve.tensor_tensor(xb[:], xb[:], row(bias), ALU.add).then_inc(s_xb, 1)

            def end3(b):
                ending.begin(b)
                dve.wait_ge(ld_c3, 16 * 3 * NG * (b + 1))
                ending.step(dve.reciprocal(C3[:, 2, :], C3[:, 2, :]))
                ending.step(dve.tensor_tensor(C3[:, 0, :], C3[:, 0, :], C3[:, 2, :], ALU.mult))
                ending.step(dve.tensor_tensor(C3[:, 1, :], C3[:, 1, :], C3[:, 2, :], ALU.mult))
                ending.step(dve.tensor_tensor(C3[:, 2, :], C3[:, 0, :], C3[:, 0, :], ALU.mult))
                ending.step(dve.tensor_tensor(C3[:, 1, :], C3[:, 1, :], C3[:, 2, :], ALU.subtract))
                dve.tensor_scalar(C3[:, 1, :], C3[:, 1, :], 0.0, None, ALU.max).then_inc(s_v, 1)

            def output3(b):
                dve.wait_ge(s_std, b + 1)
                dve.wait_ge(s_xn, b + 1)
                ending.step(dve.tensor_tensor(C3[:, 3, :], C3[:, 3, :], xn[:], ALU.mult))
                ending.step(dve.tensor_tensor(C3[:, 3, :], C3[:, 3, :], C3[:, 0, :], ALU.add))
                dve.tensor_tensor(C3[:, 3, :], C3[:, 3, :], m3[:], ALU.mult).then_inc(s_o3, 1)
                ending.end()

            def body(b):
                o = order_of(b)
                chain.begin(b)
                apart.begin(b)

                def fill(*names):
                    if not is_last(b):
                        for name in names:
                            project(name, o)

                def steps0(n):
                    if n == 4:
                        wait(dve, st_u3, 16 * b)
                    if n >= 4 and n % 2 == 0:
                        quotient0(b, (n - 4) // 2)
                    if n == 9 and not is_first(b):
                        end3(b - 1)
                    if n == 15 and not is_first(b):
                        output3(b - 1)
                attention(b, 0, steps0)
                for c in (6, 7):
                    quotient0(b, c)
                dve.wait_ge(ld_res, 16 * b + 16)
                fill(PROJ[0])
                g = take(o, "wo")
                dve.scalar_tensor_tensor(out=x0, in0=g[:, 0:D], scalar=col("bo"), in1=zR[:], op0=ALU.add,
                                         op1=ALU.add).then_inc(s_x0, 1)
                g = take(o, "mean")
                dve.wait_ge(s_x0, b + 1)
                dve.tensor_tensor(d0, x0, g[:, 0:D], ALU.subtract).then_inc(s_d0, 1)
                fill(PROJ[1], PROJ[2], PROJ[3])
                dve.wait_ge(s_sd0, b + 1)
                chain.step(dve.reciprocal(x0, sd0))
                dve.tensor_tensor(lat, d0, x0, ALU.mult).then_inc(s_lat, 1)
                blocks12(o, "q1", "qb1")
                g = take(o, "v1")
                dve.tensor_tensor(V1[:, :, :, 0:16], g[:].rearrange("p (c h d) -> p c h d", c=2, d=16),
                                  row("vb1").rearrange("p (h d) -> p h d", d=16).unsqueeze(1)
                                  .to_broadcast([P, 2, NH, 16]), ALU.add).then_inc(s_V1, 1)
                attention(b, 1, lambda n: quotient(b, 1, 0) if n == 6 else None)
                quotient(b, 1, 1)
                g = take(o, "o1")
                dve.wait_ge(s_res1, 2 * b + 1)
                dve.tensor_tensor(xa[:], g[:, 0:D], res1[:], ALU.add).then_inc(s_xa, 1)
                dve.wait_ge(s_ssq, b + 1)
                dve.tensor_scalar(stat[:, 1:2], stat[:, 0:1], 1.0 / D, 1e-6, ALU.mult, ALU.add).then_inc(s_var, 1)
                dve.wait_ge(s_pow, 3 * b + 1)
                dve.wait_ge(s_xa, 2 * b + 1)
                dve.scalar_tensor_tensor(out=xb[:], in0=xa[:], scalar=stat[:, 2:3], in1=row("pw"), op0=ALU.mult,
                                         op1=ALU.mult).then_inc(s_xb, 1)
                mlp(b, o, ("m0", "m1"), "b1", 0)
                g = take(o, "w2")
                dve.wait_ge(s_res2, 2 * b + 1)
                dve.scalar_tensor_tensor(out=x1[:], in0=g[:, 0:D], scalar=0.5, in1=res2[:], op0=ALU.mult,
                                         op1=ALU.add).then_inc(s_x1, 1)
                layer_norm(b, x1, (s_x1, b + 1), "ln1w", "ln1b", 2)
                blocks12(o, "q2", "qb2")
                g = take(o, "v2")
                dve.tensor_tensor(V2[:, :, 0:16], g[:, 0:D].rearrange("p (h d) -> p h d", d=16),
                                  row("vb2").rearrange("p (h d) -> p h d", d=16), ALU.add).then_inc(s_V2, 1)
                attention(b, 2, lambda n: quotient(b, 2, 0) if n == 3 else None)
                quotient(b, 2, 1)
                g = take(o, "o2")
                dve.wait_ge(s_res1, 2 * b + 2)
                dve.tensor_tensor(xa[:], g[:, 0:D], res1[:], ALU.add).then_inc(s_xa, 1)
                layer_norm(b, xa, (s_xa, 2 * b + 2), "ln2w", "ln2b", 3)
                mlp(b, o, ("n0", "n1"), "fcb", 1)
                g = take(o, "v3")
                dve.tensor_tensor(V3[:, :, :, 0:8], g[:, 0:D].rearrange("p (c h d) -> p c h d", c=2, d=8),
                                  row("bv").rearrange("p (h d) -> p h d", d=8).unsqueeze(1)
                                  .to_broadcast([P, 2, NH, 8]), ALU.add).then_inc(s_v3, 1)
                g = take(o, "w4")
                dve.wait_ge(s_res2, 2 * b + 2)
                dve.scalar_tensor_tensor(out=x3[:], in0=g[:, 0:D], scalar=0.5, in1=res2[:], op0=ALU.mult,
                                         op1=ALU.add).then_inc(s_x3, 1)
                for i in range(3):
                    block3(b, o, i)

                def steps3(n):
                    if n == 3:
                        block3(b, o, 3)
                    if n == 14:
                        dve.wait_ge(s_nst, 3 * b + 3)
                        dve.reciprocal(stat[:, 7:8], stat[:, 6:7]).then_inc(s_ninv, 1)
                attention(b, 3, steps3)
                chain.end()
                apart.end()

            dve.memset(Q0[:], 0.0)
            dve.memset(nmT[:], 0.0)
            dve.memset(V1[:], 1.0)
            dve.memset(V2[:], 1.0)
            dve.memset(epsc[:], 1e-5)
            dve.wait_ge(ld_par, 64)
            dve.tensor_copy(identb[:], ident[:])
            dve.tensor_copy(sel[:], sel32).then_inc(const_v, 1)
            dve.wait_ge(const_v, 1)
            for name in PROJ[:4]:
                project(name, prologue)
            dve.wait_ge(ld_rows, 16)
            every_batch(dve, body)
            end3(B - 1)
            output3(B - 1)

        @block.gpsimd
        def _(pool):
            chain = Chain(pool, p_step, P_STEPS)
            apart = Apart(pool, gate[:, 0:1], p_apart, 3)

            def power(b, k):
                pool.wait_ge(s_var, 3 * b + k)
                pool.tensor_tensor(stat[:, 2:3], stat[:, 1:2], half[:], ALU.pow).then_inc(s_pow, 1)

            def body(b):
                chain.begin(b)
                apart.begin(b)
                for c in range(8):
                    n = 2 * c
                    pool.wait_ge(p_ready, SC_N * b + n + 2)
                    wait(pool, den_done, 8 * b + c - 1)
                    pool.tensor_tensor(Psum[:, c % 2, :], Pr[:, n % 4, :], Pr[:, (n + 1) % 4, :], ALU.add)\
                        .then_inc(ps_ready, 1)
                apart.wait((s_o3, b), (ld_msk, 112 * b + 112))
                for dst, src, value in (
                        (b1row[0:1, 0:P], m1row[0:1, :], NEG), (b2row[0:1, :], m2row[0:1, :], NEG),
                        (b3row[0:1, :], m3row[0:1, :], NEG), (bcol[:, 0:1], m1col[:], NEG / 16),
                        (bcol[:, 2:3], m2col[:], NEG / 4), (bcol[:, 3:5], m3col[:], NEG * 8.0 ** -0.5)):
                    pool.tensor_scalar(dst, src, 0.0, value, ALU.is_equal, ALU.mult).then_inc(s_msk, 1)
                pool.tensor_scalar(m3[:], m3row[:], 0.0, None, ALU.add).then_inc(s_msk, 1)
                pool.wait_ge(s_lat, b + 1)
                pool.tensor_tensor(res1[:], lat, row("ob1"), ALU.add).then_inc(s_res1, 1)
                pool.tensor_tensor(res2[:], lat, row("b2"), ALU.add).then_inc(s_res2, 1)
                power(b, 1)
                power(b, 2)
                pool.wait_ge(s_x1, b + 1)
                pool.tensor_tensor(res1[:], x1[:], row("cb"), ALU.add).then_inc(s_res1, 1)
                power(b, 3)
                pool.tensor_tensor(res2[:], xa[:], row("pb"), ALU.add).then_inc(s_res2, 1)
                pool.wait_ge(s_x3, b + 1)
                pool.wait_ge(s_msk, N_MSK * (b + 1))
                pool.tensor_tensor(xm[:], x3[:], m3[:], ALU.mult).then_inc(s_xm, 1)
                pool.wait_ge(s_ninv, b + 1)
                chain.step(pool.tensor_tensor(stat3[:, 0:1], stat[:, 4:5], stat[:, 7:8], ALU.mult))
                chain.step(pool.tensor_tensor(stat3[:, 1:2], stat[:, 5:6], stat[:, 7:8], ALU.mult))
                chain.step(pool.tensor_tensor(stat3[:, 2:3], stat3[:, 0:1], stat3[:, 0:1], ALU.mult))
                chain.step(pool.tensor_tensor(stat3[:, 1:2], stat3[:, 1:2], stat3[:, 2:3], ALU.subtract), apart)
                chain.step(pool.tensor_scalar(stat3[:, 1:2], stat3[:, 1:2], 0.0, 1e-5, ALU.max, ALU.add))
                chain.step(pool.tensor_tensor(stat3[:, 1:2], stat3[:, 1:2], half[:], ALU.pow), apart)
                chain.step(pool.tensor_scalar(xn[:], xm[:], stat3[:, 0:1], stat3[:, 1:2], ALU.subtract, ALU.mult))
                pool.tensor_tensor(xn[:], xn[:], m3[:], ALU.mult).then_inc(s_xn, 1)
                chain.end()
                apart.end()

            pool.memset(b1row[:], 0.0)
            pool.memset(b2row[:], 0.0)
            pool.memset(b3row[:], 0.0)
            pool.memset(bcol[:], 0.0)
            pool.memset(half[:], -0.5)
            pool.memset(ones[:], 1.0)
            pool.memset(mean_w[:], 1.0 / P).then_inc(const_p, 1)
            pool.wait_ge(const_p, 1)
            pool.wait_ge(ld_rows, 16)
            every_batch(pool, body)


def launch_constants(np):
    ident = np.eye(P, dtype=np.float32)
    p = np.arange(P)
    hmask = np.concatenate([p[:, None] // 16 == np.arange(8)[None], p[:, None] // 8 == np.arange(16)[None]], axis=1)
    sel = np.zeros((P, HG + 1, P), np.float32)
    for h in range(HG):
        sel[h, h] = sel[HG + h, h] = 1.0
    sel[0, HG] = 1.0
    return ident, hmask.astype(np.float32), sel


def kernel(**inputs):
    import numpy as np
    import concourse.bacc as bacc
    from concourse.bass_utils import run_bass_kernel_spmd

    a = {k: np.asarray(v) for k, v in inputs.items()}
    l1 = {k[9:]: v for k, v in a.items() if k.startswith("L1_")}
    l2 = {k[9:]: v for k, v in a.items() if k.startswith("L2_")}

    def chunks(w):
        return w.reshape(-1, P, w.shape[1]).transpose(1, 0, 2)

    def columns(v):
        return v.reshape(-1, P).T

    def slots(w):
        out = np.zeros((NG, HG, 32, w.shape[1]), w.dtype)
        out[:, :, :16] = w.reshape(NG, HG, 16, -1)
        return out.reshape(NG, P, -1).transpose(1, 0, 2)

    w0 = np.stack([a["L0_xattn_" + n].T for n in ("Wqkv0", "Winj0", "Wqkv1", "Winj1")], axis=1)
    w0 = w0.reshape(P, 4, 6, 512).transpose(2, 0, 1, 3)
    kv_w, kv_b = l1["kv_w"].reshape(D, D, 2), l1["kv_b"].reshape(D, 2)
    parts = {"bo": a["L0_xattn_bo"], "rwb": a["L0_xattn_r_w_bias"].reshape(-1), "qb1": l1["q_b"],
             "kb1": kv_b[:, 0], "b1": l1["mlp_b1"], "qb2": l2["q_b"], "kb2": l2["k_b"], "fcb": l2["fc_b"],
             "bq": a["L3_xattn_bq"], "bk": a["L3_xattn_bk"]}
    rows = {"vb1": kv_b[:, 1], "ob1": l1["out_b"], "pw": l1["postnorm_w"], "b2": l1["mlp_b2"],
            "ln1w": l2["ln1_w"], "ln1b": l2["ln1_b"], "vb2": l2["v_b"], "cb": l2["cproj_b"],
            "ln2w": l2["ln2_w"], "ln2b": l2["ln2_b"], "pb": l2["proj_b"], "bv": a["L3_xattn_bv"]}
    ident, hmask, sel = launch_constants(np)
    arrays = {
        "z_in": a["x"], "ctxT_in": a["ctx_2048"].transpose(0, 2, 1).reshape(B, 2, P, P).transpose(0, 2, 1, 3),
        "ctx_in": a["ctx_2048"],
        "mask1": a["mask_BxS2_ik0"].reshape(B, 1, P),
        "mask2": a["mask_BxS2_bf1"].view(np.uint8).reshape(B, 1, P),
        "mask3": a["mask_Bx1x2048_bf1"].view(np.uint8).reshape(B, 1, D),
        "w0": w0, "wo": chunks(a["L0_xattn_Wo"].T),
        "w1qk": np.stack([chunks(l1["q_w"]), chunks(kv_w[:, :, 0])], axis=1),
        "w1v": chunks(kv_w[:, :, 1]), "w1o": slots(l1["out_w"]),
        "w1a": chunks(l1["mlp_w1"]), "w1b": chunks(l1["mlp_w2"]),
        "w2qkv": np.stack([chunks(l2[n]) for n in ("q_w", "k_w", "v_w")], axis=1),
        "w2o": slots(l2["cproj_w"]), "w2a": chunks(l2["fc_w"]), "w2b": chunks(l2["proj_w"]),
        "w3": np.stack([a["L3_xattn_" + n].T for n in ("Wq", "Wk", "Wv")], axis=1),
        "cols_in": np.concatenate([columns(parts[n]) for n in COLS], axis=1),
        "rows_in": np.concatenate([rows[n] for n in ROWS]).reshape(1, NROWS),
        "ident_in": ident, "hmask_in": hmask, "sel_in": sel,
    }
    arrays = {k: np.ascontiguousarray(v) for k, v in arrays.items()}
    nc = bacc.Bacc("TRN2", target_bir_lowering=False, num_devices=1)
    args = [nc.dram_tensor(n, v.shape, mybir.dt.from_np(v.dtype), kind="ExternalInput").ap()
            for n, v in arrays.items()]
    out = nc.dram_tensor("out", (B, P, D), F32, kind="ExternalOutput").ap()
    build(nc, *args, out)
    r = run_bass_kernel_spmd(nc, [arrays], core_ids=[0])
    return r.results[0]["out"]
```

```python
from contextlib import ExitStack

import concourse.bass as bass
from concourse import mybir
from concourse.alu_op_type import AluOpType as ALU

F32 = mybir.dt.float32
BF16 = mybir.dt.bfloat16
I32 = mybir.dt.int32
U8 = mybir.dt.uint8
ACT = mybir.ActivationFunctionType
AX_X = mybir.AxisListType.X

P = 128
B = 8
D = 256
NH = 16
HG = 4
NG = NH // HG
NQKV = 3 * NH * 64
NEG = -(2.0 ** 100)
GELU_C = 0.7978845608028654
GELU_A = 0.044715

COLS = {}
for _name, _n in (("bo", 1), ("rwb", 8), ("qb1", 2), ("kb1", 2), ("b1", 8), ("qb2", 2), ("kb2", 2),
                  ("fcb", 8), ("bq", 1), ("bk", 1), ("pw", 2), ("ln1w", 2), ("ln1b", 2), ("ln2w", 2), ("ln2b", 2)):
    COLS[_name] = (sum(n for _, n in COLS.values()), _n)
NCOLS = sum(n for _, n in COLS.values())
ROWS = {}
for _name, _n in (("vb1", D), ("ob1", D), ("b2", D), ("vb2", D),
                  ("cb", D), ("pb", D), ("bv", P)):
    ROWS[_name] = (sum(n for _, n in ROWS.values()), _n)
NROWS = sum(n for _, n in ROWS.values())

STEPS = {0: 4, 1: 2, 2: 1, 3: 4}
SC_BASE = {0: 0, 1: 16, 2: 24, 3: 28}
SC_N = 44
PV_BASE = {0: 0, 1: 10, 2: 14, 3: 18}
PV_N = 20
MX_UNITS = [(L, g, u) for L in (0, 1) for g in range(NG) for u in [*range(STEPS[L]), "T"]]
MX_UNITS += [(2, 0, 0), (2, 1, 0), (2, 0, "T"), (2, 2, 0), (2, 3, 0), (2, 2, "T")]
MX_UNITS += [(3, g, u) for g in range(NG) for u in [*range(STEPS[3]), "T"]]
MX_N = len(MX_UNITS)
SHIFTS = [(L, g) for L, g, u in MX_UNITS if u == "T"]
SHIFT_N = len(SHIFTS)

N_MSK = 7
V_STEPS = 8 + 2 + 8 * 2 + 4
P_STEPS = 7
F_STEPS = 7

PROJ = [f"qp{i}" for i in range(4)] + [f"kp{i}" for i in range(4)] + [f"vp{i}" for i in range(4)]
BODY = ["wo", "kp0", "kp1", "kp2", "q1", "k1", "v1", "v1c", "qp0", "o1", "qp1", "oT", "vp0", "m0", "m1", "k2",
        "vp1", "w2", "qp2", "v2", "yT", "vp2", "q2", "kp3", "o2", "k3", "yT2", "v3", "n0", "n1", "vp3", "w4",
        "q3", "qp3"]
LAST = [u for u in BODY if u not in PROJ]


TAKEN = {"wo": ("x0", 1, 1), 
         "q1": ("Qx", 12, 4), "k1": ("K1", 1, 1), "v1": ("V1", 2, 1), "v1c": ("V1", 2, 2), "o1": ("xa", 2, 1), "oT": ("oT", 3, 1),
         "m0": ("X", 4, 1), "m1": ("X", 4, 2), "k2": ("K2", 1, 1), "w2": ("x1", 1, 1), "yT": ("oT", 3, 2),
         "q2": ("Qx", 12, 8), "v2": ("V2", 1, 1), "o2": ("xa", 2, 2), "k3": ("K3", 1, 1),
         "yT2": ("oT", 3, 3), "n0": ("X", 4, 3), "n1": ("X", 4, 4), "v3": ("v3", 1, 1), "w4": ("x3", 1, 1),
         "q3": ("Qx", 12, 12)}
TAKEN.update({u: ({"q": "Q0", "k": "K0", "v": "V0"}[u[0]], 4, int(u[-1]) + 1) for u in PROJ})


def build(nc, z_in, ctxT_in, ctx_in, mask1, mask2, mask3, w0, wo, w1qk, w1v, w1o, w1a, w1b,
          w2qkv, w2o, w2a, w2b, w3, cols_in, rows_in, ident_in, hmask_in, sel_in, out):
    with ExitStack() as stack:
        def sb(name, shape, dt=F32):
            return stack.enter_context(nc.sbuf_tensor(name, shape, dt))

        def ps(name):
            return stack.enter_context(nc.psum_tensor(name, [P, 512], F32))

        def sem(name):
            return stack.enter_context(nc.semaphore(name))

        MX = [ps(f"MX{i}") for i in range(2)]
        SC = [ps(f"SC{i}") for i in range(2)]
        PV = [ps(f"PV{i}") for i in range(2)]
        GP = [ps(f"GP{i}") for i in range(2)]

        W0 = sb("W0", [P, 6, 4, 512])
        WO = sb("WO", [P, 8, P])
        W1QK = sb("W1QK", [P, 2, 2, D])
        W1V = sb("W1V", [P, 2, D])
        W1O = sb("W1O", [P, NG, D])
        W2QKV = sb("W2QKV", [P, 3, 2, D])
        W2O = sb("W2O", [P, NG, D])
        WA = sb("WA", [P, 2, 1024])
        WB = sb("WB", [P, 8, D])
        W3 = sb("W3", [P, 3, P])
        cols = sb("cols", [P, NCOLS])
        rows = sb("rows", [P, NROWS])
        ident = sb("ident", [P, P])
        identb = sb("identb", [P, P], BF16)
        hmask = sb("hmask", [P, 8 + 16])
        sel = sb("sel", [P, HG + 1, P], BF16)
        sel2 = sb("sel2", [P, 8, P], BF16)
        ones = sb("ones", [P, 64])
        stat0 = sb("stat0", [P, 20])

        work = sb("work", [P, 3 * HG * D])
        sel32 = work[:, 0:(HG + 9) * P].rearrange("p (h k) -> p h k", k=P)
        A0 = work[:, 0:8 * D].rearrange("p (c l) -> p c l", l=D)
        Q12 = work[:, 0:NH * P].rearrange("p (h l) -> p h l", l=P)
        Q3 = work[:].rearrange("p (h l) -> p h l", l=D)
        X, T, G = (work[:, 1024 * i:1024 * i + 1024] for i in range(3))

        zP = sb("zP", [P, D])
        uP = sb("uP", [P, D])
        zR = sb("zR", [P, D])
        uC = sb("uC", [P, D])
        hT = sb("hT", [P, 2, D])
        Q0 = sb("Q0", [P, NH, D])
        K0 = sb("K0", [P, 8, D])
        K0b = sb("K0b", [P, 2, 2, D], BF16)
        Qb = sb("Qb", [P, 2, HG, D], BF16)
        V0 = sb("V0", [P, 2, 1024])
        Pr = sb("Pr", [P, 4, 512])
        Psum = sb("Psum", [P, 2, 512])
        mx = sb("mx", [P, 2, 2, HG])
        nm = sb("nm", [P, 2, 2, 8], BF16)
        nmT = sb("nmT", [P, 2, D], BF16)
        U3 = sb("U3", [P, NG, D])
        x0, lat, junk, rec = (U3[:, i, :] for i in range(4))
        K1 = sb("K1", [P, 2, D])
        K1b = sb("K1b", [P, 2, D], BF16)
        V1 = sb("V1", [P, 2, NH, 32])
        K2 = sb("K2", [P, 2, P])
        K2b = sb("K2b", [P, 2, P], BF16)
        V2 = sb("V2", [P, NH, 32])
        K3 = sb("K3", [P, D])
        K3b = sb("K3b", [P, D], BF16)
        V3 = V1
        den = rec[:, 0:P]
        Ax = sb("Ax", [P, NG, P])
        junk3 = Ax[:, 0:2, :].rearrange("p g k -> p (g k)")
        res1 = sb("res1", [P, D])
        res2 = sb("res2", [P, D])
        xa = sb("xa", [P, D])
        xb = sb("xb", [P, D])
        oT = sb("oT", [P, 2, P])
        x1 = sb("x1", [P, D])
        x3 = x1
        stat = sb("stat", [P, 16])
        gate = sb("gate", [P, 2])
        half = sb("half", [P, 1])
        m1row = sb("m1row", [P, P], I32)
        m1col = sb("m1col", [P, 1], I32)
        m2row = sb("m2row", [P, P], U8)
        m2col = sb("m2col", [P, 1], U8)
        m3row = sb("m3row", [P, D], U8)
        m3col = sb("m3col", [P, 2], U8)
        b1row = sb("b1row", [P, D], BF16)
        b2row = sb("b2row", [P, P], BF16)
        b3row = sb("b3row", [P, D], BF16)
        bcol = sb("bcol", [P, 5])
        m3 = sb("m3", [P, D])
        xm = sb("xm", [P, D])
        xn = xm
        stat3 = sb("stat3", [P, 4])
        C3 = sb("C3", [P, 4, D])
        scratch = nc.dram_tensor("scratch", [P, NG, D], F32, kind="Internal").ap()

        def col(name, i=0):
            return cols[:, COLS[name][0] + i:COLS[name][0] + i + 1]

        def colrange(name, a, b):
            return cols[:, COLS[name][0] + a:COLS[name][0] + b]

        def row(name):
            return rows[:, ROWS[name][0]:ROWS[name][0] + ROWS[name][1]]

        ld_w0 = [sem(f"ld_w0_{i}") for i in range(6)]
        ld_proj, ld_cols, ld_par, ld_rows, ld_wo, ld_w1, ld_w2, ld_w3, ld_mlp, ld_ctx, ld_res, ld_msk, ld_c3, st_u3, st_out = (
            sem(n) for n in ("ld_proj", "ld_cols", "ld_par", "ld_rows", "ld_wo", "ld_w1", "ld_w2", "ld_w3", "ld_mlp", "ld_ctx",
                             "ld_res", "ld_msk", "ld_c3", "st_u3", "st_out"))
        const_p, const_v = sem("const_p"), sem("const_v")
        mx_full = [sem(f"mx_full{i}") for i in range(2)]
        gp_full = [sem(f"gp_full{i}") for i in range(2)]
        sc_full, pv_done, den_done = sem("sc_full"), sem("pv_done"), sem("den_done")
        mx_done, s_hi, nm_ready, nmT_ready, p_ready, ps_ready = (
            sem(n) for n in ("mx_done", "s_hi", "nm_ready", "nmT_ready", "p_ready", "ps_ready"))
        (s_Q0, s_Qb, s_K0, s_V0, s_A0, s_x0, s_x0T, s_var0, s_pow0, s_latT, s_lat, s_hT, s_Qx, s_K1, s_K1b, s_V1, s_K2,
         s_K2b, s_V2, s_K3, s_K3b, s_v3, s_V3, s_Ax, s_U3) = (sem("s_" + n) for n in (
             "Q0", "Qb", "K0", "V0", "A0", "x0", "x0T", "var0", "pow0", "latT", "lat", "hT", "Qx", "K1", "K1b", "V1", "K2",
             "K2b", "V2", "K3", "K3b", "v3", "V3", "Ax", "U3"))
        (s_res1, s_res2, s_xa, s_ssq, s_var, s_pow, s_xb, s_oT, s_X, s_sq, s_T, s_th, s_G, s_x1, s_x3) = (
            sem("s_" + n) for n in ("res1", "res2", "xa", "ssq", "var", "pow", "xb", "oT", "X", "sq", "T", "th",
                                    "G", "x1", "x3"))
        (s_msk, s_xm, s_nst, s_ninv, s_xn, s_v, s_std, s_o3) = (
            sem("s_" + n) for n in ("msk", "xm", "nst", "ninv", "xn", "v", "std", "o3"))
        v_step, p_step, f_step, v_apart, p_apart = (
            sem(n) for n in ("v_step", "p_step", "f_step", "v_apart", "p_apart"))

        def is_first(b):
            return isinstance(b, int) and b == 0

        def is_last(b):
            return isinstance(b, int) and b == B - 1

        class Order:

            def __init__(self, names, base, b):
                self.names, self.base, self.b = names, base, b

            def at(self, name):
                n = self.names.index(name)
                return n % 2, self.base + n // 2

            def bank_taken(self, name):
                n = self.names.index(name) - 2
                if n < 0 and self.b is None:
                    return None
                if n < 0:
                    name, k = (PROJ[n], 0) if is_first(self.b) else (BODY[n], self.b - 1)
                else:
                    name = self.names[n]
                    k = (0 if self.b is None else self.b + 1) if name in PROJ else self.b
                tile, per_batch, count = TAKEN[name]
                return by_tile[tile], per_batch * k + count

        by_tile = {"x0": s_x0,  "Qx": s_Qx, "K1": s_K1, "V1": s_V1,
                   "xa": s_xa, "oT": s_oT, "X": s_X, "K2": s_K2, "x1": s_x1, "V2": s_V2, "K3": s_K3,
                   "v3": s_v3, "x3": s_x3, "Q0": s_Q0, "K0": s_K0, "V0": s_V0}

        def order_of(b):
            return Order(LAST if is_last(b) else BODY, b * (len(BODY) // 2) + len(PROJ) // 2, b)

        prologue = Order(PROJ, 0, None)

        def mx_bank_taken(b, n):
            L, g, u = MX_UNITS[n - 2]
            k = b - 1 if n < 2 else b
            if u == "T":
                return nmT_ready, SHIFT_N * k + SHIFTS.index((L, g)) + 1
            return mx_done, SC_N * k + SC_BASE[L] + g * STEPS[L] + u + 1

        def pv_bank_taken(b, m):
            k, m = (b - 1, m + PV_N - 2) if m < 2 else (b, m - 2)
            if m < 8:
                return s_A0, 8 * k + m + 1
            if m < PV_BASE[1]:
                return (s_hT, k + 1) if m == 8 else (s_lat, k + 1)
            if m < PV_BASE[3]:
                return s_Ax, 8 * k + m - PV_BASE[1] + 1
            return s_U3, 2 * k + m - PV_BASE[3] + 1

        def wait(eng, s, value):
            if isinstance(value, int) and value <= 0:
                return
            eng.wait_ge(s, value)

        class Apart:

            def __init__(self, eng, scratch, s, per_batch):
                self.eng, self.scratch, self.s, self.per_batch = eng, scratch, s, per_batch

            def begin(self, b):
                self.b, self.n = b, 0

            def wait(self, *waits):
                for s, v in waits:
                    wait(self.eng, s, v)
                wait(self.eng, self.s, self.b * self.per_batch + self.n)
                self.eng.tensor_tensor(self.scratch, half[:], half[:], ALU.add).then_inc(self.s, 1)
                self.n += 1

            def end(self):
                assert self.n == self.per_batch, self.n

        class Chain:

            def __init__(self, eng, s, per_batch):
                self.eng, self.s, self.per_batch = eng, s, per_batch

            def begin(self, b):
                self.b, self.n = b, 0

            def step(self, instruction, apart=None):
                instruction.then_inc(self.s, 1)
                self.n += 1
                if apart is not None:
                    apart.wait((self.s, self.b * self.per_batch + self.n))
                else:
                    self.eng.wait_ge(self.s, self.b * self.per_batch + self.n)

            def end(self):
                assert self.n == self.per_batch, self.n

        def shifts(b, L, g):
            return SHIFT_N * b + SHIFTS.index((L, g // 2 * 2 if L == 2 else g)) + 1

        def unit_heads(L, g, u):
            if L in (0, 3):
                h = HG * g + 2 * (u // 2)
                return [h, h + 1], u % 2, D
            return list(range(HG * g, HG * g + HG)), u if L == 1 else 0, P

        def order_of_maxima(L):
            steps = STEPS[L]
            before = [[] for _ in range(NG * steps + 1)]
            if L == 2:
                before[-1], before[0], before[1] = [(0, 0), (1, 0), (0, "T"), (2, 0)], [(3, 0)], [(2, "T")]
                return before
            for _, g, u in (unit for unit in MX_UNITS if unit[0] == L):
                at = g * steps - 1 if u == "T" else g * steps + u - steps - 1
                before[max(at, -1)].append((g, u))
            return before

        EARLY = {11: 2, 12: 2, 13: 1, 14: 1}

        def early_maxima(n):
            units = order_of_maxima(0)[-1]
            if n is None:
                return units
            at = sum(count for m, count in EARLY.items() if m < n)
            return units[at:at + EARLY.get(n, 0)]

        def every_batch(eng, body):
            body(0)
            with eng.Fori(1, B - 1) as b:
                body(b)
            body(B - 1)

        assert len(BODY) % 2 == len(LAST) % 2 == 0
        block = stack.enter_context(nc.Block())

        @block.sync
        def _(sp):
            def load_mlp(a, c):
                sp.dma_start(WA[:], a).then_inc(ld_mlp, 16)
                sp.dma_start(WB[:], c).then_inc(ld_mlp, 16)

            sp.dma_start(zP[:], z_in[0]).then_inc(ld_proj, 16)
            sp.dma_start(uP[:], ctx_in[0]).then_inc(ld_proj, 16)
            for i in range(6):
                sp.dma_start(W0[:, i], w0[i]).then_inc(ld_w0[i], 16)
                if i == 0:
                    sp.dma_start(cols[:], cols_in).then_inc(ld_cols, 16)
                if i == 2:
                    sp.dma_start(ident[:], ident_in).then_inc(ld_par, 16)
                    sp.dma_start(hmask[:], hmask_in).then_inc(ld_par, 16)
                    sp.dma_start(sel32, sel_in).then_inc(ld_par, 16)
            sp.dma_start(WO[:], wo).then_inc(ld_wo, 16)
            sp.dma_start(rows[:], rows_in.to_broadcast([P, NROWS])).then_inc(ld_rows, 16)
            for dst, src in ((W1QK, w1qk), (W1V, w1v), (W1O, w1o)):
                sp.dma_start(dst[:], src).then_inc(ld_w1, 16)
            load_mlp(w1a, w1b)
            for dst, src in ((W2QKV, w2qkv), (W2O, w2o)):
                sp.dma_start(dst[:], src).then_inc(ld_w2, 16)
            sp.dma_start(W3[:], w3).then_inc(ld_w3, 16)

            def store_batch(b):
                sp.wait_ge(s_o3, b + 1)
                sp.dma_start(out[b], C3[:, 3, :]).then_inc(st_out, 16)

            def body(b):
                wait(sp, s_V3, b)
                sp.dma_start(hT[:, :, 0:P], ctxT_in[b]).then_inc(ld_ctx, 16)
                sp.dma_start(uC[:], ctx_in[b]).then_inc(ld_ctx, 16)
                wait(sp, s_x0, b)
                sp.dma_start(zR[:], z_in[b]).then_inc(ld_res, 16)
                wait(sp, s_msk, N_MSK * b)
                sp.dma_start(m1row[0:1, :], mask1[b]).then_inc(ld_msk, 16)
                sp.dma_start(m1col[:], mask1[b].rearrange("o p -> p o")).then_inc(ld_msk, 16)
                sp.dma_start(m2row[0:1, :], mask2[b]).then_inc(ld_msk, 16)
                sp.dma_start(m2col[:], mask2[b].rearrange("o p -> p o")).then_inc(ld_msk, 16)
                sp.dma_start(m3row[:], mask3[b].to_broadcast([P, D])).then_inc(ld_msk, 16)
                for c in range(2):
                    sp.dma_start(m3col[:, c:c + 1], mask3[b][:, c * P:c * P + P].rearrange("o p -> p o"))\
                        .then_inc(ld_msk, 16)
                if not is_last(b):
                    for s in (s_Q0, s_K0, s_V0):
                        sp.wait_ge(s, 4 * b + 4)
                    sp.dma_start(zP[:], z_in[b + 1]).then_inc(ld_proj, 16)
                    sp.dma_start(uP[:], ctx_in[b + 1]).then_inc(ld_proj, 16)
                if not is_first(b):
                    store_batch(b - 1)
                sp.wait_ge(s_x1, b + 1)
                load_mlp(w2a, w2b)
                if not is_last(b):
                    sp.wait_ge(s_x3, b + 1)
                    load_mlp(w1a, w1b)
                sp.wait_ge(s_U3, 2 * b + 2)
                sp.dma_start(scratch, U3[:]).then_inc(st_u3, 16)
                sp.wait_ge(st_u3, 16 * b + 16)
                for q in range(3):
                    for g in range(NG):
                        src = scratch.rearrange("(s r) g i -> g s r i", r=32)[g][:, 8 * q:8 * q + 8, :]
                        sp.dma_start(C3[32 * g:32 * g + 32, q, :], src).then_inc(ld_c3, 16)

            every_batch(sp, body)
            store_batch(B - 1)
            sp.wait_ge(st_out, 16 * B)

        @block.tensor
        def _(pe):
            def project(name, o, k):
                bank, n = o.at(name)
                i = int(name[-1])
                if name in ("qp0", "kp0"):
                    pe.wait_ge(ld_proj, 32 * k + 32)
                if n >= 1 if isinstance(n, int) else True:
                    pe.wait_ge(*o.bank_taken(name))
                if name[0] in "qk":
                    for c in range(2):
                        piece, at = divmod((2 * i + c + (8 if name[0] == "k" else 0)) * P, 512)
                        pe.wait_ge(ld_w0[piece], 16)
                        for s in range(2):
                            dst = GP[bank][:, c * D + s * P:c * D + s * P + P]
                            pe.matmul(dst, W0[:, piece, 2 * s, at:at + P], zP[:, s * P:s * P + P],
                                      start=True, stop=False)
                            mm = pe.matmul(dst, W0[:, piece, 2 * s + 1, at:at + P], uP[:, s * P:s * P + P],
                                           start=False, stop=True)
                else:
                    s, w = divmod(i, 2)
                    pe.wait_ge(ld_w0[4 + w], 16)
                    pe.matmul(GP[bank][:], zP[:, s * P:s * P + P], W0[:, 4 + w, 2 * s, :], start=True, stop=False)
                    mm = pe.matmul(GP[bank][:], uP[:, s * P:s * P + P], W0[:, 4 + w, 2 * s + 1, :],
                                   start=False, stop=True)
                mm.then_inc(gp_full[bank], 1)

            def maxima_pass(b, L, Kb, mrow, ready):
                steps = STEPS[L]
                halves = 2 if L in (0, 3) else 1

                def ready_group(g):
                    pe.wait_ge(s_Qb, 16 * b + 4 * L + g + 1)
                    if g == 0:
                        for s, v in ready:
                            pe.wait_ge(s, v)
                    if L == 0:
                        pe.wait_ge(s_K0, 4 * b + g + 1)

                def maxima(g, u):
                    n = MX_UNITS.index((L, g, u))
                    dst = MX[n % 2]
                    wait(pe, *mx_bank_taken(b, n))
                    if mrow is not None:
                        keys = mrow.shape[1]
                        pe.matmul(dst[:].rearrange("p (a k) -> p a k", k=keys), sel[:, HG, :],
                                  mrow.unsqueeze(1).to_broadcast([P, 512 // keys, keys]), start=True, stop=False,
                                  skip_group_check=True)
                    if L in (0, 3):
                        parts = [(HG * g + u, s) for s in range(2)]
                    else:
                        per = HG // steps
                        parts = [(HG * g + per * u + j, 0) for j in range(per)]
                    w = 512 // len(parts)
                    for j, (h, s) in enumerate(parts):
                        mm = pe.matmul(dst[:, j * w:j * w + w], Qb[:, g % 2, h % HG, s * P:s * P + P], Kb(h),
                                       start=mrow is None, stop=True, skip_group_check=True)
                    mm.then_inc(mx_full[n % 2], 1)

                def shift_rows(g):
                    n = MX_UNITS.index((L, g, "T"))
                    rows_out = MX[n % 2][:].bitcast(BF16)
                    wait(pe, *mx_bank_taken(b, n))
                    pe.wait_ge(nm_ready, shifts(b, L, g))
                    if L == 2:
                        mm = pe.transpose(rows_out[0:16, 0:P], nm[:, g // 2].rearrange("p s k -> p (s k)"), identb[:])
                    else:
                        for s in range(halves):
                            mm = pe.transpose(rows_out[0:8, s * P:s * P + P], nm[:, g % 2, s, :], identb[:])
                    mm.then_inc(mx_full[n % 2], 1)

                def make(g, u):
                    if u == "T":
                        shift_rows(g)
                    else:
                        if u == 0:
                            ready_group(g)
                        maxima(g, u)
                return make

            def attention(b, o, L, make, K, Qf, V, v_ready, between=None, beside=None, amid=None):
                steps = STEPS[L]

                def scores(g, u):
                    n = SC_BASE[L] + g * steps + u
                    heads, kc, w = unit_heads(L, g, u)
                    wait(pe, p_ready, SC_N * b + n - 1)
                    if u == 0:
                        pe.wait_ge(nmT_ready, shifts(b, L, g))
                    for j, h in enumerate(heads):
                        dst = SC[n % 2][:, j * w:j * w + w]
                        which, shift = (sel2[:, h % 8, :], g // 2) if L == 2 else (sel[:, h % HG, :], g % 2)
                        pe.matmul(dst, which, nmT[:, shift, 0:w], start=(j == 0), stop=False, skip_group_check=True)
                    pe.matmul(SC[n % 2][:].rearrange("p (h l) -> p h l", l=w), K(heads[0])[:, kc * P:kc * P + P],
                              Qf(heads[0], len(heads)), start=False, stop=True, skip_group_check=True)\
                        .then_inc(sc_full, 1)

                def pv(g, u):
                    n = SC_BASE[L] + g * steps + u
                    heads, kc, w = unit_heads(L, g, u)
                    m = PV_BASE[L] + {0: 2 * g + u // 2, 3: g // 2}.get(L, g)
                    pe.wait_ge(p_ready, SC_N * b + n + 1)
                    if (kc == 0 if L == 0 else u == 0 and (L < 3 or g % 2 == 0)):
                        wait(pe, *pv_bank_taken(b, m))
                    at = w * (g % 2) if L == 3 else 0
                    for j, h in enumerate(heads):
                        if L == 0:
                            dst, v = PV[m % 2][64 * j:64 * j + 64, 0:D], V[:, kc, h * 64:h * 64 + 64]
                        else:
                            s = 32 * (h % HG)
                            dst, v = PV[m % 2][s:s + 32, at:at + w], V(h, kc)
                        mm = pe.matmul(dst, v, Pr[:, n % 4, j * w:j * w + w], start=(kc == 0),
                                       stop=(kc == 1 or L == 2), skip_group_check=True)
                    mm.then_inc(pv_done, 1)

                def denominator(c):
                    pe.wait_ge(ps_ready, 8 * b + c + 1)
                    for j in range(2):
                        mm = pe.matmul(PV[c % 2][64 * j:64 * j + 64, D:2 * D], ones[:],
                                       Psum[:, c % 2, j * D:j * D + D], start=True, stop=True,
                                       skip_group_check=True)
                    mm.then_inc(den_done, 1)

                def out_chunk(c):
                    bank, n = o.at("wo")
                    if c == 0:
                        pe.wait_ge(*o.bank_taken("wo"))
                        pe.wait_ge(ld_wo, 16)
                    pe.wait_ge(s_A0, 8 * b + c + 1)
                    mm = pe.matmul(GP[bank][:, 0:D], WO[:, c, :], A0[:, c, :], start=(c == 0), stop=(c == 7),
                                   skip_group_check=True)
                    if c == 7:
                        mm.then_inc(gp_full[bank], 1)

                if L != 0:
                    for g, u in order_of_maxima(L)[-1]:
                        if (g, u) == (0, "T") and amid:
                            amid()
                        make(g, u)
                units = [(g, u) for g in range(NG) for u in range(steps)]
                for n, (g, u) in enumerate(units):
                    for unit in order_of_maxima(L)[n]:
                        make(*unit)
                    scores(g, u)
                    if n == 2:
                        pe.wait_ge(*v_ready)
                    if n >= 2:
                        pv(*units[n - 2])
                    if beside:
                        beside(n)
                    if L == 0 and n % 2 and n >= 3:
                        denominator((n - 3) // 2)
                    if L == 0 and n % 2 and n >= 7:
                        out_chunk((n - 7) // 2)
                pv(*units[-2])
                pv(*units[-1])
                if L == 0:
                    denominator(7)
                    for c in range(5, 8):
                        if c == 7:
                            between()
                        out_chunk(c)

            def maxima0(b):
                return maxima_pass(b, 0, lambda h: K0b[:, h // HG % 2, h // 2 % 2, :], None, [])

            def body(b):
                o = order_of(b)

                def fill(*names):
                    if not is_last(b):
                        for name in names:
                            project(name, o, b + 1)

                def begin(name, *ready):
                    bank, n = o.at(name)
                    pe.wait_ge(*o.bank_taken(name))
                    for s, v in ready:
                        pe.wait_ge(s, v)
                    return GP[bank], gp_full[bank]

                def transpose_pair(name, src, ready):
                    g, full = begin(name, ready)
                    for c in range(2):
                        mm = pe.transpose(g[:, c * P:c * P + P], src[:, c * P:c * P + P], ident[:])
                    mm.then_inc(full, 1)

                def heads_T(name, W, rhs, width, *ready):
                    g, full = begin(name, *ready)
                    for m in range(2):
                        for c in range(2):
                            mm = pe.matmul(g[:, m * width:m * width + width], W[:, c, m * P:m * P + P], rhs(c),
                                           start=(c == 0), stop=(c == 1), skip_group_check=True)
                    mm.then_inc(full, 1)

                def slots_out(name, W, which):
                    g, full = begin(name)
                    for s in range(NG):
                        pe.wait_ge(s_Ax, 8 * b + 4 * which + s + 1)
                        mm = pe.matmul(g[:, 0:D], Ax[:, s, :], W[:, s, :], start=(s == 0), stop=(s == NG - 1))
                    mm.then_inc(full, 1)

                def mlp_in(name, *ready):
                    g, full = begin(name, *ready)
                    for j in range(4):
                        f = 4 * int(name[1]) + j
                        for c in range(2):
                            mm = pe.matmul(g[:, j * P:j * P + P], WA[:, c, f * P:f * P + P], oT[:, c, :],
                                           start=(c == 0), stop=(c == 1), skip_group_check=True)
                    mm.then_inc(full, 1)

                def mlp_out(name, which):
                    g, full = begin(name)
                    for f in range(8):
                        if f % 4 == 0:
                            pe.wait_ge(s_G, 4 * b + 2 * which + f // 4 + 1)
                        mm = pe.matmul(g[:, 0:D], G[:, f * P:f * P + P], WB[:, f, :], start=(f == 0), stop=(f == 7))
                    mm.then_inc(full, 1)

                attention(b, o, 0, maxima0(b), lambda h: K0[:, h // 2, :], lambda h, n: Q0[:, h:h + n, :], V0, (s_V0, 4 * b + 4),
                          lambda: fill("kp0"))
                wait(pe, *pv_bank_taken(b, 8))
                pe.wait_ge(s_x0, b + 1)
                for c in range(2):
                    mm = pe.transpose(PV[0][:, c * P:c * P + P], x0[:, c * P:c * P + P], ident[:])
                mm.then_inc(s_x0T, 1)
                fill("kp1", "kp2")
                heads_T("q1", W1QK[:, 0], lambda c: hT[:, c, P:D], P, (s_hT, b + 1), (ld_w1, 48))
                heads_T("k1", W1QK[:, 1], lambda c: hT[:, c, :], D, (ld_ctx, 32 * b + 32))

                def v1(name, kc):
                    g, full = begin(name)
                    for c in range(2):
                        mm = pe.matmul(g[:, 0:D], hT[:, c, kc * P:kc * P + P], W1V[:, c, :],
                                       start=(c == 0), stop=(c == 1))
                    mm.then_inc(full, 1)
                v1("v1", 1)

                def amid1():
                    wait(pe, *pv_bank_taken(b, 9))
                    for c in range(2):
                        mm = pe.transpose(PV[1][:, c * P:c * P + P], hT[:, c, P:D], ident[:])
                    mm.then_inc(s_latT, 1)
                    v1("v1c", 0)
                    fill("qp0")

                make = maxima_pass(b, 1, lambda h: K1b[:, h // 8, :], b1row[:],
                                   [(s_K1b, b + 1), (s_msk, N_MSK * b + N_MSK - 1)])
                attention(b, o, 1, make, lambda h: K1[:, h // 8, :], lambda h, n: Q12[:, h:h + n, :],
                          lambda h, kc: V1[:, kc, h, :], (s_V1, 2 * b + 2), amid=amid1)
                slots_out("o1", W1O, 0)
                fill("qp1")
                transpose_pair("oT", xb, (s_xb, 3 * b + 1))
                fill("vp0")
                mlp_in("m0", (s_oT, 3 * b + 1), (ld_mlp, 64 * b + 32))
                mlp_in("m1")
                heads_T("k2", W2QKV[:, 1], lambda c: hT[:, c, 0:P], P, (ld_w2, 32))
                fill("vp1")
                mlp_out("w2", 0)
                fill("qp2")
                g, full = begin("v2")
                for c in range(2):
                    mm = pe.matmul(g[:, 0:D], hT[:, c, 0:P], W2QKV[:, 2, c, :], start=(c == 0), stop=(c == 1))
                mm.then_inc(full, 1)
                transpose_pair("yT", xb, (s_xb, 3 * b + 2))
                fill("vp2")
                heads_T("q2", W2QKV[:, 0], lambda c: oT[:, c, :], P, (s_oT, 3 * b + 2))
                fill("kp3")
                make = maxima_pass(b, 2, lambda h: K2b[:, h // 8, :], b2row[:], [(s_K2b, b + 1)])
                attention(b, o, 2, make, lambda h: K2[:, h // 8, :], lambda h, n: Q12[:, h:h + n, :],
                          lambda h, kc: V2[:, h, :], (s_V2, b + 1))
                slots_out("o2", W2O, 1)
                g, full = begin("k3", (ld_w3, 16))
                pe.matmul(g[:, 0:D], W3[:, 1, :], uC[:], start=True, stop=True).then_inc(full, 1)
                transpose_pair("yT2", xb, (s_xb, 3 * b + 3))
                g, full = begin("v3")
                for kc in range(2):
                    mm = pe.matmul(g[:, kc * P:kc * P + P], uC[:, kc * P:kc * P + P], W3[:, 2, :],
                                   start=True, stop=True, skip_group_check=True)
                mm.then_inc(full, 1)
                mlp_in("n0", (s_oT, 3 * b + 3), (ld_mlp, 64 * b + 64))
                mlp_in("n1")
                fill("vp3")
                mlp_out("w4", 1)
                g, full = begin("q3", (s_x3, b + 1))
                pe.matmul(g[:, 0:D], W3[:, 0, :], x3[:], start=True, stop=True).then_inc(full, 1)
                make = maxima_pass(b, 3, lambda h: K3b[:], b3row[:], [(s_K3b, b + 1)])
                make0 = None if is_last(b) else maxima0(b + 1)

                def beside(n):
                    if make0:
                        for unit in early_maxima(n):
                            make0(*unit)
                attention(b, o, 3, make, lambda h: K3[:], lambda h, n: Q3[:, h % 12:h % 12 + n, :], lambda h, kc: V3[:, kc, h, :],
                          (s_V3, b + 1), beside=beside, amid=lambda: fill("qp3"))

            for name in PROJ:
                project(name, prologue, 0)
            pe.wait_ge(const_v, 2)
            pe.wait_ge(const_p, 1)
            pe.wait_ge(ld_par, 48)
            for unit in early_maxima(None):
                maxima0(0)(*unit)
            every_batch(pe, body)

        @block.scalar
        def _(act):
            def take(o, name):
                bank, n = o.at(name)
                act.wait_ge(gp_full[bank], n + 1)
                return GP[bank]

            def project(name, o):
                g = take(o, name)
                i = int(name[-1])
                if name[0] == "k":
                    act.activation(K0[:, 2 * i:2 * i + 2, :].rearrange("p c l -> p (c l)"), g[:], ACT.Copy)\
                        .then_inc(s_K0, 1)
                else:
                    s, w = divmod(i, 2)
                    act.activation(V0[:, s, w * 512:w * 512 + 512], g[:], ACT.Copy).then_inc(s_V0, 1)

            def shift_rows(b, L, g):
                n = MX_UNITS.index((L, g, "T"))
                w = D if L in (0, 3) else P
                act.wait_ge(mx_full[n % 2], b * (MX_N // 2) + n // 2 + 1)
                rows, ring = (16, g // 2) if L == 2 else (8, g % 2)
                act.activation(nmT[0:rows, ring, 0:w], MX[n % 2][:].bitcast(BF16)[0:rows, 0:w], ACT.Copy)\
                    .then_inc(nmT_ready, 1)

            def cast(b, L, g):
                j = 4 * L + g - 2
                k, j = (b - 1, j + 16) if j < 0 else (b, j)
                wait(act, mx_done, SC_N * k + SC_BASE[j // 4] + (j % 4 + 1) * STEPS[j // 4])
                dst = Qb[:, g % 2]
                if L == 0:
                    act.wait_ge(s_K0, 4 * b + g + 1)
                    act.activation(K0b[:, g % 2], K0[:, 2 * g:2 * g + 2, :], ACT.Copy)
                    act.wait_ge(s_Q0, 4 * b + g + 1)
                    src = Q0[:, HG * g:HG * g + HG, :]
                elif L == 3:
                    act.wait_ge(s_Qx, 12 * b + 9 + g)
                    src = Q3[:, HG * (g % 3):HG * (g % 3) + HG, :]
                else:
                    act.wait_ge(s_Qx, 12 * b + 4 * (L - 1) + g + 1)
                    dst, src = Qb[:, g % 2, :, 0:P], Q12[:, HG * g:HG * g + HG, :]
                act.activation(dst, src, ACT.Copy).then_inc(s_Qb, 1)

            def early(b):
                return [lambda: cast(b, 0, 0), lambda: cast(b, 0, 1), lambda: shift_rows(b, 0, 0)]

            def attention(b, L, scale, after=None, amid=None, filling=None):
                steps = STEPS[L]

                def exp(n):
                    kc = unit_heads(L, *divmod(n, steps))[1]
                    n += SC_BASE[L]
                    act.wait_ge(sc_full, SC_N * b + n + 1)
                    wait(act, pv_done, SC_N * b + n - 3)
                    if 4 <= n < 20:
                        act.wait_ge(ps_ready, 8 * b + (n - 4) // 2 + 1)
                    bias = {0: 0.0, 1: bcol[:, kc:kc + 1], 2: bcol[:, 2:3], 3: bcol[:, 3 + kc:4 + kc]}[L]
                    act.activation(Pr[:, n % 4, :], SC[n % 2][:], ACT.Exp, bias=bias, scale=scale)\
                        .then_inc(p_ready, 1)

                if L != 0:
                    if L != 3:
                        cast(b, L, 0)
                    if amid:
                        amid()
                    cast(b, L, 1)
                    if L == 2:
                        cast(b, L, 2)
                        cast(b, L, 3)
                    shift_rows(b, L, 0)
                    if L == 1:
                        cast(b, L, 2)
                    if filling:
                        filling()
                for n in range(NG * steps):
                    for g, u in order_of_maxima(L)[n]:
                        if u == "T":
                            shift_rows(b, L, g)
                    exp(n)
                    g, u = divmod(n + steps + 3, steps)
                    if L != 2 and u == 0 and 2 <= g < NG:
                        cast(b, L, g)
                    if after:
                        after(n)

            def std3(b):
                act.wait_ge(s_v, b + 1)
                wait(act, st_out, 16 * b)
                act.activation(C3[:, 3, :], C3[:, 1, :], ACT.Sqrt).then_inc(s_std, 1)

            def mlp(b, which, between, after=lambda: None):
                for i in range(2):
                    h = slice(512 * i, 512 * i + 512)
                    act.wait_ge(s_X, 4 * b + 2 * which + i + 1)
                    act.activation(T[:, h], X[:, h], ACT.Square, scale=GELU_A ** 0.5).then_inc(s_sq, 1)
                between()
                for i in range(2):
                    h = slice(512 * i, 512 * i + 512)
                    act.wait_ge(s_T, 4 * b + 2 * which + i + 1)
                    act.activation(T[:, h], T[:, h], ACT.Tanh, scale=GELU_C).then_inc(s_th, 1)
                after()

            def body(b):
                o = order_of(b)

                def fill(*names):
                    if not is_last(b):
                        for name in names:
                            project(name, o)

                def turned(name, weight, bias=None):
                    g = take(o, name)
                    for c in range(2):
                        ins = act.activation(oT[:, c, :], g[:, c * P:c * P + P], ACT.Identity, scale=col(weight, c),
                                             bias=col(bias, c) if bias else 0.0)
                    ins.then_inc(s_oT, 1)

                def keys(name, K, bias, width, s):
                    g = take(o, name)
                    for m in range(len(bias)):
                        ins = act.activation(K[:, m, :], g[:, m * width:m * width + width], ACT.Identity,
                                             bias=bias[m])
                    ins.then_inc(s, 1)

                def keys_bf16(K, Kb, s, sb):
                    act.wait_ge(s, b + 1)
                    act.activation(Kb, K, ACT.Copy).then_inc(sb, 1)

                attention(b, 0, 0.125)
                if not is_first(b):
                    std3(b - 1)
                fill("kp0", "kp1", "kp2")

                def latents():
                    act.wait_ge(s_latT, b + 1)
                    act.activation(lat, PV[1][:, 0:D], ACT.Copy).then_inc(s_lat, 1)

                def keys1():
                    keys("k1", K1[:], [col("kb1", 0), col("kb1", 1)], D, s_K1)
                    keys_bf16(K1[:], K1b[:], s_K1, s_K1b)
                attention(b, 1, 1.0 / 16, amid=keys1, filling=latents)
                act.wait_ge(s_xa, 2 * b + 1)
                act.activation(junk, xa[:], ACT.Square, accum_out=stat[:, 0:1]).then_inc(s_ssq, 1)
                turned("oT", "pw")
                fill("vp0")
                mlp(b, 0, lambda: keys("k2", K2[:], [col("kb2", 0), col("kb2", 1)], P, s_K2),
                    lambda: keys_bf16(K2[:], K2b[:], s_K2, s_K2b))
                fill("vp1")
                turned("yT", "ln1w", "ln1b")
                fill("vp2")
                attention(b, 2, 0.25, filling=lambda: fill("kp3"))
                keys("k3", K3[:].unsqueeze(1), [col("bk")], D, s_K3)
                turned("yT2", "ln2w", "ln2b")

                def squares():
                    act.wait_ge(s_v3, b + 1)
                    act.activation(V3[:, :, :, 8:16], V3[:, :, :, 0:8], ACT.Square).then_inc(s_V3, 1)
                mlp(b, 1, lambda: None, lambda: (squares(), keys_bf16(K3[:], K3b[:], s_K3, s_K3b)))
                fill("vp3")
                def sums(i):
                    act.wait_ge(pv_done, SC_N * b + SC_BASE[3] + 8 * i + 8)
                    wait(act, st_u3, 16 * b)
                    act.activation(U3[:, 2 * i:2 * i + 2, :].rearrange("p g i -> p (g i)"), PV[(PV_BASE[3] + i) % 2][:],
                                   ACT.Copy).then_inc(s_U3, 1)

                def after(n):
                    if n == 10:
                        sums(0)
                    if n in (8, 12, 14) and not is_last(b):
                        early(b + 1)[(8, 12, 14).index(n)]()
                attention(b, 3, 8.0 ** -0.5, after)
                sums(1)
                act.wait_ge(s_xm, b + 1)
                for i, (src, func) in enumerate(((xm, ACT.Copy), (xm, ACT.Square), (m3, ACT.Copy))):
                    act.activation(junk3, src[:], func, accum_out=stat[:, 4 + i:5 + i]).then_inc(s_nst, 1)
                    act.wait_ge(s_nst, 3 * b + i + 1)

            for name in PROJ[4:]:
                project(name, prologue)
            act.wait_ge(const_v, 2)
            act.wait_ge(const_p, 1)
            act.wait_ge(ld_cols, 16)
            for step in early(0):
                step()
            every_batch(act, body)
            std3(B - 1)

        @block.vector
        def _(dve):
            chain = Chain(dve, v_step, V_STEPS)
            ending = Chain(dve, f_step, F_STEPS)
            apart = Apart(dve, gate[:, 1:2], v_apart, 11)

            def take(o, name):
                bank, n = o.at(name)
                dve.wait_ge(gp_full[bank], n + 1)
                return GP[bank]

            def project(name, o):
                g = take(o, name)
                i = int(name[-1])
                for r in range(2):
                    p = slice(64 * r, 64 * r + 64)
                    bias = colrange("rwb", 2 * i, 2 * i + 2)[p].unsqueeze(2).to_broadcast([64, 2, D])
                    ins = dve.tensor_tensor(Q0[p, 4 * i + r:4 * i + r + 3:2, :],
                                            g[p, :].rearrange("p (c l) -> p c l", c=2), bias, ALU.add)
                ins.then_inc(s_Q0, 1)

            def maxima(b, L, g, u):
                steps = STEPS[L]
                halves = 2 if L in (0, 3) else 1
                if u == "T":
                    return
                n = MX_UNITS.index((L, g, u))
                dve.wait_ge(mx_full[n % 2], b * (MX_N // 2) + n // 2 + 1)
                if halves == 2:
                    dst, a = mx[:, g % 2, :, u], 2
                elif L == 2:
                    dst, a = mx[:, g // 2, g % 2, :], HG
                else:
                    a = HG // steps
                    dst = mx[:, g % 2, 0, a * u:a * u + a]
                dve.tensor_reduce(dst, MX[n % 2][:].rearrange("p (a k) -> p a k", a=a), AX_X, ALU.max,
                                  negate=True).then_inc(mx_done, 1)
                if u == steps - 1 and (L != 2 or g % 2):
                    if L == 2:
                        m, at = (t[:, g // 2].rearrange("p s k -> p (s k)") for t in (mx, nm))
                        hi, lo = at[:, 0:8], at[:, 8:16]
                    else:
                        m, hi, lo = mx[:, g % 2, 0:halves], nm[:, g % 2, 0:halves, 0:4], nm[:, g % 2, 0:halves, 4:8]
                    dve.wait_ge(mx_done, SC_N * b + SC_BASE[L] + (g + 1) * steps)
                    dve.tensor_copy(hi, m).then_inc(s_hi, 1)
                    dve.wait_ge(s_hi, shifts(b, L, g))
                    dve.tensor_tensor(lo, m, hi, ALU.subtract).then_inc(nm_ready, 1)

            def attention(b, L, after_step=None, amid=lambda: None):
                if L != 0:
                    for g, u in order_of_maxima(L)[-1]:
                        if (g, u) == (0, "T"):
                            amid()
                        maxima(b, L, g, u)
                for n in range(NG * STEPS[L]):
                    for unit in order_of_maxima(L)[n]:
                        maxima(b, L, *unit)
                    if after_step:
                        after_step(n)

            def quotient0(b, c):
                dve.wait_ge(den_done, 8 * b + c + 1)
                wait(dve, s_Ax, 8 * b) if c == 0 else dve.wait_ge(s_A0, 8 * b + c)
                chain.step(dve.reciprocal(rec, PV[c % 2][:, D:2 * D]))
                dve.tensor_tensor(A0[:, c, :], PV[c % 2][:, 0:D], rec, ALU.mult).then_inc(s_A0, 1)

            def quotient(b, L, g):
                bank = PV[(PV_BASE[L] + g) % 2][:, 0:P]
                used = NG * (L - 1) + g
                apart.wait((s_Ax, 8 * b + used) if used else (s_A0, 8 * b + 8),
                           (pv_done, SC_N * b + SC_BASE[L] + (g + 1) * STEPS[L]))
                chain.step(dve.stream_shuffle(den, bank, [16 + r % 16 for r in range(32)]))
                chain.step(dve.reciprocal(den, den))
                dve.tensor_tensor(Ax[:, g, :], bank, den, ALU.mult).then_inc(s_Ax, 1)

            def blocks12(o, name, bias):
                g = take(o, name)
                for i in range(NG):
                    dve.scalar_tensor_tensor(
                        out=Q12[:, HG * i:HG * i + HG, :],
                        in0=g[:, i // 2 * P:i // 2 * P + P].unsqueeze(1).to_broadcast([P, HG, P]),
                        scalar=col(bias, i // 2),
                        in1=hmask[:, HG * (i % 2):HG * (i % 2) + HG].unsqueeze(2).to_broadcast([P, HG, P]),
                        op0=ALU.add, op1=ALU.mult).then_inc(s_Qx, 1)

            def block3(b, o, i):
                g = take(o, "q3")
                at = HG * (i % 3)
                if i == 3:
                    dve.wait_ge(sc_full, SC_N * b + SC_BASE[3] + 4)
                k = HG * i + 8
                blocks = [(Q3[:, at:at + HG, :], s_Qx)]
                if i == 0:
                    dve.wait_ge(mx_done, SC_N * b + SC_BASE[2] + 3 * STEPS[2])
                    blocks.insert(0, (Qb[:, 0], s_Qb))
                for dst, s in blocks:
                    dve.scalar_tensor_tensor(
                        out=dst, in0=g[:, 0:D].unsqueeze(1).to_broadcast([P, HG, D]), scalar=col("bq"),
                        in1=hmask[:, k:k + HG].unsqueeze(2).to_broadcast([P, HG, D]),
                        op0=ALU.add, op1=ALU.mult).then_inc(s, 1)

            def mlp(b, o, names, bias, which):
                for i, name in enumerate(names):
                    g = take(o, name)
                    h = slice(512 * i, 512 * i + 512)
                    dve.tensor_tensor(X[:, h].rearrange("p (f k) -> p f k", k=P),
                                      g[:].rearrange("p (f k) -> p f k", k=P),
                                      colrange(bias, 4 * i, 4 * i + 4).unsqueeze(2).to_broadcast([P, 4, P]),
                                      ALU.add).then_inc(s_X, 1)
                for i in range(2):
                    h = slice(512 * i, 512 * i + 512)
                    dve.wait_ge(s_sq, 4 * b + 2 * which + i + 1)
                    dve.scalar_tensor_tensor(out=T[:, h], in0=T[:, h], scalar=1.0, in1=X[:, h], op0=ALU.add,
                                             op1=ALU.mult).then_inc(s_T, 1)
                for i in range(2):
                    h = slice(512 * i, 512 * i + 512)
                    dve.wait_ge(s_th, 4 * b + 2 * which + i + 1)
                    dve.scalar_tensor_tensor(out=G[:, h], in0=T[:, h], scalar=1.0, in1=X[:, h], op0=ALU.add,
                                             op1=ALU.mult).then_inc(s_G, 1)

            def layer_norm(b, src, ready, k, meanwhile=lambda: None):
                dve.wait_ge(*ready)
                chain.step(dve.bn_stats(stat[:, 8:14], src[:]), apart)
                chain.step(dve.bn_aggr(stat[:, 14:16], stat[:, 8:14]))
                dve.tensor_scalar(stat[:, 1:2], stat[:, 15:16], 1e-5, None, ALU.add).then_inc(s_var, 1)
                meanwhile()
                dve.wait_ge(s_pow, 3 * b + k)
                dve.tensor_scalar(xb[:], src[:], stat[:, 14:15], stat[:, 2:3], ALU.subtract, ALU.mult)\
                    .then_inc(s_xb, 1)

            def end3(b):
                ending.begin(b)
                dve.wait_ge(ld_c3, 16 * 3 * NG * (b + 1))
                ending.step(dve.reciprocal(C3[:, 2, :], C3[:, 2, :]))
                ending.step(dve.tensor_tensor(C3[:, 0, :], C3[:, 0, :], C3[:, 2, :], ALU.mult))
                ending.step(dve.tensor_tensor(C3[:, 1, :], C3[:, 1, :], C3[:, 2, :], ALU.mult))
                ending.step(dve.tensor_tensor(C3[:, 2, :], C3[:, 0, :], C3[:, 0, :], ALU.mult))
                ending.step(dve.tensor_tensor(C3[:, 1, :], C3[:, 1, :], C3[:, 2, :], ALU.subtract))
                dve.tensor_scalar(C3[:, 1, :], C3[:, 1, :], 0.0, None, ALU.max).then_inc(s_v, 1)

            def output3(b):
                dve.wait_ge(s_std, b + 1)
                dve.wait_ge(s_xn, b + 1)
                ending.step(dve.tensor_tensor(C3[:, 3, :], C3[:, 3, :], xn[:], ALU.mult))
                ending.step(dve.tensor_tensor(C3[:, 3, :], C3[:, 3, :], C3[:, 0, :], ALU.add))
                dve.tensor_tensor(C3[:, 3, :], C3[:, 3, :], m3[:], ALU.mult).then_inc(s_o3, 1)
                ending.end()

            def body(b):
                o = order_of(b)
                chain.begin(b)
                apart.begin(b)

                def fill(*names):
                    if not is_last(b):
                        for name in names:
                            project(name, o)

                def steps0(n):
                    if n == 4:
                        wait(dve, st_u3, 16 * b)
                    if n >= 4 and n % 2 == 0:
                        quotient0(b, (n - 4) // 2)
                    if n == 11 and not is_first(b):
                        end3(b - 1)
                def v1(name, kc):
                    g = take(o, name)
                    dve.tensor_tensor(V1[:, kc, :, 0:16], g[:, 0:D].rearrange("p (h d) -> p h d", d=16),
                                      row("vb1").rearrange("p (h d) -> p h d", d=16), ALU.add).then_inc(s_V1, 1)

                attention(b, 0, steps0)
                for c in (6, 7):
                    quotient0(b, c)
                dve.wait_ge(ld_res, 16 * b + 16)
                g = take(o, "wo")
                dve.scalar_tensor_tensor(out=x0, in0=g[:, 0:D], scalar=col("bo"), in1=zR[:], op0=ALU.add,
                                         op1=ALU.add).then_inc(s_x0, 1)
                dve.wait_ge(s_x0T, b + 1)
                g = PV[0]
                for c in range(2):
                    ins = dve.bn_stats(stat0[:, 6 * c:6 * c + 6], g[:, c * P:c * P + P])
                chain.step(ins, apart)
                for c in range(2):
                    ins = dve.bn_aggr(stat0[:, 12 + 2 * c:14 + 2 * c], stat0[:, 6 * c:6 * c + 6])
                chain.step(ins)
                dve.tensor_scalar(stat0[:, 16:18], stat0[:, 13:16:2], 1e-5, None, ALU.add).then_inc(s_var0, 1)
                dve.wait_ge(s_pow0, b + 1)
                for c in range(2):
                    ins = dve.tensor_scalar(hT[:, c, P:D], g[:, c * P:c * P + P], stat0[:, 12 + 2 * c:13 + 2 * c],
                                            stat0[:, 18 + c:19 + c], ALU.subtract, ALU.mult)
                ins.then_inc(s_hT, 1)
                blocks12(o, "q1", "qb1")
                v1("v1", 1)
                def steps1(n):
                    if n >= 4 and n % 2 == 0:
                        quotient(b, 1, (n - 4) // 2)
                    if n == 5 and not is_first(b):
                        output3(b - 1)
                attention(b, 1, steps1, lambda: (v1("v1c", 0), fill("qp0")))
                quotient(b, 1, 2)
                quotient(b, 1, 3)
                g = take(o, "o1")
                dve.wait_ge(s_res1, 2 * b + 1)
                dve.tensor_tensor(xa[:], g[:, 0:D], res1[:], ALU.add).then_inc(s_xa, 1)
                dve.wait_ge(s_ssq, b + 1)
                dve.tensor_scalar(stat[:, 1:2], stat[:, 0:1], 1.0 / D, 1e-6, ALU.mult, ALU.add).then_inc(s_var, 1)
                fill("qp1")
                dve.wait_ge(s_pow, 3 * b + 1)
                dve.wait_ge(s_xa, 2 * b + 1)
                dve.tensor_scalar(xb[:], xa[:], stat[:, 2:3], None, ALU.mult).then_inc(s_xb, 1)
                mlp(b, o, ("m0", "m1"), "b1", 0)
                g = take(o, "w2")
                dve.wait_ge(s_res2, 2 * b + 1)
                dve.scalar_tensor_tensor(out=x1[:], in0=g[:, 0:D], scalar=0.5, in1=res2[:], op0=ALU.mult,
                                         op1=ALU.add).then_inc(s_x1, 1)
                def meanwhile():
                    fill("qp2")
                    g = take(o, "v2")
                    dve.tensor_tensor(V2[:, :, 0:16], g[:, 0:D].rearrange("p (h d) -> p h d", d=16),
                                      row("vb2").rearrange("p (h d) -> p h d", d=16), ALU.add).then_inc(s_V2, 1)
                layer_norm(b, x1, (s_x1, b + 1), 2, meanwhile)
                blocks12(o, "q2", "qb2")
                attention(b, 2, lambda n: quotient(b, 2, n - 3) if n == 3 else None)
                for g in (1, 2, 3):
                    quotient(b, 2, g)
                g = take(o, "o2")
                dve.wait_ge(s_res1, 2 * b + 2)
                dve.tensor_tensor(xa[:], g[:, 0:D], res1[:], ALU.add).then_inc(s_xa, 1)
                layer_norm(b, xa, (s_xa, 2 * b + 2), 3)
                g = take(o, "v3")
                dve.tensor_tensor(V3[:, :, :, 0:8], g[:, 0:D].rearrange("p (c h d) -> p c h d", c=2, d=8),
                                  row("bv").rearrange("p (h d) -> p h d", d=8).unsqueeze(1)
                                  .to_broadcast([P, 2, NH, 8]), ALU.add).then_inc(s_v3, 1)
                mlp(b, o, ("n0", "n1"), "fcb", 1)
                g = take(o, "w4")
                dve.wait_ge(s_res2, 2 * b + 2)
                dve.scalar_tensor_tensor(out=x3[:], in0=g[:, 0:D], scalar=0.5, in1=res2[:], op0=ALU.mult,
                                         op1=ALU.add).then_inc(s_x3, 1)
                block3(b, o, 0)

                def steps3(n):
                    if n == 0:
                        fill("qp3")
                    if n == 3:
                        block3(b, o, 3)
                    if not is_last(b):
                        for unit in early_maxima(n):
                            maxima(b + 1, 0, *unit)
                attention(b, 3, steps3, lambda: (block3(b, o, 1), block3(b, o, 2)))
                dve.wait_ge(s_nst, 3 * b + 3)
                dve.reciprocal(stat[:, 7:8], stat[:, 6:7]).then_inc(s_ninv, 1)
                chain.end()
                apart.end()

            dve.memset(Q0[:], 0.0)
            dve.memset(nmT[:], 0.0)
            dve.memset(V1[:], 1.0)
            dve.memset(V2[:], 1.0).then_inc(const_v, 1)
            dve.wait_ge(const_v, 1)
            dve.wait_ge(ld_cols, 16)
            for name in PROJ[:4]:
                project(name, prologue)
            dve.wait_ge(ld_par, 48)
            dve.tensor_copy(identb[:], ident[:])
            dve.tensor_copy(sel[:], sel32[:, 0:HG + 1, :])
            dve.tensor_copy(sel2[:], sel32[:, HG + 1:, :]).then_inc(const_v, 1)
            for unit in early_maxima(None):
                maxima(0, 0, *unit)
            dve.wait_ge(ld_rows, 16)
            every_batch(dve, body)
            end3(B - 1)
            output3(B - 1)

        @block.gpsimd
        def _(pool):
            chain = Chain(pool, p_step, P_STEPS)
            apart = Apart(pool, gate[:, 0:1], p_apart, 4)

            def power(b, k):
                pool.wait_ge(s_var, 3 * b + k)
                pool.tensor_tensor(stat[:, 2:3], stat[:, 1:2], half[:], ALU.pow).then_inc(s_pow, 1)

            def body(b):
                chain.begin(b)
                apart.begin(b)
                for c in range(8):
                    if c == 4:
                        apart.wait((ld_msk, 112 * b + 112))
                        for dst, src, value in (
                                (b1row[0:1, 0:P], m1row[0:1, :], NEG), (b2row[0:1, :], m2row[0:1, :], NEG),
                                (b3row[0:1, :], m3row[0:1, :], NEG), (bcol[:, 0:1], m1col[:], NEG / 16),
                                (bcol[:, 2:3], m2col[:], NEG / 4), (bcol[:, 3:5], m3col[:], NEG * 8.0 ** -0.5)):
                            pool.tensor_scalar(dst, src, 0.0, value, ALU.is_equal, ALU.mult).then_inc(s_msk, 1)
                    n = 2 * c
                    pool.wait_ge(p_ready, SC_N * b + n + 2)
                    wait(pool, den_done, 8 * b + c - 1)
                    pool.tensor_tensor(Psum[:, c % 2, :], Pr[:, n % 4, :], Pr[:, (n + 1) % 4, :], ALU.add)\
                        .then_inc(ps_ready, 1)
                pool.wait_ge(s_var0, b + 1)
                pool.tensor_tensor(stat0[:, 18:20], stat0[:, 16:18], half[:].to_broadcast([P, 2]), ALU.pow)\
                    .then_inc(s_pow0, 1)
                pool.wait_ge(s_lat, b + 1)
                pool.tensor_tensor(res1[:], lat, row("ob1"), ALU.add).then_inc(s_res1, 1)
                pool.tensor_tensor(res2[:], lat, row("b2"), ALU.add).then_inc(s_res2, 1)
                apart.wait((s_o3, b))
                pool.tensor_scalar(m3[:], m3row[:], 0.0, None, ALU.add).then_inc(s_msk, 1)
                power(b, 1)
                power(b, 2)
                pool.wait_ge(s_x1, b + 1)
                pool.tensor_tensor(res1[:], x1[:], row("cb"), ALU.add).then_inc(s_res1, 1)
                power(b, 3)
                pool.tensor_tensor(res2[:], xa[:], row("pb"), ALU.add).then_inc(s_res2, 1)
                pool.wait_ge(s_x3, b + 1)
                pool.wait_ge(s_msk, N_MSK * (b + 1))
                pool.tensor_tensor(xm[:], x3[:], m3[:], ALU.mult).then_inc(s_xm, 1)
                pool.wait_ge(s_ninv, b + 1)
                chain.step(pool.tensor_tensor(stat3[:, 0:1], stat[:, 4:5], stat[:, 7:8], ALU.mult))
                chain.step(pool.tensor_tensor(stat3[:, 1:2], stat[:, 5:6], stat[:, 7:8], ALU.mult))
                chain.step(pool.tensor_tensor(stat3[:, 2:3], stat3[:, 0:1], stat3[:, 0:1], ALU.mult))
                chain.step(pool.tensor_tensor(stat3[:, 1:2], stat3[:, 1:2], stat3[:, 2:3], ALU.subtract), apart)
                chain.step(pool.tensor_scalar(stat3[:, 1:2], stat3[:, 1:2], 0.0, 1e-5, ALU.max, ALU.add))
                chain.step(pool.tensor_tensor(stat3[:, 1:2], stat3[:, 1:2], half[:], ALU.pow), apart)
                chain.step(pool.tensor_scalar(xn[:], xm[:], stat3[:, 0:1], stat3[:, 1:2], ALU.subtract, ALU.mult))
                pool.tensor_tensor(xn[:], xn[:], m3[:], ALU.mult).then_inc(s_xn, 1)
                chain.end()
                apart.end()

            pool.memset(b1row[:], 0.0)
            pool.memset(b2row[:], 0.0)
            pool.memset(b3row[:], 0.0)
            pool.memset(bcol[:], 0.0)
            pool.memset(half[:], -0.5)
            pool.memset(ones[:], 1.0).then_inc(const_p, 1)
            pool.wait_ge(const_p, 1)
            pool.wait_ge(ld_rows, 16)
            every_batch(pool, body)


def launch_constants(np):
    ident = np.eye(P, dtype=np.float32)
    p = np.arange(P)
    hmask = np.concatenate([p[:, None] // 16 == np.arange(8)[None], p[:, None] // 8 == np.arange(16)[None]], axis=1)
    sel = np.zeros((P, HG + 9, P), np.float32)
    for h in range(HG):
        sel[h, h] = sel[HG + h, h] = 1.0
    sel[0, HG] = 1.0
    for h in range(8):
        sel[h, HG + 1 + h] = sel[8 + h, HG + 1 + h] = 1.0
    return ident, hmask.astype(np.float32), sel


def kernel(**inputs):
    import numpy as np
    import concourse.bacc as bacc
    from concourse.bass_utils import run_bass_kernel_spmd

    a = {k: np.asarray(v) for k, v in inputs.items()}
    l1 = {k[9:]: v for k, v in a.items() if k.startswith("L1_")}
    l2 = {k[9:]: v for k, v in a.items() if k.startswith("L2_")}

    def chunks(w):
        return w.reshape(-1, P, w.shape[1]).transpose(1, 0, 2)

    def columns(v):
        return v.reshape(-1, P).T

    def slots(w):
        out = np.zeros((NG, HG, 32, w.shape[1]), w.dtype)
        out[:, :, :16] = w.reshape(NG, HG, 16, -1)
        return out.reshape(NG, P, -1).transpose(1, 0, 2)

    w0 = np.stack([a["L0_xattn_" + n].T for n in ("Wqkv0", "Winj0", "Wqkv1", "Winj1")], axis=1)
    w0 = w0.reshape(P, 4, 6, 512).transpose(2, 0, 1, 3)
    kv_w, kv_b = l1["kv_w"].reshape(D, D, 2), l1["kv_b"].reshape(D, 2)
    parts = {"bo": a["L0_xattn_bo"], "rwb": a["L0_xattn_r_w_bias"].reshape(-1), "qb1": l1["q_b"],
             "kb1": kv_b[:, 0], "b1": l1["mlp_b1"], "qb2": l2["q_b"], "kb2": l2["k_b"], "fcb": l2["fc_b"],
             "bq": a["L3_xattn_bq"], "bk": a["L3_xattn_bk"], "pw": l1["postnorm_w"], "ln1w": l2["ln1_w"],
             "ln1b": l2["ln1_b"], "ln2w": l2["ln2_w"], "ln2b": l2["ln2_b"]}
    rows = {"vb1": kv_b[:, 1], "ob1": l1["out_b"], "b2": l1["mlp_b2"],
            "vb2": l2["v_b"], "cb": l2["cproj_b"],
            "pb": l2["proj_b"], "bv": a["L3_xattn_bv"]}
    ident, hmask, sel = launch_constants(np)
    arrays = {
        "z_in": a["x"], "ctxT_in": a["ctx_2048"].transpose(0, 2, 1).reshape(B, 2, P, P).transpose(0, 2, 1, 3),
        "ctx_in": a["ctx_2048"],
        "mask1": a["mask_BxS2_ik0"].reshape(B, 1, P),
        "mask2": a["mask_BxS2_bf1"].view(np.uint8).reshape(B, 1, P),
        "mask3": a["mask_Bx1x2048_bf1"].view(np.uint8).reshape(B, 1, D),
        "w0": w0, "wo": chunks(a["L0_xattn_Wo"].T),
        "w1qk": np.stack([chunks(l1["q_w"]), chunks(kv_w[:, :, 0])], axis=1),
        "w1v": chunks(kv_w[:, :, 1]), "w1o": slots(l1["out_w"]),
        "w1a": chunks(l1["mlp_w1"]), "w1b": chunks(l1["mlp_w2"]),
        "w2qkv": np.stack([chunks(l2[n]) for n in ("q_w", "k_w", "v_w")], axis=1),
        "w2o": slots(l2["cproj_w"]), "w2a": chunks(l2["fc_w"]), "w2b": chunks(l2["proj_w"]),
        "w3": np.stack([a["L3_xattn_" + n].T for n in ("Wq", "Wk", "Wv")], axis=1),
        "cols_in": np.concatenate([columns(parts[n]) for n in COLS], axis=1),
        "rows_in": np.concatenate([rows[n] for n in ROWS]).reshape(1, NROWS),
        "ident_in": ident, "hmask_in": hmask, "sel_in": sel,
    }
    arrays = {k: np.ascontiguousarray(v) for k, v in arrays.items()}
    nc = bacc.Bacc("TRN2", target_bir_lowering=False, num_devices=1)
    args = [nc.dram_tensor(n, v.shape, mybir.dt.from_np(v.dtype), kind="ExternalInput").ap()
            for n, v in arrays.items()]
    out = nc.dram_tensor("out", (B, P, D), F32, kind="ExternalOutput").ap()
    build(nc, *args, out)
    r = run_bass_kernel_spmd(nc, [arrays], core_ids=[0])
    return r.results[0]["out"]
```

```python
from contextlib import ExitStack

import concourse.bass as bass
from concourse import mybir
from concourse.alu_op_type import AluOpType as ALU

F32 = mybir.dt.float32
BF16 = mybir.dt.bfloat16
I32 = mybir.dt.int32
U8 = mybir.dt.uint8
ACT = mybir.ActivationFunctionType
AX_X = mybir.AxisListType.X

P = 128
B = 8
D = 256
NH = 16
HG = 4
NG = NH // HG
NEG = -(2.0 ** 100)
GELU_C = 0.7978845608028654
GELU_A = 0.044715

COLS = {}
for _name, _n in (("bo", 1), ("rwb", 8), ("qb1", 2), ("kb1", 2), ("b1", 8), ("qb2", 2), ("kb2", 2),
                  ("fcb", 8), ("bq", 1), ("bk", 1), ("pw", 2), ("ln1w", 2), ("ln1b", 2), ("ln2w", 2), ("ln2b", 2)):
    COLS[_name] = (sum(n for _, n in COLS.values()), _n)
NCOLS = sum(n for _, n in COLS.values())
ROWS = {}
for _name, _n in (("vb1", D), ("ob1", D), ("b2", D), ("vb2", D),
                  ("cb", D), ("pb", D), ("bv", P)):
    ROWS[_name] = (sum(n for _, n in ROWS.values()), _n)
NROWS = sum(n for _, n in ROWS.values())

STEPS = {0: 4, 1: 2, 2: 1, 3: 4}
SC_BASE = {0: 0, 1: 16, 2: 24, 3: 28}
SC_N = 44
LAG = {0: 2, 1: 1, 2: 1, 3: 1}
PV_BASE = {0: 0, 1: 10, 2: 14, 3: 18}
PV_N = 20
MX_UNITS = [(L, g, u) for L in (0, 1) for g in range(NG) for u in [*range(STEPS[L]), "T"]]
MX_UNITS += [(2, 0, 0), (2, 1, 0), (2, 0, "T"), (2, 2, 0), (2, 3, 0), (2, 2, "T")]
MX_UNITS += [(3, g, u) for g in range(NG) for u in [*range(STEPS[3]), "T"]]
MX_N = len(MX_UNITS)
SHIFTS = [(L, g) for L, g, u in MX_UNITS if u == "T"]
SHIFT_N = len(SHIFTS)

N_MSK = 7
V_STEPS = 8 + 2 + 8 * 2 + 4
P_STEPS = 7
F_STEPS = 7

PROJ = [f"qp{i}" for i in range(4)] + [f"kp{i}" for i in range(4)] + [f"vp{i}" for i in range(4)]
BODY = ["wo", "kp0", "kp1", "kp2", "q1", "k1", "v1", "v1c", "qp0", "o1", "vp0", "oT", "vp1", "m0", "m1", "k2",
        "qp1", "w2", "kp3", "v2", "yT", "vp2", "q2", "qp2", "o2", "k3", "yT2", "v3", "n0", "n1", "vp3", "w4",
        "q3", "qp3"]
LAST = [u for u in BODY if u not in PROJ]


TAKEN = {"wo": ("x0", 1, 1), "q1": ("qs", 3, 1), "k1": ("K1", 1, 1), "v1": ("V1", 2, 1), "v1c": ("V1", 2, 2),
         "o1": ("xa", 2, 1), "oT": ("oT", 3, 1),
         "m0": ("X", 4, 1), "m1": ("X", 4, 2), "k2": ("K2", 1, 1), "w2": ("x1", 1, 1), "yT": ("oT", 3, 2),
         "q2": ("qs", 3, 2), "v2": ("V2", 1, 1), "o2": ("xa", 2, 2), "k3": ("K3", 1, 1),
         "yT2": ("oT", 3, 3), "n0": ("X", 4, 3), "n1": ("X", 4, 4), "v3": ("v3", 1, 1), "w4": ("x3", 1, 1),
         "q3": ("qs", 3, 3)}
TAKEN.update({u: ({"q": "Q0", "k": "K0", "v": "V0"}[u[0]], 4, int(u[-1]) + 1) for u in PROJ})


def build(nc, z_in, ctxT_in, ctx_in, mask1, mask2, mask3, w0, wo, w1qk, w1v, w1o, w1a, w1b,
          w2qkv, w2o, w2a, w2b, w3, cols_in, rows_in, ident_in, hmask_in, sel_in, out):
    with ExitStack() as stack:
        def sb(name, shape, dt=F32):
            return stack.enter_context(nc.sbuf_tensor(name, shape, dt))

        def ps(name):
            return stack.enter_context(nc.psum_tensor(name, [P, 512], F32))

        def sem(name):
            return stack.enter_context(nc.semaphore(name))

        MX = [ps(f"MX{i}") for i in range(2)]
        SC = [ps(f"SC{i}") for i in range(2)]
        PV = [ps(f"PV{i}") for i in range(2)]
        GP = [ps(f"GP{i}") for i in range(2)]

        W0 = sb("W0", [P, 6, 4, 512])
        WO = sb("WO", [P, 8, P])
        W1QK = sb("W1QK", [P, 2, 2, D])
        W1V = sb("W1V", [P, 2, D])
        W1O = sb("W1O", [P, NG, D])
        W2QKV = sb("W2QKV", [P, 3, 2, D])
        W2O = sb("W2O", [P, NG, D])
        WA = sb("WA", [P, 2, 1024])
        WB = sb("WB", [P, 8, D])
        W3 = sb("W3", [P, 3, P])
        cols = sb("cols", [P, NCOLS])
        rows = sb("rows", [P, NROWS])
        ident = sb("ident", [P, P])
        identb = sb("identb", [P, P], BF16)
        hmask = sb("hmask", [P, 8 + 16])
        sel = sb("sel", [P, 2 * HG, P], BF16)
        ones = sb("ones", [P, 64])
        stat0 = sb("stat0", [P, 20])

        work = sb("work", [P, 3 * HG * D])
        sel32 = work[:, 0:2 * HG * P].rearrange("p (h k) -> p h k", k=P)
        A0 = work[:, 0:8 * D].rearrange("p (c l) -> p c l", l=D)
        Q12 = work[:, 0:NH * P].rearrange("p (h l) -> p h l", l=P)
        Q3 = work[:].rearrange("p (h l) -> p h l", l=D)
        X, T, G = (work[:, 1024 * i:1024 * i + 1024] for i in range(3))

        zP = sb("zP", [P, D])
        uP = sb("uP", [P, D])
        zR = sb("zR", [P, D])
        uC = sb("uC", [P, D])
        hT = sb("hT", [P, 2, D])
        Q0 = sb("Q0", [P, NH, D])
        K0 = sb("K0", [P, 8, D])
        K0b = sb("K0b", [P, 2, 2, D], BF16)
        Qb = sb("Qb", [P, 2, HG, D], BF16)
        V0 = sb("V0", [P, 2, 1024])
        Pr = sb("Pr", [P, 4, 512])
        Psum = sb("Psum", [P, 2, 512])
        nm = sb("nm", [P, 2, 2, HG], BF16)
        nmT = sb("nmT", [P, 2, D], BF16)
        U3 = sb("U3", [P, NG, D])
        x0, lat, junk, rec = (U3[:, i, :] for i in range(4))
        qs = sb("qs", [P, D])
        K1 = sb("K1", [P, 2, D])
        K1b = sb("K1b", [P, 2, D], BF16)
        V1 = sb("V1", [P, 2, NH, 32])
        K2 = sb("K2", [P, 2, P])
        K2b = sb("K2b", [P, 2, P], BF16)
        V2 = sb("V2", [P, NH, 32])
        K3 = sb("K3", [P, D])
        K3b = sb("K3b", [P, D], BF16)
        V3 = V1
        Ax = sb("Ax", [P, NG, P])
        junk3 = Ax[:, 0:2, :].rearrange("p g k -> p (g k)")
        res1 = sb("res1", [P, D])
        res2 = sb("res2", [P, D])
        xa = sb("xa", [P, D])
        xb = sb("xb", [P, D])
        oT = sb("oT", [P, 2, P])
        x1 = sb("x1", [P, D])
        x3 = x1
        stat = sb("stat", [P, 16])
        gate = sb("gate", [P, 3])
        half = sb("half", [P, 1])
        m1row = sb("m1row", [P, P], I32)
        m1col = sb("m1col", [P, 1], I32)
        m2row = sb("m2row", [P, P], U8)
        m2col = sb("m2col", [P, 1], U8)
        m3row = sb("m3row", [P, D], U8)
        m3col = sb("m3col", [P, 2], U8)
        b1row = sb("b1row", [P, D], BF16)
        b2row = sb("b2row", [P, P], BF16)
        b3row = sb("b3row", [P, D], BF16)
        bcol = sb("bcol", [P, 5])
        m3 = sb("m3", [P, D])
        xm = sb("xm", [P, D])
        xn = xm
        stat3 = sb("stat3", [P, 4])
        C3 = sb("C3", [P, 4, D])
        scratch = nc.dram_tensor("scratch", [P, NG, D], F32, kind="Internal").ap()

        def col(name, i=0):
            return cols[:, COLS[name][0] + i:COLS[name][0] + i + 1]

        def colrange(name, a, b):
            return cols[:, COLS[name][0] + a:COLS[name][0] + b]

        def row(name):
            return rows[:, ROWS[name][0]:ROWS[name][0] + ROWS[name][1]]

        ld_w0 = [sem(f"ld_w0_{i}") for i in range(6)]
        (ld_proj, ld_cols, ld_par, ld_rows, ld_wo, ld_w1, ld_w2, ld_w3, ld_mlp, ld_ctx, ld_res, ld_msk, ld_c3,
         st_u3, st_out) = (sem(n) for n in (
             "ld_proj", "ld_cols", "ld_par", "ld_rows", "ld_wo", "ld_w1", "ld_w2", "ld_w3", "ld_mlp", "ld_ctx",
             "ld_res", "ld_msk", "ld_c3", "st_u3", "st_out"))
        const_p, const_v = sem("const_p"), sem("const_v")
        mx_full = [sem(f"mx_full{i}") for i in range(2)]
        gp_full = [sem(f"gp_full{i}") for i in range(2)]
        sc_full, pv_done, den_done = sem("sc_full"), sem("pv_done"), sem("den_done")
        mx_done, nmT_ready, p_ready, ps_ready = (
            sem(n) for n in ("mx_done", "nmT_ready", "p_ready", "ps_ready"))
        (s_Q0, s_Qb, s_K0, s_V0, s_A0, s_x0, s_x0T, s_var0, s_pow0, s_latT, s_lat, s_hT, s_qs,
         s_Qx, s_K1, s_K1b, s_V1, s_K2,
         s_K2b, s_V2, s_K3, s_K3b, s_v3, s_V3, s_Ax, s_U3) = (sem("s_" + n) for n in (
             "Q0", "Qb", "K0", "V0", "A0", "x0", "x0T", "var0", "pow0", "latT", "lat", "hT", "qs",
             "Qx", "K1", "K1b", "V1", "K2",
             "K2b", "V2", "K3", "K3b", "v3", "V3", "Ax", "U3"))
        (s_res1, s_res2, s_xa, s_ssq, s_var, s_pow, s_xb, s_oT, s_X, s_sq, s_T, s_th, s_G, s_x1, s_x3) = (
            sem("s_" + n) for n in ("res1", "res2", "xa", "ssq", "var", "pow", "xb", "oT", "X", "sq", "T", "th",
                                    "G", "x1", "x3"))
        (s_msk, s_xm, s_nst, s_ninv, s_xn, s_v, s_std, s_o3) = (
            sem("s_" + n) for n in ("msk", "xm", "nst", "ninv", "xn", "v", "std", "o3"))
        v_step, p_step, f_step, v_apart, p_apart, n_apart = (
            sem(n) for n in ("v_step", "p_step", "f_step", "v_apart", "p_apart", "n_apart"))

        def is_first(b):
            return isinstance(b, int) and b == 0

        def is_last(b):
            return isinstance(b, int) and b == B - 1

        class Order:

            def __init__(self, names, base, b):
                self.names, self.base, self.b = names, base, b

            def at(self, name):
                n = self.names.index(name)
                return n % 2, self.base + n // 2

            def bank_taken(self, name):
                n = self.names.index(name) - 2
                if n < 0 and self.b is None:
                    return None
                if n < 0:
                    name, k = (PROJ[n], 0) if is_first(self.b) else (BODY[n], self.b - 1)
                else:
                    name = self.names[n]
                    k = (0 if self.b is None else self.b + 1) if name in PROJ else self.b
                tile, per_batch, count = TAKEN[name]
                return by_tile[tile], per_batch * k + count

        by_tile = {"x0": s_x0,  "qs": s_qs, "K1": s_K1, "V1": s_V1,
                   "xa": s_xa, "oT": s_oT, "X": s_X, "K2": s_K2, "x1": s_x1, "V2": s_V2, "K3": s_K3,
                   "v3": s_v3, "x3": s_x3, "Q0": s_Q0, "K0": s_K0, "V0": s_V0}

        def order_of(b):
            return Order(LAST if is_last(b) else BODY, b * (len(BODY) // 2) + len(PROJ) // 2, b)

        prologue = Order(PROJ, 0, None)

        def mx_bank_taken(b, n):
            L, g, u = MX_UNITS[n - 2]
            k = b - 1 if n < 2 else b
            if u == "T":
                return nmT_ready, SHIFT_N * k + SHIFTS.index((L, g)) + 1
            return mx_done, SC_N * k + SC_BASE[L] + g * STEPS[L] + u + 1

        def pv_bank_taken(b, m):
            k, m = (b - 1, m + PV_N - 2) if m < 2 else (b, m - 2)
            if m < 8:
                return s_A0, 8 * k + m + 1
            if m < PV_BASE[1]:
                return (s_hT, k + 1) if m == 8 else (s_lat, k + 1)
            if m < PV_BASE[3]:
                return s_Ax, 8 * k + m - PV_BASE[1] + 1
            return s_U3, 2 * k + m - PV_BASE[3] + 1

        def wait(eng, s, value):
            if isinstance(value, int) and value <= 0:
                return
            eng.wait_ge(s, value)

        class Apart:

            def __init__(self, eng, scratch, s, per_batch):
                self.eng, self.scratch, self.s, self.per_batch = eng, scratch, s, per_batch

            def begin(self, b):
                self.b, self.n = b, 0

            def wait(self, *waits):
                for s, v in waits:
                    wait(self.eng, s, v)
                wait(self.eng, self.s, self.b * self.per_batch + self.n)
                self.eng.tensor_tensor(self.scratch, half[:], half[:], ALU.add).then_inc(self.s, 1)
                self.n += 1

            def end(self):
                assert self.n == self.per_batch, self.n

        class Chain:

            def __init__(self, eng, s, per_batch):
                self.eng, self.s, self.per_batch = eng, s, per_batch

            def begin(self, b):
                self.b, self.n = b, 0

            def step(self, instruction, apart=None):
                instruction.then_inc(self.s, 1)
                self.n += 1
                if apart is not None:
                    apart.wait((self.s, self.b * self.per_batch + self.n))
                else:
                    self.eng.wait_ge(self.s, self.b * self.per_batch + self.n)

            def end(self):
                assert self.n == self.per_batch, self.n

        def shifts(b, L, g):
            return SHIFT_N * b + SHIFTS.index((L, g // 2 * 2 if L == 2 else g)) + 1

        def unit_heads(L, g, u):
            if L in (0, 3):
                h = HG * g + 2 * (u // 2)
                return [h, h + 1], u % 2, D
            return list(range(HG * g, HG * g + HG)), u if L == 1 else 0, P

        def order_of_maxima(L):
            steps = STEPS[L]
            before = [[] for _ in range(NG * steps + 1)]
            if L == 2:
                before[-1], before[0], before[1] = [(0, 0), (1, 0), (0, "T"), (2, 0)], [(3, 0)], [(2, "T")]
                return before
            for _, g, u in (unit for unit in MX_UNITS if unit[0] == L):
                at = g * steps - 1 if u == "T" else g * steps + u - steps - 1
                before[max(at, -1)].append((g, u))
            if L == 3:
                before[-1].remove((1, 0))
                before[0:4] = [[], [(1, 0), (1, 1)], [(1, 2), (1, 3)], [(1, "T"), (2, 0)]]
            return before

        EARLY = {11: 2, 12: 2, 13: 1, 14: 1}

        def early_maxima(n):
            units = order_of_maxima(0)[-1]
            if n is None:
                return units
            at = sum(count for m, count in EARLY.items() if m < n)
            return units[at:at + EARLY.get(n, 0)]

        def every_batch(eng, body):
            body(0)
            with eng.Fori(1, B - 1) as b:
                body(b)
            body(B - 1)

        assert len(BODY) % 2 == len(LAST) % 2 == 0
        block = stack.enter_context(nc.Block())

        @block.sync
        def _(sp):
            def load_mlp(a, c):
                sp.dma_start(WA[:], a).then_inc(ld_mlp, 16)
                sp.dma_start(WB[:], c).then_inc(ld_mlp, 16)

            sp.dma_start(zP[:], z_in[0]).then_inc(ld_proj, 16)
            sp.dma_start(uP[:], ctx_in[0]).then_inc(ld_proj, 16)
            for i in range(6):
                sp.dma_start(W0[:, i], w0[i]).then_inc(ld_w0[i], 16)
                if i == 0:
                    sp.dma_start(cols[:], cols_in).then_inc(ld_cols, 16)
                if i == 2:
                    sp.dma_start(ident[:], ident_in).then_inc(ld_par, 16)
                    sp.dma_start(hmask[:], hmask_in).then_inc(ld_par, 16)
                    sp.dma_start(sel32, sel_in).then_inc(ld_par, 16)
            sp.dma_start(WO[:], wo).then_inc(ld_wo, 16)
            sp.dma_start(rows[:], rows_in.to_broadcast([P, NROWS])).then_inc(ld_rows, 16)
            for dst, src in ((W1QK, w1qk), (W1V, w1v), (W1O, w1o)):
                sp.dma_start(dst[:], src).then_inc(ld_w1, 16)
            load_mlp(w1a, w1b)
            for dst, src in ((W2QKV, w2qkv), (W2O, w2o)):
                sp.dma_start(dst[:], src).then_inc(ld_w2, 16)
            sp.dma_start(W3[:], w3).then_inc(ld_w3, 16)

            def store_batch(b):
                sp.wait_ge(s_o3, b + 1)
                sp.dma_start(out[b], C3[:, 3, :]).then_inc(st_out, 16)

            def body(b):
                wait(sp, s_V3, b)
                sp.dma_start(hT[:, :, 0:P], ctxT_in[b]).then_inc(ld_ctx, 16)
                sp.dma_start(uC[:], ctx_in[b]).then_inc(ld_ctx, 16)
                wait(sp, s_x0, b)
                sp.dma_start(zR[:], z_in[b]).then_inc(ld_res, 16)
                wait(sp, s_msk, N_MSK * b)
                sp.dma_start(m1row[0:1, :], mask1[b]).then_inc(ld_msk, 16)
                sp.dma_start(m1col[:], mask1[b].rearrange("o p -> p o")).then_inc(ld_msk, 16)
                sp.dma_start(m2row[0:1, :], mask2[b]).then_inc(ld_msk, 16)
                sp.dma_start(m2col[:], mask2[b].rearrange("o p -> p o")).then_inc(ld_msk, 16)
                sp.dma_start(m3row[:], mask3[b].to_broadcast([P, D])).then_inc(ld_msk, 16)
                for c in range(2):
                    sp.dma_start(m3col[:, c:c + 1], mask3[b][:, c * P:c * P + P].rearrange("o p -> p o"))\
                        .then_inc(ld_msk, 16)
                if not is_last(b):
                    for s in (s_Q0, s_K0, s_V0):
                        sp.wait_ge(s, 4 * b + 4)
                    sp.dma_start(zP[:], z_in[b + 1]).then_inc(ld_proj, 16)
                    sp.dma_start(uP[:], ctx_in[b + 1]).then_inc(ld_proj, 16)
                if not is_first(b):
                    store_batch(b - 1)
                sp.wait_ge(s_x1, b + 1)
                load_mlp(w2a, w2b)
                if not is_last(b):
                    sp.wait_ge(s_x3, b + 1)
                    load_mlp(w1a, w1b)
                for half in range(2):
                    sp.wait_ge(s_U3, 2 * b + half + 1)
                    sp.dma_start(scratch[:, 2 * half:2 * half + 2], U3[:, 2 * half:2 * half + 2, :])\
                        .then_inc(st_u3, 16)
                    sp.wait_ge(st_u3, 32 * b + 16 * half + 16)
                    for q in range(3):
                        for g in (2 * half, 2 * half + 1):
                            src = scratch.rearrange("(s r) g i -> g s r i", r=32)[g][:, 8 * q:8 * q + 8, :]
                            sp.dma_start(C3[32 * g:32 * g + 32, q, :], src).then_inc(ld_c3, 16)

            every_batch(sp, body)
            store_batch(B - 1)
            sp.wait_ge(st_out, 16 * B)

        @block.tensor
        def _(pe):
            def project(name, o, k):
                bank, n = o.at(name)
                i = int(name[-1])
                if name in ("qp0", "kp0"):
                    pe.wait_ge(ld_proj, 32 * k + 32)
                if o.b is not None or n >= 1:
                    pe.wait_ge(*o.bank_taken(name))
                if name[0] in "qk":
                    for c in range(2):
                        piece, at = divmod((2 * i + c + (8 if name[0] == "k" else 0)) * P, 512)
                        pe.wait_ge(ld_w0[piece], 16)
                        for s in range(2):
                            dst = GP[bank][:, c * D + s * P:c * D + s * P + P]
                            pe.matmul(dst, W0[:, piece, 2 * s, at:at + P], zP[:, s * P:s * P + P],
                                      start=True, stop=False)
                            mm = pe.matmul(dst, W0[:, piece, 2 * s + 1, at:at + P], uP[:, s * P:s * P + P],
                                           start=False, stop=True)
                else:
                    s, w = divmod(i, 2)
                    pe.wait_ge(ld_w0[4 + w], 16)
                    pe.matmul(GP[bank][:], zP[:, s * P:s * P + P], W0[:, 4 + w, 2 * s, :], start=True, stop=False)
                    mm = pe.matmul(GP[bank][:], uP[:, s * P:s * P + P], W0[:, 4 + w, 2 * s + 1, :],
                                   start=False, stop=True)
                mm.then_inc(gp_full[bank], 1)

            def maxima_pass(b, L, Kb, mrow, ready):
                steps = STEPS[L]
                halves = 2 if L in (0, 3) else 1

                def ready_group(g):
                    pe.wait_ge(s_Qb, 17 * b + 4 * L + g + 1 + (L == 3 and g > 0))
                    if g == 0:
                        for s, v in ready:
                            pe.wait_ge(s, v)
                    if L == 0:
                        pe.wait_ge(s_K0, 4 * b + g + 1)

                def maxima(g, u):
                    n = MX_UNITS.index((L, g, u))
                    dst = MX[n % 2]
                    if (L, g, u) == (3, 0, 2):
                        pe.wait_ge(s_Qb, 17 * b + 14)
                    wait(pe, *mx_bank_taken(b, n))
                    if mrow is not None:
                        keys = mrow.shape[1]
                        pe.matmul(dst[:].rearrange("p (a k) -> p a k", k=keys), sel[:, 0, :],
                                  mrow.unsqueeze(1).to_broadcast([P, 512 // keys, keys]), start=True, stop=False,
                                  skip_group_check=True)
                    if L in (0, 3):
                        parts = [(HG * g + u, s) for s in range(2)]
                    else:
                        per = HG // steps
                        parts = [(HG * g + per * u + j, 0) for j in range(per)]
                    w = 512 // len(parts)
                    for j, (h, s) in enumerate(parts):
                        mm = pe.matmul(dst[:, j * w:j * w + w], Qb[:, g % 2, h % HG, s * P:s * P + P], Kb(h),
                                       start=mrow is None, stop=True, skip_group_check=True)
                    mm.then_inc(mx_full[n % 2], 1)

                def shift_rows(g):
                    n = MX_UNITS.index((L, g, "T"))
                    rows_out = MX[n % 2][:].bitcast(BF16)
                    wait(pe, *mx_bank_taken(b, n))
                    pe.wait_ge(mx_done, SC_N * b + SC_BASE[L] + (g + (2 if L == 2 else 1)) * steps)
                    if L == 2:
                        mm = pe.transpose(rows_out[0:8, 0:P], nm[:, g // 2].rearrange("p s k -> p (s k)"), identb[:])
                    else:
                        for s in range(halves):
                            mm = pe.transpose(rows_out[0:4, s * P:s * P + P], nm[:, g % 2, s, :], identb[:])
                    mm.then_inc(mx_full[n % 2], 1)

                def make(g, u):
                    if u == "T":
                        shift_rows(g)
                    else:
                        if u == 0:
                            ready_group(g)
                        maxima(g, u)
                return make

            def attention(b, o, L, make, K, Qf, V, v_ready, between=None, beside=None, amid=None):
                steps = STEPS[L]

                def scores(g, u):
                    n = SC_BASE[L] + g * steps + u
                    heads, kc, w = unit_heads(L, g, u)
                    wait(pe, p_ready, SC_N * b + n - 1)
                    if u == 0:
                        pe.wait_ge(nmT_ready, shifts(b, L, g))
                    for j, h in enumerate(heads):
                        dst = SC[n % 2][:, j * w:j * w + w]
                        which, shift = (sel[:, h % 8, :], g // 2) if L == 2 else (sel[:, h % HG, :], g % 2)
                        pe.matmul(dst, which, nmT[:, shift, 0:w], start=(j == 0), stop=False, skip_group_check=True)
                    pe.matmul(SC[n % 2][:].rearrange("p (h l) -> p h l", l=w), K(heads[0])[:, kc * P:kc * P + P],
                              Qf(heads[0], len(heads)), start=False, stop=True, skip_group_check=True)\
                        .then_inc(sc_full, 1)

                def pv(g, u):
                    n = SC_BASE[L] + g * steps + u
                    heads, kc, w = unit_heads(L, g, u)
                    m = PV_BASE[L] + {0: 2 * g + u // 2, 3: g // 2}.get(L, g)
                    pe.wait_ge(p_ready, SC_N * b + n + 1)
                    if (kc == 0 if L == 0 else u == 0 and (L < 3 or g % 2 == 0)):
                        wait(pe, *pv_bank_taken(b, m))
                    at = w * (g % 2) if L == 3 else 0
                    for j, h in enumerate(heads):
                        if L == 0:
                            dst, v = PV[m % 2][64 * j:64 * j + 64, 0:D], V[:, kc, h * 64:h * 64 + 64]
                        else:
                            s = 32 * (h % HG)
                            dst, v = PV[m % 2][s:s + 32, at:at + w], V(h, kc)
                        mm = pe.matmul(dst, v, Pr[:, n % 4, j * w:j * w + w], start=(kc == 0),
                                       stop=(kc == 1 or L == 2), skip_group_check=True)
                    mm.then_inc(pv_done, 1)

                def denominator(c):
                    pe.wait_ge(ps_ready, 8 * b + c + 1)
                    for j in range(2):
                        mm = pe.matmul(PV[c % 2][64 * j:64 * j + 64, D:2 * D], ones[:],
                                       Psum[:, c % 2, j * D:j * D + D], start=True, stop=True,
                                       skip_group_check=True)
                    mm.then_inc(den_done, 1)

                def out_chunk(c):
                    bank, n = o.at("wo")
                    if c == 0:
                        pe.wait_ge(*o.bank_taken("wo"))
                        pe.wait_ge(ld_wo, 16)
                    pe.wait_ge(s_A0, 8 * b + c + 1)
                    mm = pe.matmul(GP[bank][:, 0:D], WO[:, c, :], A0[:, c, :], start=(c == 0), stop=(c == 7),
                                   skip_group_check=True)
                    if c == 7:
                        mm.then_inc(gp_full[bank], 1)

                if L != 0:
                    for g, u in order_of_maxima(L)[-1]:
                        if (g, u) == (0, "T") and amid:
                            amid()
                        make(g, u)
                units = [(g, u) for g in range(NG) for u in range(steps)]
                for n, (g, u) in enumerate(units):
                    for unit in order_of_maxima(L)[n]:
                        make(*unit)
                    scores(g, u)
                    if n == LAG[L]:
                        pe.wait_ge(*v_ready)
                    if n >= LAG[L]:
                        pv(*units[n - LAG[L]])
                    if beside:
                        beside(n)
                    if L == 0 and n % 2 and n >= 3:
                        denominator((n - 3) // 2)
                    if L == 0 and n % 2 and n >= 7:
                        out_chunk((n - 7) // 2)
                for unit in units[-LAG[L]:]:
                    pv(*unit)
                if L == 0:
                    denominator(7)
                    for c in range(5, 8):
                        if c == 7:
                            between()
                        out_chunk(c)

            def maxima0(b):
                return maxima_pass(b, 0, lambda h: K0b[:, h // HG % 2, h // 2 % 2, :], None, [])

            def body(b):
                o = order_of(b)

                def fill(*names):
                    if not is_last(b):
                        for name in names:
                            project(name, o, b + 1)

                def begin(name, *ready):
                    bank, n = o.at(name)
                    pe.wait_ge(*o.bank_taken(name))
                    for s, v in ready:
                        pe.wait_ge(s, v)
                    return GP[bank], gp_full[bank]

                def transpose_pair(name, src, ready):
                    g, full = begin(name, ready)
                    for c in range(2):
                        mm = pe.transpose(g[:, c * P:c * P + P], src[:, c * P:c * P + P], ident[:])
                    mm.then_inc(full, 1)

                def heads_T(name, W, rhs, width, *ready):
                    g, full = begin(name, *ready)
                    for m in range(2):
                        for c in range(2):
                            mm = pe.matmul(g[:, m * width:m * width + width], W[:, c, m * P:m * P + P], rhs(c),
                                           start=(c == 0), stop=(c == 1), skip_group_check=True)
                    mm.then_inc(full, 1)

                def slots_out(name, W, which):
                    g, full = begin(name)
                    for s in range(NG):
                        pe.wait_ge(s_Ax, 8 * b + 4 * which + s + 1)
                        mm = pe.matmul(g[:, 0:D], Ax[:, s, :], W[:, s, :], start=(s == 0), stop=(s == NG - 1))
                    mm.then_inc(full, 1)

                def mlp_in(name, *ready):
                    g, full = begin(name, *ready)
                    for j in range(4):
                        f = 4 * int(name[1]) + j
                        for c in range(2):
                            mm = pe.matmul(g[:, j * P:j * P + P], WA[:, c, f * P:f * P + P], oT[:, c, :],
                                           start=(c == 0), stop=(c == 1), skip_group_check=True)
                    mm.then_inc(full, 1)

                def mlp_out(name, which):
                    g, full = begin(name)
                    for f in range(8):
                        if f % 4 == 0:
                            pe.wait_ge(s_G, 4 * b + 2 * which + f // 4 + 1)
                        mm = pe.matmul(g[:, 0:D], G[:, f * P:f * P + P], WB[:, f, :], start=(f == 0), stop=(f == 7))
                    mm.then_inc(full, 1)

                attention(b, o, 0, maxima0(b), lambda h: K0[:, h // 2, :], lambda h, n: Q0[:, h:h + n, :], V0,
                          (s_V0, 4 * b + 4),
                          lambda: fill("kp0"))
                wait(pe, *pv_bank_taken(b, 8))
                pe.wait_ge(s_x0, b + 1)
                for c in range(2):
                    mm = pe.transpose(PV[0][:, c * P:c * P + P], x0[:, c * P:c * P + P], ident[:])
                mm.then_inc(s_x0T, 1)
                fill("kp1", "kp2")
                heads_T("q1", W1QK[:, 0], lambda c: hT[:, c, P:D], P, (s_hT, b + 1), (ld_w1, 48))
                heads_T("k1", W1QK[:, 1], lambda c: hT[:, c, :], D, (ld_ctx, 32 * b + 32))

                def v1(name, kc):
                    g, full = begin(name)
                    for c in range(2):
                        mm = pe.matmul(g[:, 0:D], hT[:, c, kc * P:kc * P + P], W1V[:, c, :],
                                       start=(c == 0), stop=(c == 1))
                    mm.then_inc(full, 1)
                v1("v1", 1)

                def amid1():
                    wait(pe, *pv_bank_taken(b, 9))
                    for c in range(2):
                        mm = pe.transpose(PV[1][:, c * P:c * P + P], hT[:, c, P:D], ident[:])
                    mm.then_inc(s_latT, 1)
                    v1("v1c", 0)
                    fill("qp0")

                make = maxima_pass(b, 1, lambda h: K1b[:, h // 8, :], b1row[:],
                                   [(s_K1b, b + 1), (s_msk, N_MSK * b + N_MSK - 1)])
                attention(b, o, 1, make, lambda h: K1[:, h // 8, :], lambda h, n: Q12[:, h:h + n, :],
                          lambda h, kc: V1[:, kc, h, :], (s_V1, 2 * b + 2), amid=amid1)
                slots_out("o1", W1O, 0)
                fill("vp0")
                transpose_pair("oT", xb, (s_xb, 3 * b + 1))
                fill("vp1")
                mlp_in("m0", (s_oT, 3 * b + 1), (ld_mlp, 64 * b + 32))
                mlp_in("m1")
                heads_T("k2", W2QKV[:, 1], lambda c: hT[:, c, 0:P], P, (ld_w2, 32))
                fill("qp1")
                mlp_out("w2", 0)
                fill("kp3")
                g, full = begin("v2")
                for c in range(2):
                    mm = pe.matmul(g[:, 0:D], hT[:, c, 0:P], W2QKV[:, 2, c, :], start=(c == 0), stop=(c == 1))
                mm.then_inc(full, 1)
                transpose_pair("yT", xb, (s_xb, 3 * b + 2))
                fill("vp2")
                heads_T("q2", W2QKV[:, 0], lambda c: oT[:, c, :], P, (s_oT, 3 * b + 2))
                fill("qp2")
                make = maxima_pass(b, 2, lambda h: K2b[:, h // 8, :], b2row[:], [(s_K2b, b + 1)])
                attention(b, o, 2, make, lambda h: K2[:, h // 8, :], lambda h, n: Q12[:, h:h + n, :],
                          lambda h, kc: V2[:, h, :], (s_V2, b + 1))
                slots_out("o2", W2O, 1)
                g, full = begin("k3", (ld_w3, 16))
                pe.matmul(g[:, 0:D], W3[:, 1, :], uC[:], start=True, stop=True).then_inc(full, 1)
                transpose_pair("yT2", xb, (s_xb, 3 * b + 3))
                g, full = begin("v3")
                for kc in range(2):
                    mm = pe.matmul(g[:, kc * P:kc * P + P], uC[:, kc * P:kc * P + P], W3[:, 2, :],
                                   start=True, stop=True, skip_group_check=True)
                mm.then_inc(full, 1)
                mlp_in("n0", (s_oT, 3 * b + 3), (ld_mlp, 64 * b + 64))
                mlp_in("n1")
                fill("vp3")
                mlp_out("w4", 1)
                g, full = begin("q3", (s_x3, b + 1))
                pe.matmul(g[:, 0:D], W3[:, 0, :], x3[:], start=True, stop=True).then_inc(full, 1)
                make = maxima_pass(b, 3, lambda h: K3b[:], b3row[:], [(s_K3b, b + 1)])
                make0 = None if is_last(b) else maxima0(b + 1)

                def beside(n):
                    if make0:
                        for unit in early_maxima(n):
                            make0(*unit)
                attention(b, o, 3, make, lambda h: K3[:], lambda h, n: Q3[:, h % 12:h % 12 + n, :],
                          lambda h, kc: V3[:, kc, h, :],
                          (s_V3, b + 1), beside=beside, amid=lambda: fill("qp3"))

            for name in PROJ:
                project(name, prologue, 0)
            pe.wait_ge(const_v, 2)
            pe.wait_ge(const_p, 1)
            pe.wait_ge(ld_par, 48)
            for unit in early_maxima(None):
                maxima0(0)(*unit)
            every_batch(pe, body)

        @block.scalar
        def _(act):
            def take(o, name):
                bank, n = o.at(name)
                act.wait_ge(gp_full[bank], n + 1)
                return GP[bank]

            def project(name, o):
                g = take(o, name)
                i = int(name[-1])
                if name[0] == "k":
                    act.activation(K0[:, 2 * i:2 * i + 2, :].rearrange("p c l -> p (c l)"), g[:], ACT.Copy)\
                        .then_inc(s_K0, 1)
                else:
                    s, w = divmod(i, 2)
                    act.activation(V0[:, s, w * 512:w * 512 + 512], g[:], ACT.Copy).then_inc(s_V0, 1)

            def shift_rows(b, L, g):
                n = MX_UNITS.index((L, g, "T"))
                w = D if L in (0, 3) else P
                act.wait_ge(mx_full[n % 2], b * (MX_N // 2) + n // 2 + 1)
                rows, ring = (8, g // 2) if L == 2 else (4, g % 2)
                act.activation(nmT[0:rows, ring, 0:w], MX[n % 2][:].bitcast(BF16)[0:rows, 0:w], ACT.Copy)\
                    .then_inc(nmT_ready, 1)

            def cast(b, L, g):
                j = 4 * L + g - 2
                k, j = (b - 1, j + 16) if j < 0 else (b, j)
                wait(act, mx_done, SC_N * k + SC_BASE[j // 4] + (j % 4 + 1) * STEPS[j // 4])
                dst = Qb[:, g % 2]
                if L == 0:
                    act.wait_ge(s_K0, 4 * b + g + 1)
                    act.activation(K0b[:, g % 2], K0[:, 2 * g:2 * g + 2, :], ACT.Copy)
                    act.wait_ge(s_Q0, 4 * b + g + 1)
                    src = Q0[:, HG * g:HG * g + HG, :]
                elif L == 3:
                    act.wait_ge(s_Qx, 11 * b + 8 + g)
                    src = Q3[:, HG * (g % 3):HG * (g % 3) + HG, :]
                else:
                    act.wait_ge(s_Qx, 11 * b + 4 * (L - 1) + g + 1)
                    dst, src = Qb[:, g % 2, :, 0:P], Q12[:, HG * g:HG * g + HG, :]
                act.activation(dst, src, ACT.Copy).then_inc(s_Qb, 1)

            def early(b):
                return [lambda: cast(b, 0, 0), lambda: cast(b, 0, 1), lambda: shift_rows(b, 0, 0)]

            def attention(b, L, scale, after=None, amid=None, filling=None):
                steps = STEPS[L]

                def exp(n):
                    kc = unit_heads(L, *divmod(n, steps))[1]
                    n += SC_BASE[L]
                    act.wait_ge(sc_full, SC_N * b + n + 1)
                    wait(act, pv_done, SC_N * b + n - 3)
                    if 4 <= n < 20:
                        act.wait_ge(ps_ready, 8 * b + (n - 4) // 2 + 1)
                    bias = {0: 0.0, 1: bcol[:, kc:kc + 1], 2: bcol[:, 2:3], 3: bcol[:, 3 + kc:4 + kc]}[L]
                    act.activation(Pr[:, n % 4, :], SC[n % 2][:], ACT.Exp, bias=bias, scale=scale)\
                        .then_inc(p_ready, 1)

                if L in (1, 2):
                    cast(b, L, 0)
                    if amid:
                        amid()
                    cast(b, L, 1)
                if L == 2:
                    cast(b, L, 2)
                    cast(b, L, 3)
                if L != 0:
                    shift_rows(b, L, 0)
                if L == 3:
                    cast(b, L, 1)
                if L == 1:
                    cast(b, L, 2)
                if filling:
                    filling()
                for n in range(NG * steps):
                    for g, u in order_of_maxima(L)[n]:
                        if u == "T":
                            shift_rows(b, L, g)
                    exp(n)
                    g, u = divmod(n + steps + 3, steps)
                    if L != 2 and u == 0 and 2 <= g < NG:
                        cast(b, L, g)
                    if after:
                        after(n)

            def std3(b):
                act.wait_ge(s_v, b + 1)
                wait(act, st_out, 16 * b)
                act.activation(C3[:, 3, :], C3[:, 1, :], ACT.Sqrt).then_inc(s_std, 1)

            def mlp(b, which, between, after=lambda: None):
                for i in range(2):
                    h = slice(512 * i, 512 * i + 512)
                    act.wait_ge(s_X, 4 * b + 2 * which + i + 1)
                    act.activation(T[:, h], X[:, h], ACT.Square, scale=GELU_A ** 0.5).then_inc(s_sq, 1)
                between()
                for i in range(2):
                    h = slice(512 * i, 512 * i + 512)
                    act.wait_ge(s_T, 4 * b + 2 * which + i + 1)
                    act.activation(T[:, h], T[:, h], ACT.Tanh, scale=GELU_C).then_inc(s_th, 1)
                after()

            def body(b):
                o = order_of(b)

                def fill(*names):
                    if not is_last(b):
                        for name in names:
                            project(name, o)

                def turned(name, weight, bias=None):
                    g = take(o, name)
                    for c in range(2):
                        ins = act.activation(oT[:, c, :], g[:, c * P:c * P + P], ACT.Identity, scale=col(weight, c),
                                             bias=col(bias, c) if bias else 0.0)
                    ins.then_inc(s_oT, 1)

                def keys(name, K, bias, width, s):
                    g = take(o, name)
                    for m in range(len(bias)):
                        ins = act.activation(K[:, m, :], g[:, m * width:m * width + width], ACT.Identity,
                                             bias=bias[m])
                    ins.then_inc(s, 1)

                def keys_bf16(K, Kb, s, sb):
                    act.wait_ge(s, b + 1)
                    act.activation(Kb, K, ACT.Copy).then_inc(sb, 1)

                attention(b, 0, 0.125)
                if not is_first(b):
                    std3(b - 1)
                fill("kp0", "kp1", "kp2")

                def latents():
                    act.wait_ge(s_latT, b + 1)
                    act.activation(lat, PV[1][:, 0:D], ACT.Copy).then_inc(s_lat, 1)

                def keys1():
                    g = take(o, "k1")
                    for dst, sem_done in ((K1b, s_K1b), (K1, s_K1)):
                        for m in range(2):
                            ins = act.activation(dst[:, m, :], g[:, m * D:m * D + D], ACT.Identity, bias=col("kb1", m))
                        ins.then_inc(sem_done, 1)
                attention(b, 1, 1.0 / 16, amid=keys1, filling=latents)
                act.wait_ge(s_xa, 2 * b + 1)
                act.activation(junk, xa[:], ACT.Square, accum_out=stat[:, 0:1]).then_inc(s_ssq, 1)
                fill("vp0")
                turned("oT", "pw")
                fill("vp1")
                mlp(b, 0, lambda: keys("k2", K2[:], [col("kb2", 0), col("kb2", 1)], P, s_K2),
                    lambda: keys_bf16(K2[:], K2b[:], s_K2, s_K2b))
                fill("kp3")
                turned("yT", "ln1w", "ln1b")
                fill("vp2")
                attention(b, 2, 0.25)
                keys("k3", K3[:].unsqueeze(1), [col("bk")], D, s_K3)
                turned("yT2", "ln2w", "ln2b")

                def squares():
                    act.wait_ge(s_v3, b + 1)
                    act.activation(V3[:, :, :, 8:16], V3[:, :, :, 0:8], ACT.Square).then_inc(s_V3, 1)
                mlp(b, 1, lambda: None, lambda: (squares(), keys_bf16(K3[:], K3b[:], s_K3, s_K3b)))
                fill("vp3")
                def sums(i):
                    act.wait_ge(pv_done, SC_N * b + SC_BASE[3] + 8 * i + 8)
                    wait(act, st_u3, 32 * b)
                    act.activation(U3[:, 2 * i:2 * i + 2, :].rearrange("p g i -> p (g i)"), PV[(PV_BASE[3] + i) % 2][:],
                                   ACT.Copy).then_inc(s_U3, 1)

                act.wait_ge(s_qs, 3 * b + 3)
                for h in range(HG):
                    act.activation(Q3[:, h, :], qs[:], ACT.Copy, scale=hmask[:, 8 + h:9 + h])

                def after(n):
                    if n == 10:
                        sums(0)
                    if n in (8, 12, 14) and not is_last(b):
                        early(b + 1)[(8, 12, 14).index(n)]()
                attention(b, 3, 8.0 ** -0.5, after)
                sums(1)
                act.wait_ge(s_xm, b + 1)
                for i, (src, func) in enumerate(((xm, ACT.Copy), (xm, ACT.Square), (m3, ACT.Copy))):
                    act.activation(junk3, src[:], func, accum_out=stat[:, 4 + i:5 + i]).then_inc(s_nst, 1)
                    act.wait_ge(s_nst, 3 * b + i + 1)

            for name in PROJ[4:]:
                project(name, prologue)
            act.wait_ge(const_v, 2)
            act.wait_ge(const_p, 1)
            act.wait_ge(ld_cols, 16)
            for step in early(0):
                step()
            every_batch(act, body)
            std3(B - 1)

        @block.vector
        def _(dve):
            chain = Chain(dve, v_step, V_STEPS)
            ending = Chain(dve, f_step, F_STEPS)
            apart = Apart(dve, gate[:, 1:2], v_apart, 11)

            def take(o, name):
                bank, n = o.at(name)
                dve.wait_ge(gp_full[bank], n + 1)
                return GP[bank]

            def project(name, o):
                g = take(o, name)
                i = int(name[-1])
                for r in range(2):
                    p = slice(64 * r, 64 * r + 64)
                    bias = colrange("rwb", 2 * i, 2 * i + 2)[p].unsqueeze(2).to_broadcast([64, 2, D])
                    ins = dve.tensor_tensor(Q0[p, 4 * i + r:4 * i + r + 3:2, :],
                                            g[p, :].rearrange("p (c l) -> p c l", c=2), bias, ALU.add)
                ins.then_inc(s_Q0, 1)

            def maxima(b, L, g, u):
                steps = STEPS[L]
                halves = 2 if L in (0, 3) else 1
                if u == "T":
                    return
                n = MX_UNITS.index((L, g, u))
                dve.wait_ge(mx_full[n % 2], b * (MX_N // 2) + n // 2 + 1)
                if halves == 2:
                    dst, a = nm[:, g % 2, :, u], 2
                elif L == 2:
                    dst, a = nm[:, g // 2, g % 2, :], HG
                else:
                    a = HG // steps
                    dst = nm[:, g % 2, 0, a * u:a * u + a]
                dve.tensor_reduce(dst, MX[n % 2][:].rearrange("p (a k) -> p a k", a=a), AX_X, ALU.max,
                                  negate=True).then_inc(mx_done, 1)

            def attention(b, L, after_step=None, amid=lambda: None):
                if L != 0:
                    for g, u in order_of_maxima(L)[-1]:
                        if (g, u) == (0, "T"):
                            amid()
                        maxima(b, L, g, u)
                if after_step:
                    after_step(-1)
                for n in range(NG * STEPS[L]):
                    for unit in order_of_maxima(L)[n]:
                        maxima(b, L, *unit)
                    if after_step:
                        after_step(n)

            def quotient0(b, c):
                dve.wait_ge(den_done, 8 * b + c + 1)
                wait(dve, s_Ax, 8 * b) if c == 0 else dve.wait_ge(s_A0, 8 * b + c)
                chain.step(dve.reciprocal(rec, PV[c % 2][:, D:2 * D]))
                dve.tensor_tensor(A0[:, c, :], PV[c % 2][:, 0:D], rec, ALU.mult).then_inc(s_A0, 1)

            def quotient(b, L, g):
                bank = PV[(PV_BASE[L] + g) % 2][:, 0:P]
                used = NG * (L - 1) + g
                den = rec[:, g % 2 * P:g % 2 * P + P]
                apart.wait((s_Ax, 8 * b + used - 1) if used > 1 else (s_A0, 8 * b + 8),
                           (pv_done, SC_N * b + SC_BASE[L] + (g + 1) * STEPS[L]))
                chain.step(dve.stream_shuffle(den, bank, [16 + r % 16 for r in range(32)]))
                chain.step(dve.reciprocal(den, den))
                dve.tensor_tensor(Ax[:, g, :], bank, den, ALU.mult).then_inc(s_Ax, 1)

            def queries(b, o, L, bias):
                g = take(o, f"q{L}")
                n = bias[2] - bias[1]
                dst, src = (t[:, 0:D].rearrange("p (c k) -> p c k", c=n) for t in (qs, g))
                dve.tensor_tensor(dst, src, colrange(*bias).unsqueeze(2).to_broadcast([P, n, D // n]), ALU.add)\
                    .then_inc(s_qs, 1)
                dve.wait_ge(s_qs, 3 * b + L)

            def blocks12(b, o, L):
                queries(b, o, L, (f"qb{L}", 0, 2))
                for i in range(NG):
                    dve.tensor_tensor(
                        Q12[:, HG * i:HG * i + HG, :],
                        qs[:, i // 2 * P:i // 2 * P + P].unsqueeze(1).to_broadcast([P, HG, P]),
                        hmask[:, HG * (i % 2):HG * (i % 2) + HG].unsqueeze(2).to_broadcast([P, HG, P]), ALU.mult)\
                        .then_inc(s_Qx, 1)

            def block3(b, dst, h):
                n = dst.shape[1]
                return dve.tensor_tensor(dst, qs[:].unsqueeze(1).to_broadcast([P, n, D]),
                                         hmask[:, 8 + h:8 + h + n].unsqueeze(2).to_broadcast([P, n, D]), ALU.mult)

            def mlp(b, o, names, bias, which):
                for i, name in enumerate(names):
                    g = take(o, name)
                    h = slice(512 * i, 512 * i + 512)
                    dve.tensor_tensor(X[:, h].rearrange("p (f k) -> p f k", k=P),
                                      g[:].rearrange("p (f k) -> p f k", k=P),
                                      colrange(bias, 4 * i, 4 * i + 4).unsqueeze(2).to_broadcast([P, 4, P]),
                                      ALU.add).then_inc(s_X, 1)
                for i in range(2):
                    h = slice(512 * i, 512 * i + 512)
                    dve.wait_ge(s_sq, 4 * b + 2 * which + i + 1)
                    dve.scalar_tensor_tensor(out=T[:, h], in0=T[:, h], scalar=1.0, in1=X[:, h], op0=ALU.add,
                                             op1=ALU.mult).then_inc(s_T, 1)
                for i in range(2):
                    h = slice(512 * i, 512 * i + 512)
                    dve.wait_ge(s_th, 4 * b + 2 * which + i + 1)
                    dve.scalar_tensor_tensor(out=G[:, h], in0=T[:, h], scalar=1.0, in1=X[:, h], op0=ALU.add,
                                             op1=ALU.mult).then_inc(s_G, 1)

            def layer_norm(b, src, ready, k, meanwhile=lambda: None):
                dve.wait_ge(*ready)
                chain.step(dve.bn_stats(stat[:, 8:14], src[:]), apart)
                chain.step(dve.bn_aggr(stat[:, 14:16], stat[:, 8:14]))
                dve.tensor_scalar(stat[:, 1:2], stat[:, 15:16], 1e-5, None, ALU.add).then_inc(s_var, 1)
                meanwhile()
                dve.wait_ge(s_pow, 3 * b + k)
                dve.tensor_scalar(xb[:], src[:], stat[:, 14:15], stat[:, 2:3], ALU.subtract, ALU.mult)\
                    .then_inc(s_xb, 1)

            def end3(b):
                ending.begin(b)
                dve.wait_ge(ld_c3, 16 * 3 * NG * (b + 1))
                ending.step(dve.reciprocal(C3[:, 2, :], C3[:, 2, :]))
                ending.step(dve.tensor_tensor(C3[:, 0, :], C3[:, 0, :], C3[:, 2, :], ALU.mult))
                ending.step(dve.tensor_tensor(C3[:, 1, :], C3[:, 1, :], C3[:, 2, :], ALU.mult))
                ending.step(dve.tensor_tensor(C3[:, 2, :], C3[:, 0, :], C3[:, 0, :], ALU.mult))
                ending.step(dve.tensor_tensor(C3[:, 1, :], C3[:, 1, :], C3[:, 2, :], ALU.subtract))
                dve.tensor_scalar(C3[:, 1, :], C3[:, 1, :], 0.0, None, ALU.max).then_inc(s_v, 1)

            def output3(b):
                dve.wait_ge(s_std, b + 1)
                dve.wait_ge(s_xn, b + 1)
                ending.step(dve.tensor_tensor(C3[:, 3, :], C3[:, 3, :], xn[:], ALU.mult))
                ending.step(dve.tensor_tensor(C3[:, 3, :], C3[:, 3, :], C3[:, 0, :], ALU.add))
                dve.tensor_tensor(C3[:, 3, :], C3[:, 3, :], m3[:], ALU.mult).then_inc(s_o3, 1)
                ending.end()

            def body(b):
                o = order_of(b)
                chain.begin(b)
                apart.begin(b)

                def fill(*names):
                    if not is_last(b):
                        for name in names:
                            project(name, o)

                def steps0(n):
                    if n == 4:
                        wait(dve, st_u3, 32 * b)
                    if n >= 4 and n % 2 == 0:
                        quotient0(b, (n - 4) // 2)
                    if n == 11 and not is_first(b):
                        end3(b - 1)
                def v1(name, kc):
                    g = take(o, name)
                    dve.tensor_tensor(V1[:, kc, :, 0:16], g[:, 0:D].rearrange("p (h d) -> p h d", d=16),
                                      row("vb1").rearrange("p (h d) -> p h d", d=16), ALU.add).then_inc(s_V1, 1)

                attention(b, 0, steps0)
                for c in (6, 7):
                    quotient0(b, c)
                dve.wait_ge(ld_res, 16 * b + 16)
                g = take(o, "wo")
                dve.scalar_tensor_tensor(out=x0, in0=g[:, 0:D], scalar=col("bo"), in1=zR[:], op0=ALU.add,
                                         op1=ALU.add).then_inc(s_x0, 1)
                dve.wait_ge(s_x0T, b + 1)
                g = PV[0]
                for c in range(2):
                    ins = dve.bn_stats(stat0[:, 6 * c:6 * c + 6], g[:, c * P:c * P + P])
                chain.step(ins, apart)
                for c in range(2):
                    ins = dve.bn_aggr(stat0[:, 12 + 2 * c:14 + 2 * c], stat0[:, 6 * c:6 * c + 6])
                chain.step(ins)
                dve.tensor_scalar(stat0[:, 16:18], stat0[:, 13:16:2], 1e-5, None, ALU.add).then_inc(s_var0, 1)
                dve.wait_ge(s_pow0, b + 1)
                for c in range(2):
                    ins = dve.tensor_scalar(hT[:, c, P:D], g[:, c * P:c * P + P], stat0[:, 12 + 2 * c:13 + 2 * c],
                                            stat0[:, 18 + c:19 + c], ALU.subtract, ALU.mult)
                ins.then_inc(s_hT, 1)
                blocks12(b, o, 1)
                v1("v1", 1)
                def steps1(n):
                    if n >= 3 and n % 2:
                        quotient(b, 1, (n - 3) // 2)
                attention(b, 1, steps1, lambda: (v1("v1c", 0), fill("qp0")))
                quotient(b, 1, 3)
                g = take(o, "o1")
                dve.wait_ge(s_res1, 2 * b + 1)
                dve.tensor_tensor(xa[:], g[:, 0:D], res1[:], ALU.add).then_inc(s_xa, 1)
                dve.wait_ge(s_ssq, b + 1)
                dve.tensor_scalar(stat[:, 1:2], stat[:, 0:1], 1.0 / D, 1e-6, ALU.mult, ALU.add).then_inc(s_var, 1)
                dve.wait_ge(s_pow, 3 * b + 1)
                dve.wait_ge(s_xa, 2 * b + 1)
                dve.tensor_scalar(xb[:], xa[:], stat[:, 2:3], None, ALU.mult).then_inc(s_xb, 1)
                mlp(b, o, ("m0", "m1"), "b1", 0)
                fill("qp1")
                if not is_first(b):
                    output3(b - 1)
                g = take(o, "w2")
                dve.wait_ge(s_res2, 2 * b + 1)
                dve.scalar_tensor_tensor(out=x1[:], in0=g[:, 0:D], scalar=0.5, in1=res2[:], op0=ALU.mult,
                                         op1=ALU.add).then_inc(s_x1, 1)
                def meanwhile():
                    g = take(o, "v2")
                    dve.tensor_tensor(V2[:, :, 0:16], g[:, 0:D].rearrange("p (h d) -> p h d", d=16),
                                      row("vb2").rearrange("p (h d) -> p h d", d=16), ALU.add).then_inc(s_V2, 1)
                layer_norm(b, x1, (s_x1, b + 1), 2, meanwhile)
                blocks12(b, o, 2)
                attention(b, 2, lambda n: fill("qp2") if n == 1 else None)
                for g in range(NG):
                    quotient(b, 2, g)
                g = take(o, "o2")
                dve.wait_ge(s_res1, 2 * b + 2)
                dve.tensor_tensor(xa[:], g[:, 0:D], res1[:], ALU.add).then_inc(s_xa, 1)
                layer_norm(b, xa, (s_xa, 2 * b + 2), 3)
                g = take(o, "v3")
                dve.tensor_tensor(V3[:, :, :, 0:8], g[:, 0:D].rearrange("p (c h d) -> p c h d", c=2, d=8),
                                  row("bv").rearrange("p (h d) -> p h d", d=8).unsqueeze(1)
                                  .to_broadcast([P, 2, NH, 8]), ALU.add).then_inc(s_v3, 1)
                mlp(b, o, ("n0", "n1"), "fcb", 1)
                g = take(o, "w4")
                dve.wait_ge(s_res2, 2 * b + 2)
                dve.scalar_tensor_tensor(out=x3[:], in0=g[:, 0:D], scalar=0.5, in1=res2[:], op0=ALU.mult,
                                         op1=ALU.add).then_inc(s_x3, 1)
                queries(b, o, 3, ("bq", 0, 1))
                dve.wait_ge(mx_done, SC_N * b + SC_BASE[2] + 3 * STEPS[2])
                for h in (0, 2):
                    block3(b, Qb[:, 0, h:h + 2], h).then_inc(s_Qb, 1)

                def steps3(n):
                    if n == -1:
                        block3(b, Q3[:, HG:2 * HG, :], HG).then_inc(s_Qx, 1)
                    if n == 0:
                        block3(b, Q3[:, 2 * HG:3 * HG, :], 2 * HG).then_inc(s_Qx, 1)
                    if n == 1:
                        fill("qp3")
                    if n == 3:
                        dve.wait_ge(sc_full, SC_N * b + SC_BASE[3] + 4)
                        block3(b, Q3[:, 0:HG, :], 3 * HG).then_inc(s_Qx, 1)
                    if not is_last(b):
                        for unit in early_maxima(n):
                            maxima(b + 1, 0, *unit)
                attention(b, 3, steps3)
                dve.wait_ge(s_nst, 3 * b + 3)
                dve.reciprocal(stat[:, 7:8], stat[:, 6:7]).then_inc(s_ninv, 1)
                chain.end()
                apart.end()

            dve.memset(Q0[:], 0.0)
            dve.memset(nmT[:], 0.0)
            dve.memset(V1[:], 1.0)
            dve.memset(V2[:], 1.0).then_inc(const_v, 1)
            dve.wait_ge(const_v, 1)
            dve.wait_ge(ld_cols, 16)
            for name in PROJ[:4]:
                project(name, prologue)
            dve.wait_ge(ld_par, 48)
            dve.tensor_copy(identb[:], ident[:])
            dve.tensor_copy(sel[:], sel32).then_inc(const_v, 1)
            for unit in early_maxima(None):
                maxima(0, 0, *unit)
            dve.wait_ge(ld_rows, 16)
            every_batch(dve, body)
            end3(B - 1)
            output3(B - 1)

        @block.gpsimd
        def _(pool):
            apart = Apart(pool, gate[:, 0:1], p_apart, 2)
            norm = Chain(pool, p_step, P_STEPS)
            norm_apart = Apart(pool, gate[:, 2:3], n_apart, 2)

            def power(b, k):
                pool.wait_ge(s_var, 3 * b + k)
                pool.tensor_tensor(stat[:, 2:3], stat[:, 1:2], half[:], ALU.pow).then_inc(s_pow, 1)

            def norm3(b):
                norm.begin(b)
                norm_apart.begin(b)
                pool.wait_ge(s_ninv, b + 1)
                norm.step(pool.tensor_tensor(stat3[:, 0:1], stat[:, 4:5], stat[:, 7:8], ALU.mult))
                norm.step(pool.tensor_tensor(stat3[:, 1:2], stat[:, 5:6], stat[:, 7:8], ALU.mult))
                norm.step(pool.tensor_tensor(stat3[:, 2:3], stat3[:, 0:1], stat3[:, 0:1], ALU.mult))
                norm.step(pool.tensor_tensor(stat3[:, 1:2], stat3[:, 1:2], stat3[:, 2:3], ALU.subtract), norm_apart)
                norm.step(pool.tensor_scalar(stat3[:, 1:2], stat3[:, 1:2], 0.0, 1e-5, ALU.max, ALU.add))
                norm.step(pool.tensor_tensor(stat3[:, 1:2], stat3[:, 1:2], half[:], ALU.pow), norm_apart)
                norm.step(pool.tensor_scalar(xn[:], xm[:], stat3[:, 0:1], stat3[:, 1:2], ALU.subtract, ALU.mult))
                pool.tensor_tensor(xn[:], xn[:], m3[:], ALU.mult).then_inc(s_xn, 1)
                norm.end()
                norm_apart.end()

            def body(b):
                apart.begin(b)
                for c in range(8):
                    n = 2 * c
                    pool.wait_ge(p_ready, SC_N * b + n + 2)
                    wait(pool, den_done, 8 * b + c - 1)
                    pool.tensor_tensor(Psum[:, c % 2, :], Pr[:, n % 4, :], Pr[:, (n + 1) % 4, :], ALU.add)\
                        .then_inc(ps_ready, 1)
                apart.wait((ld_msk, 112 * b + 112))
                for dst, src, value in (
                        (b1row[0:1, 0:P], m1row[0:1, :], NEG), (b2row[0:1, :], m2row[0:1, :], NEG),
                        (b3row[0:1, :], m3row[0:1, :], NEG), (bcol[:, 0:1], m1col[:], NEG / 16),
                        (bcol[:, 2:3], m2col[:], NEG / 4), (bcol[:, 3:5], m3col[:], NEG * 8.0 ** -0.5)):
                    pool.tensor_scalar(dst, src, 0.0, value, ALU.is_equal, ALU.mult).then_inc(s_msk, 1)
                pool.wait_ge(s_var0, b + 1)
                pool.tensor_tensor(stat0[:, 18:20], stat0[:, 16:18], half[:].to_broadcast([P, 2]), ALU.pow)\
                    .then_inc(s_pow0, 1)
                pool.wait_ge(s_lat, b + 1)
                pool.tensor_tensor(res1[:], lat, row("ob1"), ALU.add).then_inc(s_res1, 1)
                pool.tensor_tensor(res2[:], lat, row("b2"), ALU.add).then_inc(s_res2, 1)
                if not is_first(b):
                    norm3(b - 1)
                power(b, 1)
                power(b, 2)
                pool.wait_ge(s_x1, b + 1)
                pool.tensor_tensor(res1[:], x1[:], row("cb"), ALU.add).then_inc(s_res1, 1)
                apart.wait((s_o3, b))
                pool.tensor_scalar(m3[:], m3row[:], 0.0, None, ALU.add).then_inc(s_msk, 1)
                power(b, 3)
                pool.tensor_tensor(res2[:], xa[:], row("pb"), ALU.add).then_inc(s_res2, 1)
                pool.wait_ge(s_x3, b + 1)
                pool.wait_ge(s_msk, N_MSK * (b + 1))
                pool.tensor_tensor(xm[:], x3[:], m3[:], ALU.mult).then_inc(s_xm, 1)
                apart.end()

            pool.memset(b1row[:], 0.0)
            pool.memset(b2row[:], 0.0)
            pool.memset(b3row[:], 0.0)
            pool.memset(bcol[:], 0.0)
            pool.memset(half[:], -0.5)
            pool.memset(ones[:], 1.0).then_inc(const_p, 1)
            pool.wait_ge(const_p, 1)
            pool.wait_ge(ld_rows, 16)
            every_batch(pool, body)
            norm3(B - 1)


def launch_constants(np):
    ident = np.eye(P, dtype=np.float32)
    p = np.arange(P)
    hmask = np.concatenate([p[:, None] // 16 == np.arange(8)[None], p[:, None] // 8 == np.arange(16)[None]], axis=1)
    sel = np.zeros((P, 2 * HG, P), np.float32)
    for h in range(2 * HG):
        sel[h, h] = 1.0
    return ident, hmask.astype(np.float32), sel


def kernel(**inputs):
    import numpy as np
    import concourse.bacc as bacc
    from concourse.bass_utils import run_bass_kernel_spmd

    a = {k: np.asarray(v) for k, v in inputs.items()}
    l1 = {k[9:]: v for k, v in a.items() if k.startswith("L1_")}
    l2 = {k[9:]: v for k, v in a.items() if k.startswith("L2_")}

    def chunks(w):
        return w.reshape(-1, P, w.shape[1]).transpose(1, 0, 2)

    def columns(v):
        return v.reshape(-1, P).T

    def slots(w):
        out = np.zeros((NG, HG, 32, w.shape[1]), w.dtype)
        out[:, :, :16] = w.reshape(NG, HG, 16, -1)
        return out.reshape(NG, P, -1).transpose(1, 0, 2)

    w0 = np.stack([a["L0_xattn_" + n].T for n in ("Wqkv0", "Winj0", "Wqkv1", "Winj1")], axis=1)
    w0 = w0.reshape(P, 4, 6, 512).transpose(2, 0, 1, 3)
    kv_w, kv_b = l1["kv_w"].reshape(D, D, 2), l1["kv_b"].reshape(D, 2)
    parts = {"bo": a["L0_xattn_bo"], "rwb": a["L0_xattn_r_w_bias"].reshape(-1), "qb1": l1["q_b"],
             "kb1": kv_b[:, 0], "b1": l1["mlp_b1"], "qb2": l2["q_b"], "kb2": l2["k_b"], "fcb": l2["fc_b"],
             "bq": a["L3_xattn_bq"], "bk": a["L3_xattn_bk"], "pw": l1["postnorm_w"], "ln1w": l2["ln1_w"],
             "ln1b": l2["ln1_b"], "ln2w": l2["ln2_w"], "ln2b": l2["ln2_b"]}
    rows = {"vb1": kv_b[:, 1], "ob1": l1["out_b"], "b2": l1["mlp_b2"],
            "vb2": l2["v_b"], "cb": l2["cproj_b"],
            "pb": l2["proj_b"], "bv": a["L3_xattn_bv"]}
    ident, hmask, sel = launch_constants(np)
    arrays = {
        "z_in": a["x"], "ctxT_in": a["ctx_2048"].transpose(0, 2, 1).reshape(B, 2, P, P).transpose(0, 2, 1, 3),
        "ctx_in": a["ctx_2048"],
        "mask1": a["mask_BxS2_ik0"].reshape(B, 1, P),
        "mask2": a["mask_BxS2_bf1"].view(np.uint8).reshape(B, 1, P),
        "mask3": a["mask_Bx1x2048_bf1"].view(np.uint8).reshape(B, 1, D),
        "w0": w0, "wo": chunks(a["L0_xattn_Wo"].T),
        "w1qk": np.stack([chunks(l1["q_w"]), chunks(kv_w[:, :, 0])], axis=1),
        "w1v": chunks(kv_w[:, :, 1]), "w1o": slots(l1["out_w"]),
        "w1a": chunks(l1["mlp_w1"]), "w1b": chunks(l1["mlp_w2"]),
        "w2qkv": np.stack([chunks(l2[n]) for n in ("q_w", "k_w", "v_w")], axis=1),
        "w2o": slots(l2["cproj_w"]), "w2a": chunks(l2["fc_w"]), "w2b": chunks(l2["proj_w"]),
        "w3": np.stack([a["L3_xattn_" + n].T for n in ("Wq", "Wk", "Wv")], axis=1),
        "cols_in": np.concatenate([columns(parts[n]) for n in COLS], axis=1),
        "rows_in": np.concatenate([rows[n] for n in ROWS]).reshape(1, NROWS),
        "ident_in": ident, "hmask_in": hmask, "sel_in": sel,
    }
    arrays = {k: np.ascontiguousarray(v) for k, v in arrays.items()}
    nc = bacc.Bacc("TRN2", target_bir_lowering=False, num_devices=1)
    args = [nc.dram_tensor(n, v.shape, mybir.dt.from_np(v.dtype), kind="ExternalInput").ap()
            for n, v in arrays.items()]
    out = nc.dram_tensor("out", (B, P, D), F32, kind="ExternalOutput").ap()
    build(nc, *args, out)
    r = run_bass_kernel_spmd(nc, [arrays], core_ids=[0])
    return r.results[0]["out"]
```
